# Optimizing a Trainium2 kernel written in Bass

```python
import numpy as np
import jax
import jax.numpy as jnp

def _softmax(x, axis=-1):
    return jax.nn.softmax(x, axis=axis)

def _gelu(x):
    return jax.nn.gelu(x, approximate=True)

def _silu(x):
    return jax.nn.silu(x)

def _sigmoid(x):
    return jax.nn.sigmoid(x)

def _layernorm(x, axis=-1, eps=1e-05):
    m = jnp.mean(x, axis=axis, keepdims=True)
    v = jnp.var(x, axis=axis, keepdims=True)
    return (x - m) / jnp.sqrt(v + eps)

def _scatter_add(tgt, idx, src, axis=0):
    return tgt.at[idx].add(src)

def _segment_sum(src, seg, n):
    return jax.ops.segment_sum(src, seg, n)
kernel_name = 'mk_flamingo_gated_d2_seqx_r8_54fc59'

def setup_inputs(seed: int=0):
    np.random.seed(seed)
    _w = jnp.asarray

    def _rec_inputs():
        import jax
        import jax.numpy as jnp
        _rk = jax.random.key(seed)
        x = -0.0002928 + 1 * jax.random.normal(jax.random.fold_in(_rk, 1), (8, 128, 256), jnp.float32)
        _lenS = 128 - jax.random.randint(jax.random.fold_in(_rk, 7), (8,), 0, max(1, 128 // 4) + 1, jnp.int32)
        _lenS2 = 128 - jax.random.randint(jax.random.fold_in(_rk, 8), (8,), 0, max(1, 128 // 4) + 1, jnp.int32)
        fside_S2_0 = -0.00337071 + 1.01897 * jax.random.normal(jax.random.fold_in(_rk, 11), (128,), jnp.float32)
        _ctx_2048P = jax.random.normal(jax.random.fold_in(_rk, 12), (8, 16, 256), jnp.float32)
        _ctx_2048c = jax.random.dirichlet(jax.random.fold_in(_rk, 512), 0.3 * jnp.ones((16,), jnp.float32), (8, 128))
        _ctx_2048t = jnp.einsum('bsk,bkd->bsd', _ctx_2048c, _ctx_2048P)
        _ctx_2048t = _ctx_2048t * jax.lax.rsqrt(jnp.mean(jnp.square(_ctx_2048t)) + 1e-12) * 0.953939
        ctx_2048 = 0.000675642 + 1.00031 * (_ctx_2048t + 0.3 * jax.random.normal(jax.random.fold_in(_rk, 612), (8, 128, 256), jnp.float32))
        _validS = jnp.arange(128)[None, :] < _lenS[:, None]
        _validS2 = jnp.arange(128)[None, :] < _lenS2[:, None]
        _causal = jnp.tril(jnp.ones((128, 128), dtype=bool))
        mask_Bx1x2048_fk1 = jnp.where(jnp.ones((8, 1, 256), dtype=bool), 1.0, 0.0).astype(jnp.float32)
        _g = jax.random.normal(jax.random.fold_in(_rk, 9001), (2, 2), jnp.float32)
        _g = jnp.sign(_g) * jnp.maximum(jnp.abs(_g), 1.0) + (_g == 0) * 1.0
        g_xattn = _g[0]
        g_ffn = _g[1]
        return (x, fside_S2_0, ctx_2048, mask_Bx1x2048_fk1, g_xattn, g_ffn)
    x, fside_S2_0, ctx_2048, mask_Bx1x2048_fk1, g_xattn, g_ffn = _rec_inputs()

    def _L0_xattn_setup():
        import jax, jax.numpy as jnp
        import numpy as np
        key = jax.random.key(seed)
        ks = jax.random.split(key, 5)
        B, D, L, NH = (2, 128, 256, 8)
        H = D // NH
        return {'v': jax.random.normal(ks[0], (B, D, L), jnp.float32), 'k': jax.random.normal(ks[1], (H, L), jnp.float32) * 0.1, 'bias': jax.random.normal(ks[2], (D,), jnp.float32), 'x1': jax.random.normal(ks[3], (B, D, L), jnp.float32), 'x2': jax.random.normal(ks[4], (B, D, L), jnp.float32), 'num_heads': NH}
    _L0_xattn_all = _L0_xattn_setup()
    _L0_xattn_in = {k: v for k, v in _L0_xattn_all.items() if k in ('k',)}
    del _L0_xattn_all

    def _L0_ffn_setup():
        import jax, jax.numpy as jnp
        import numpy as np
        LHS_BITS = 8
        RHS_BITS = 8

        def fake_quant(x, bits, axes):
            qmax = 2.0 ** (bits - 1) - 1.0
            amax = jnp.max(jnp.abs(x), axis=axes, keepdims=True)
            scale = jnp.where(amax > 0, amax / qmax, jnp.ones_like(amax))
            q = jnp.clip(jnp.round(x / scale), -qmax, qmax) * scale
            return x + jax.lax.stop_gradient(q - x)
        key = jax.random.key(seed)
        k1, k2, k3 = jax.random.split(key, 3)
        B, S, D, F = (4, 256, 256, 256)
        x = jax.random.normal(k1, (B, S, D), dtype=jnp.float32)
        kernel = jax.random.normal(k2, (D, F), dtype=jnp.float32) * (1.0 / np.sqrt(D))
        bias = jax.random.normal(k3, (F,), dtype=jnp.float32) * 0.02
        return {'x': x, 'kernel': kernel, 'bias': bias}
    _L0_ffn_all = _L0_ffn_setup()
    _L0_ffn_in = {k: v for k, v in _L0_ffn_all.items() if k in ('kernel', 'bias')}
    del _L0_ffn_all

    def _L1_xattn_setup():
        import math
        import jax, jax.numpy as jnp
        import numpy as np
        SIZE = 128
        HEADS = 16
        HEAD_DIM = SIZE // HEADS
        B, T, S = (2, 256, 256)
        NEG = 1000000.0
        key = jax.random.key(seed)
        ks = jax.random.split(key, 10)
        target = jax.random.normal(ks[0], (B, SIZE, T), dtype=jnp.float32)
        source = jax.random.normal(ks[1], (B, SIZE, S), dtype=jnp.float32)
        target_mask = (jax.random.uniform(ks[2], (B, 1, T)) > 0.1).astype(jnp.float32)
        source_mask = (jax.random.uniform(ks[3], (B, 1, S)) > 0.1).astype(jnp.float32)
        scale = 1.0 / math.sqrt(SIZE)
        Wq = jax.random.normal(ks[4], (SIZE, SIZE), dtype=jnp.float32) * scale
        Wk = jax.random.normal(ks[5], (SIZE, SIZE), dtype=jnp.float32) * scale
        Wv = jax.random.normal(ks[6], (SIZE, SIZE), dtype=jnp.float32) * scale
        bq = jax.random.normal(ks[7], (SIZE,), dtype=jnp.float32) * 0.01
        bk = jax.random.normal(ks[8], (SIZE,), dtype=jnp.float32) * 0.01
        bv = jax.random.normal(ks[9], (SIZE,), dtype=jnp.float32) * 0.01
        return {'target': target, 'source': source, 'target_mask': target_mask, 'source_mask': source_mask, 'Wq': Wq, 'bq': bq, 'Wk': Wk, 'bk': bk, 'Wv': Wv, 'bv': bv}
    _L1_xattn_all = _L1_xattn_setup()
    _L1_xattn_in = {k: v for k, v in _L1_xattn_all.items() if k in ('Wq', 'bq', 'Wk', 'bk', 'Wv', 'bv')}
    del _L1_xattn_all

    def _L1_ffn_setup():
        import jax, jax.numpy as jnp
        import numpy as np
        B, S, H = (2, 128, 256)
        E, K = (8, 2)
        I = 176
        IS = 704
        WSCALE = 0.02
        key = jax.random.key(seed)
        ks = jax.random.split(key, 9)
        f32 = jnp.float32
        return {'hidden_states': jax.random.normal(ks[0], (B, S, H), dtype=f32), 'gate_w': jax.random.normal(ks[1], (E, H), dtype=f32) * WSCALE, 'w_gate': jax.random.normal(ks[2], (E, H, I), dtype=f32) * WSCALE, 'w_up': jax.random.normal(ks[3], (E, H, I), dtype=f32) * WSCALE, 'w_down': jax.random.normal(ks[4], (E, I, H), dtype=f32) * WSCALE, 'sw_gate': jax.random.normal(ks[5], (H, IS), dtype=f32) * WSCALE, 'sw_up': jax.random.normal(ks[6], (H, IS), dtype=f32) * WSCALE, 'sw_down': jax.random.normal(ks[7], (IS, H), dtype=f32) * WSCALE, 'shared_gate_w': jax.random.normal(ks[8], (H, 1), dtype=f32) * WSCALE}
    _L1_ffn_all = _L1_ffn_setup()
    _L1_ffn_in = {k: v for k, v in _L1_ffn_all.items() if k in ('gate_w', 'w_gate', 'w_up', 'w_down', 'sw_gate', 'sw_up', 'sw_down', 'shared_gate_w')}
    del _L1_ffn_all
    return {'x': x, 'fside_S2_0': fside_S2_0, 'ctx_2048': ctx_2048, 'mask_Bx1x2048_fk1': mask_Bx1x2048_fk1, 'g_xattn': g_xattn, 'g_ffn': g_ffn, 'L0_xattn_k': _L0_xattn_in['k'], 'L0_ffn_kernel': _L0_ffn_in['kernel'], 'L0_ffn_bias': _L0_ffn_in['bias'], 'L1_xattn_Wq': _L1_xattn_in['Wq'], 'L1_xattn_bq': _L1_xattn_in['bq'], 'L1_xattn_Wk': _L1_xattn_in['Wk'], 'L1_xattn_bk': _L1_xattn_in['bk'], 'L1_xattn_Wv': _L1_xattn_in['Wv'], 'L1_xattn_bv': _L1_xattn_in['bv'], 'L1_ffn_gate_w': _L1_ffn_in['gate_w'], 'L1_ffn_w_gate': _L1_ffn_in['w_gate'], 'L1_ffn_w_up': _L1_ffn_in['w_up'], 'L1_ffn_w_down': _L1_ffn_in['w_down'], 'L1_ffn_sw_gate': _L1_ffn_in['sw_gate'], 'L1_ffn_sw_up': _L1_ffn_in['sw_up'], 'L1_ffn_sw_down': _L1_ffn_in['sw_down'], 'L1_ffn_shared_gate_w': _L1_ffn_in['shared_gate_w']}

def reference(x, fside_S2_0, ctx_2048, mask_Bx1x2048_fk1, g_xattn, g_ffn, L0_xattn_k, L0_ffn_kernel, L0_ffn_bias, L1_xattn_Wq, L1_xattn_bq, L1_xattn_Wk, L1_xattn_bk, L1_xattn_Wv, L1_xattn_bv, L1_ffn_gate_w, L1_ffn_w_gate, L1_ffn_w_up, L1_ffn_w_down, L1_ffn_sw_gate, L1_ffn_sw_up, L1_ffn_sw_down, L1_ffn_shared_gate_w):
    import jax
    import jax.numpy as jnp

    def _L0_xattn_ref(v, k, bias, x1, x2, num_heads):
        import jax, jax.numpy as jnp
        import numpy as np
        B, D, L = v.shape
        H = D // num_heads
        fft_size = 2 * L
        vr = v.reshape(B, H, num_heads, L)
        x1r = x1.reshape(B, H, num_heads, L)
        x2r = x2.reshape(B, H, num_heads, L)
        kv = vr[:, :, :, None, :] * x2r[:, :, None, :, :]
        k_f = jnp.fft.rfft(k.astype(jnp.float32), n=fft_size)
        y = jnp.fft.irfft(jnp.fft.rfft(kv, n=fft_size) * k_f[None, :, None, None, :], n=fft_size)[..., :L]
        skip = bias.astype(jnp.float32).reshape(H, num_heads)[None, :, :, None, None]
        y = y + kv * skip
        out = jnp.einsum('bhijl,bhil->bhjl', y, x1r)
        return out.reshape(B, D, L)

    def _L0_ffn_ref(x, kernel, bias):
        import jax, jax.numpy as jnp
        import numpy as np
        LHS_BITS = 8
        RHS_BITS = 8

        def fake_quant(x, bits, axes):
            qmax = 2.0 ** (bits - 1) - 1.0
            amax = jnp.max(jnp.abs(x), axis=axes, keepdims=True)
            scale = jnp.where(amax > 0, amax / qmax, jnp.ones_like(amax))
            q = jnp.clip(jnp.round(x / scale), -qmax, qmax) * scale
            return x + jax.lax.stop_gradient(q - x)
        bq = fake_quant(bias, RHS_BITS, -1)
        xq = fake_quant(x, LHS_BITS, -1)
        kq = fake_quant(kernel, RHS_BITS, 0)
        y = jnp.einsum('bsd,df->bsf', xq, kq)
        y = y + bq[None, None, :]
        y = jax.nn.relu(y)
        return fake_quant(y, LHS_BITS, -1)

    def _L1_xattn_ref(target, source, target_mask, source_mask, Wq, bq, Wk, bk, Wv, bv):
        import math
        import jax, jax.numpy as jnp
        import numpy as np
        SIZE = 128
        HEADS = 16
        HEAD_DIM = SIZE // HEADS
        B, T, S = (2, 256, 256)
        NEG = 1000000.0
        b, _, t = target.shape
        s = source.shape[-1]
        q = jnp.einsum('oc,bct->bot', Wq, target) + bq[None, :, None]
        k = jnp.einsum('oc,bcs->bos', Wk, source) + bk[None, :, None]
        v = jnp.einsum('oc,bcs->bos', Wv, source) + bv[None, :, None]
        q = q.reshape(b, HEADS, HEAD_DIM, t)
        k = k.reshape(b, HEADS, HEAD_DIM, s)
        v = v.reshape(b, HEADS, HEAD_DIM, s)
        dot = jnp.einsum('bhdt,bhds->bhts', q, k) / math.sqrt(HEAD_DIM)
        mask = target_mask[:, :, :, None] * source_mask[:, :, None, :]
        dot = mask * dot - (1.0 - mask) * NEG
        amap = jax.nn.softmax(dot, axis=-1) * mask
        out = jnp.einsum('bhts,bhds->bhdt', amap, v)
        return out.reshape(b, HEADS * HEAD_DIM, t)

    def _L1_ffn_ref(hidden_states, gate_w, w_gate, w_up, w_down, sw_gate, sw_up, sw_down, shared_gate_w):
        import jax, jax.numpy as jnp
        import numpy as np
        B, S, H = (2, 128, 256)
        E, K = (8, 2)
        I = 176
        IS = 704
        WSCALE = 0.02
        x = hidden_states
        logits = jnp.einsum('bsh,eh->bse', x, gate_w)
        probs = jax.nn.softmax(logits, axis=-1)
        top_w, top_i = jax.lax.top_k(probs, K)
        top_w = top_w / jnp.sum(top_w, axis=-1, keepdims=True)
        onehot = jax.nn.one_hot(top_i, E, dtype=x.dtype)
        combine = jnp.einsum('bsk,bske->bse', top_w, onehot)
        g = jnp.einsum('bsh,ehi->besi', x, w_gate)
        u = jnp.einsum('bsh,ehi->besi', x, w_up)
        h = jax.nn.silu(g) * u
        expert_out = jnp.einsum('besi,eih->besh', h, w_down)
        moe_out = jnp.einsum('besh,bse->bsh', expert_out, combine)
        sh = jax.nn.silu(x @ sw_gate) * (x @ sw_up)
        shared_out = sh @ sw_down
        shared_gate = jax.nn.sigmoid(x @ shared_gate_w)
        return moe_out + shared_out * shared_gate
    x = x + jnp.tanh(g_xattn[0]) * _L0_xattn_ref(_layernorm(x, axis=-1), L0_xattn_k, fside_S2_0, ctx_2048, ctx_2048, 8)
    x = x + jnp.tanh(g_ffn[0]) * _L0_ffn_ref(_layernorm(x, axis=-1), L0_ffn_kernel, L0_ffn_bias)
    x = x + jnp.tanh(g_xattn[1]) * _L1_xattn_ref(_layernorm(x, axis=-1), ctx_2048, mask_Bx1x2048_fk1, mask_Bx1x2048_fk1, L1_xattn_Wq, L1_xattn_bq, L1_xattn_Wk, L1_xattn_bk, L1_xattn_Wv, L1_xattn_bv)
    x = x + jnp.tanh(g_ffn[1]) * _L1_ffn_ref(_layernorm(x, axis=-1), L1_ffn_gate_w, L1_ffn_w_gate, L1_ffn_w_up, L1_ffn_w_down, L1_ffn_sw_gate, L1_ffn_sw_up, L1_ffn_sw_down, L1_ffn_shared_gate_w)
    return x

_drawn_inputs = setup_inputs


def setup_inputs(seed=0):
    import zlib

    import numpy as np

    out = dict(_drawn_inputs(seed))
    spreads = {'g_ffn': (-1.0, 0.6)}
    factors = {'L0_ffn_bias': 8.0,
     'L1_xattn_bq': 48.009,
     'L1_xattn_bk': 64.0,
     'L1_xattn_bv': 64.0,
     'L1_ffn_gate_w': 8.0,
     'L1_ffn_w_gate': 8.0,
     'L1_ffn_w_up': 8.0,
     'L1_ffn_w_down': 8.0,
     'L1_ffn_sw_gate': 8.0,
     'L1_ffn_sw_up': 8.0,
     'L1_ffn_sw_down': 8.0,
     'L1_ffn_shared_gate_w': 8.0}
    for name, (base, spread) in spreads.items():
        noise = np.random.default_rng([zlib.crc32(name.encode()), seed]).standard_normal(out[name].shape)
        drawn = base * np.exp(spread * noise) if base else spread * noise
        out[name] = jnp.asarray(drawn.astype(out[name].dtype))
    for name, factor in factors.items():
        out[name] = (out[name] * factor).astype(out[name].dtype)
    return out
```

```python
import concourse.bass as bass
from concourse import mybir
from contextlib import ExitStack

B, TOK, L = 8, 128, 256
NH0, HD0 = 16, 8
NH1, HD1 = 16, 8
NE, EI, SI = 8, 176, 704
NI = NE * EI + SI
NCH = -(-NI // 128)
WCOLS = 2 * 128 + 2 * 128 + L + 128
NEG = 1000000.0
QMAX = 127.0
ROUND = 12582912.0
EPS = 1e-05
NU = 2 * B
HU = NH1 // 2


def flamingo_program(nc, x, ctx, ctxT, mask, maskT, kpad, skip, gains, kern, biasq, wqkvT, bqk, bv,
                     routerT, wpack, ident_d, heads_d, earlier_d, out):
    f32, f32r, bf16 = mybir.dt.float32, mybir.dt.float32r, mybir.dt.bfloat16
    ALU, ACT, AX = mybir.AluOpType, mybir.ActivationFunctionType, mybir.AxisListType
    ds = bass.ds
    stack = ExitStack()
    with stack:
        def sb(name, shape, dt=f32):
            return stack.enter_context(nc.sbuf_tensor(name, shape, dt))

        def sem(name):
            return stack.enter_context(nc.semaphore(name))

        X = sb("X", [128, B, L])
        C = sb("C", [128, B, L])
        XN = sb("XN", [128, B, L])
        CT = sb("CT", [128, 2, B, TOK])
        VT = sb("VT", [128, 2, B, TOK])
        OT = sb("OT", [128, 2, B, TOK])
        CG = sb("CG", [128, B, L])
        T = sb("T", [128, 4, L])
        KVP = sb("KVP", [128, 4, 1024])
        ident = sb("ident", [128, 128])
        identb = sb("identb", [128, 128], bf16)
        ones = sb("ones", [128, 128])
        heads = sb("heads", [128, 128])
        skipc = sb("skipc", [128, 1])
        gain = sb("gain", [128, 4])
        tg = sb("tg", [128, 4])
        mhalf = sb("mhalf", [128, B])
        bst = sb("bst", [128, B, 6])
        mv = sb("mv", [128, B, 2])
        ve = sb("ve", [128, B])
        rstd = sb("rstd", [128, B])
        kq = sb("kq", [128, 2, L], bf16)
        akf = sb("akf", [128, 2])
        skb = sb("skb", [128, L])
        bqb = sb("bqb", [128, L])
        small = sb("small", [128, 16, B])
        W3 = sb("W3", [128, 3, 128])
        bqk_sb = sb("bqk_sb", [128, 2])
        bv_sb = sb("bv_sb", [128, 128])
        smt = sb("smt", [128, 2 * B])
        MB = sb("MB", [128, B, L])
        msk = sb("msk", [B, L])
        HI = sb("HI", [128, B, L], f32r)
        LO = sb("LO", [128, B, L], f32r)
        VA = sb("VA", [128, 2 * B, NH1, 16])
        VR = sb("VR", [128, 2, 2, NH1, 16])
        QS = [sb(f"QS{j}", [128, HU, L], f32r) for j in range(4)]
        KS = [sb(f"KS{j}", [128, HU, L], f32r) for j in range(4)]
        negm = sb("negm", [128, 2, HU, 2])
        mT = sb("mT", [16, 2, 2, 128], f32r)
        osb = sb("osb", [128, 2, 4, L])
        rden = sb("rden", [128, 2, L])
        def row(t):
            return t.rearrange("p h l -> p (h l)")

        kw, kt2 = osb[:, 0, 0:2, :], osb[:, 0, 2:4, :]
        kinv = osb[:, 1, 0, :]
        diag = osb[:, 1, 1, :].rearrange("p (f c) -> p f c", f=2)
        mtmp = osb[0:B, 1, 2:4, :]
        nd = T[:, :, :].rearrange("p (r s) l -> p r s l", r=2)
        qb = T[:, :, :].rearrange("p j l -> p (j l)").bitcast(bf16).rearrange("p (b l) -> p b l", b=B)
        qbT = VR[:, :, :, :, :].rearrange("p r k h c -> p (r k h c)").bitcast(bf16).rearrange("p (k b t) -> p k b t", k=2, b=B)
        CR = VA[:, 0:B, :, :].rearrange("p b h c -> p (b h c)").rearrange("p (k b t) -> p k b t", k=2, b=B)
        KF = OT[:, :, :, :].rearrange("p k b t -> p (k b t)")
        VF = VT[:, :, :, :].rearrange("p k b t -> p (k b t)")
        QF = row(CG[:, :, :])
        AQ = row(QS[3][0:B, 0:6, :]).rearrange("p (r l) -> p r l", r=6)
        AK = row(KS[3][0:B, 0:6, :]).rearrange("p (r l) -> p r l", r=6)
        EXPS = [KVP[:, 2 * r:2 * r + 2, :].rearrange("p a n -> p (a n)") for r in range(2)]
        XT = VT
        XTH = row(HI[:, :, :]).rearrange("p (k t) -> p k t", k=2)
        XTL = row(LO[:, :, :]).rearrange("p (k t) -> p k t", k=2)
        WST = [row(C[:, :, :])[:, r * 1024:r * 1024 + WCOLS] for r in range(2)]
        SIL = [KVP[:, 2, r * 512:(r + 1) * 512] for r in range(2)]
        TU = [KVP[:, 3, r * 512:(r + 1) * 512] for r in range(2)]
        HH = [osb[:, 0, 2 * r:2 * r + 2, :].rearrange("p a l -> p (a l)") for r in range(2)]
        WHI = [row(QS[r][:, :, :])[:, 0:WCOLS] for r in range(4)]
        WLO = [row(KS[r][:, :, :])[:, 0:768] for r in range(4)]
        HHI = [row(QS[r][:, :, :])[:, 1024:1536] for r in range(2)]
        HLO = [row(KS[r][:, :, :])[:, 1024:1536] for r in range(2)]
        CBT = [row(QS[t][:, :, :])[:, 1536:2048] for t in range(2)]
        ZR = row(KS[0][:, :, :])[:, 1536:2048]
        R1, R2 = (QF[:, c:c + 256].rearrange("p (b i j) -> p b i j", b=B // 2, i=NE) for c in (1536, 1792))
        rt = sb("rt", [128, 2, NE + 1])
        LG = sb("LG", [128, B, NE + 1])
        EX = sb("EX", [128, B, NE])
        early = sb("early", [128, NE, NE])
        rank = sb("rank", [128, B, NE])
        CB = sb("CB", [128, B, NE + 1])

        PS = stack.enter_context(nc.psum_tensor("PS", [128, 8, 512], f32))

        def banks(a, n):
            return PS[:, a:a + n, :].rearrange("p a c -> p (a c)")

        def scratch(name, shape):
            return nc.dram_tensor(name, shape, f32, kind="Internal").ap()

        q_dram = scratch("q_dram", [B, 3, 128, L])
        k_dram = scratch("k_dram", [B, 2, 128, L])
        aq_dram = scratch("aq_dram", [B, 6, L])
        ak_dram = scratch("ak_dram", [B, 6, L])
        o_dram = scratch("o_dram", [B, 128, 2, L])

        names = """x_in ctx_in ctxT_in consts_in kern_in attn_in mask_in router_in
            consts_done wq_done tanh_done var_done rstd_done xn_done vt_ps vt_done vc_done g_ps cg_done
            dstep astep pstep kt_ps diag_done sk_ps kq_done kv_done y_ps yx_done ot_part ot_ps x1_done
            kp_ps k_done k_hi k_lo k_out vp_ps v_t v_done va_ones aux_done aux_out zeroed mq_done
            xq_t xq_done qT_ps qT_done f_ps x2_done q_ps q_done q_hi q_lo q_out
            s_ps s_used mx_done mt_done e_ps p_done pv_done o_sb o_out
            vr_done turned rden_done x3_done xt_ps xt_done xth_done xtl_done l_ps l_done l_exp cb_done
            cbt_ps cbt_done cbt_zero acc_zero zr_done whi_done wlo_done w_used
            guc_g guc_u guc_c sil_done t_done h_done hhi_done hlo_done down_done y_done out_done""".split()
        S = {n: sem(n) for n in names}
        T_in = [sem(f"T_in{j}") for j in range(4)]
        st_in = [sem(f"st_in{j}") for j in range(4)]
        m_in = [sem(f"m_in{j}") for j in range(4)]
        w_in = [sem(f"w_in{j}") for j in range(2)]
        nd_in = [sem(f"nd_in{j}") for j in range(2)]

        block = stack.enter_context(nc.Block())

        def need(eng, name, n):
            if not (isinstance(n, int) and n <= 0):
                eng.wait_ge(S[name], n)

        def after(eng, ins, name, n):
            ins.then_inc(S[name], 1)
            eng.wait_ge(S[name], n)

        def tile_bank(j, k):
            return 2 * ((5 * j + (k or -1)) % 2)

        def turn_bank(j):
            return 2 * ((j + 1) % 2)

        class Steps:

            def __init__(self, eng, name):
                self.eng, self.name, self.n = eng, name, 0

            def tick(self, ins):
                ins.then_inc(S[self.name], 1)
                self.n += 1

            def sync(self):
                self.eng.wait_ge(S[self.name], self.n)

            def link(self, ins):
                self.tick(ins)
                self.sync()

        @block.sync
        def _(sp):
            sp.dma_start(X[:, :, :], x.rearrange("b p l -> p b l")).then_inc(S["x_in"], 16)
            sp.dma_start(CR, ctxT[1].rearrange("(k p) b t -> p k b t", p=128)).then_inc(S["ctxT_in"], 16)
            sp.dma_start(CT[:, :, :, :], ctxT[0].rearrange("(k p) b t -> p k b t", p=128)).then_inc(S["ctxT_in"], 16)
            shifted = bass.AP(kpad.tensor, L - 127, [[2 * L, NH0], [1, 128], [1, L]])

            def load_T(i):
                for j in range(4):
                    need(sp, "y_ps", 4 * i + j - 3)
                    sp.dma_start(T[:, j, :], shifted[ds(4 * i + j, 1), :, :].rearrange("h p l -> (h p) l")).then_inc(T_in[j], 16)

            load_T(0)
            with sp.Fori(1, NH0 // 4) as i:
                load_T(i)

            sp.wait_ge(S["aux_done"], 13)
            sp.dma_start(aq_dram, AQ.bitcast(f32)).then_inc(S["aux_out"], 16)
            sp.dma_start(ak_dram, AK.bitcast(f32)).then_inc(S["aux_out"], 16)
            def store_part(dst, part, src):
                return sp.dma_start(dst[:, part].rearrange("b p t -> p b t"), src[:, :, :].bitcast(f32))

            sp.wait_ge(S["k_hi"], 4)
            store_part(k_dram, 0, HI).then_inc(S["k_out"], 16)
            sp.wait_ge(S["k_lo"], 4)
            store_part(k_dram, 1, LO).then_inc(S["k_out"], 16)
            sp.wait_ge(S["q_hi"], 4)
            store_part(q_dram, 0, HI).then_inc(S["q_out"], 16)
            store_part(q_dram, 2, HI).then_inc(S["q_out"], 16)
            sp.wait_ge(S["q_lo"], 4)
            store_part(q_dram, 1, LO).then_inc(S["q_out"], 16)
            sp.wait_ge(S["k_out"], 32)
            sp.wait_ge(S["q_out"], 48)
            sp.wait_ge(S["aux_out"], 32)
            sp.wait_ge(S["zeroed"], 8)

            def stack_rows(src, parts, b, half, n):
                v = bass.AP(src.tensor, half * HU * L, [[128 * L, parts * (B - 1) + n], [NH1 * L, 2 * HD1], [1, HU * L]])
                return v[ds(parts * b, n), :, :]

            def load_stack(i, j):
                b, half = 2 * i + j // 2, j % 2
                need(sp, "e_ps", 8 * (4 * i + j - 3))
                sp.dma_start(QS[j][0:32, :, :].bitcast(f32), stack_rows(q_dram, 3, b, half, 2)).then_inc(st_in[j], 16)
                for r in range(2):
                    sp.dma_start(KS[j][16 * r:16 * r + 16, :, :].bitcast(f32), stack_rows(k_dram, 2, b, half, 1)).then_inc(st_in[j], 16)
                for dst, src in ((QS, aq_dram), (KS, ak_dram)):
                    rows = src[ds(b, 1), :, :].rearrange("b r t -> (b r) t").unsqueeze(1).to_broadcast([6, HU, L])
                    sp.dma_start(dst[j][32:38, :, :].bitcast(f32), rows).then_inc(st_in[j], 16)

            def move_max(i, j):
                sp.wait_ge(S["mt_done"], 2 * (4 * i + j) + 2)
                for s in range(2):
                    sp.dma_start(QS[j][36 + s:37 + s, :, :].bitcast(f32).rearrange("p h (c t) -> p (h c) t", c=2),
                                 mT[:, j % 2, s, :].bitcast(f32)).then_inc(m_in[j], 16)

            def store_o(b, r):
                sp.wait_ge(S["o_sb"], 4 * b + 4)
                for c in range(4):
                    dst = o_dram[ds(b, 1)].rearrange("b (a c d) s t -> (b c) (d s) a t", a=4, c=4)[c]
                    sp.dma_start(dst, osb[32 * c:32 * c + 16, r, :, :]).then_inc(S["o_out"], 16)

            def load_nd(b, r):
                sp.wait_ge(S["o_out"], 64 * b + 64)
                need(sp, "x3_done", 3 * (b - 1) + 1)
                sp.dma_start(nd[:, r, :, :], o_dram[ds(b, 1)].rearrange("b c s t -> (b c) s t")).then_inc(nd_in[r], 16)

            for j in range(4):
                load_stack(0, j)
            move_max(0, 0)

            def load_w(c, r, first=False):
                if not first:
                    sp.wait_ge(S["whi_done"], c - 1)
                    sp.wait_ge(S["wlo_done"], c - 1)
                sp.dma_start(WST[r], wpack[ds(c, 1), :, :].rearrange("c p n -> (c p) n")).then_inc(w_in[r], 16)

            def sp_unit(i, j, first, last):
                b = 2 * i + j // 2
                if not (last and j == 3):
                    move_max(i + (j + 1) // 4, (j + 1) % 4)
                if j % 2 == 0 and not (first and j == 0):
                    store_o(b - 1, (j // 2 + 1) % 2)
                if not last:
                    load_stack(i + 1, j)
                if j % 2 == (0 if last else 1) and not (first and j == 1):
                    load_nd(b - 1, (j // 2 + 1) % 2)

            for j in range(4):
                sp_unit(0, j, True, False)
            with sp.Fori(1, B // 2 - 1) as i:
                for j in range(4):
                    sp_unit(i, j, False, False)
            load_w(0, 0, True)
            load_w(1, 1, True)
            for j in range(4):
                sp_unit(B // 2 - 1, j, False, True)
            store_o(B - 1, 1)
            load_nd(B - 1, 1)

            for c in range(2, 4):
                load_w(c, c % 2)
            with sp.Fori(1, NCH // 4) as i:
                for r in range(4):
                    load_w(4 * i + r, r % 2)
            load_w(NCH - 1, 0)
            for t in range(2):
                sp.wait_ge(S["y_done"], 4 * t + 4)
                sp.dma_start(out[4 * t:4 * t + 4].rearrange("b p l -> p b l"), X[:, 4 * t:4 * t + 4, :]).then_inc(S["out_done"], 16)
            sp.wait_ge(S["out_done"], 32)

        @block.scalar
        def _(act):
            for dst, src, name in (
                (ident[:, :], ident_d, "consts_in"), (heads[:, :], heads_d, "consts_in"),
                (skipc[:, :], skip.rearrange("(p a) -> p a", a=1), "consts_in"),
                (gain[:, :], gains.partition_broadcast(128), "consts_in"),
                (kw, kern.rearrange("(k p) f -> p k f", p=128), "kern_in"),
                (bqb[:, :], biasq.partition_broadcast(128), "kern_in"),
                (C[:, :, :], ctx.rearrange("b p l -> p b l"), "ctx_in"),
                (W3[:, :, :], wqkvT.rearrange("w p n -> p w n"), "attn_in"),
                (bqk_sb[:, :], bqk, "attn_in"), (bv_sb[:, :], bv.partition_broadcast(128), "attn_in"),
                (smt[:, :], maskT, "mask_in"), (msk[:, :], mask, "mask_in"),
                (MB[:, :, :], mask.partition_broadcast(128), "mask_in"),
                (rt[:, :, :], routerT.rearrange("(k p) e -> p k e", p=128), "router_in"),
                (early[:, :, :], earlier_d.partition_broadcast(128), "router_in"),
            ):
                act.dma_start(dst, src).then_inc(S[name], 16)
            act.wait_ge(S["consts_in"], 64)
            act.activation(tg[:, :], gain[:, :], ACT.Tanh).then_inc(S["tanh_done"], 1)
            for n in range(4):
                act.wait_ge(S["vt_ps"], n + 1)
                act.activation(VF[:, n * 512:(n + 1) * 512], PS[:, 4 + n, :], ACT.Copy).then_inc(S["vt_done"], 1)
            for n in range(4):
                act.wait_ge(S["k_done"], n + 1)
                act.activation(row(HI[:, :, :])[:, n * 512:(n + 1) * 512], KF[:, n * 512:(n + 1) * 512], ACT.Copy).then_inc(S["k_hi"], 1)
            act.wait_ge(S["xq_t"], 1)
            act.activation(row(qb), row(CG[:, :, :]), ACT.Copy, bias=-ROUND).then_inc(S["xq_done"], 1)
            act.wait_ge(S["qT_ps"], 1)
            act.activation(qbT.rearrange("p k b t -> p (k b t)"), banks(0, 2).bitcast(bf16), ACT.Copy).then_inc(S["qT_done"], 1)
            act.wait_ge(S["k_out"], 32)
            for n in range(4):
                act.wait_ge(S["q_done"], n + 1)
                act.activation(row(HI[:, :, :])[:, n * 512:(n + 1) * 512], QF[:, n * 512:(n + 1) * 512], ACT.Copy).then_inc(S["q_hi"], 1)

            def exps(i, j, q):
                u = 4 * i + j
                for g in range(4):
                    act.wait_ge(S["e_ps"], 8 * u + 4 * q + g + 1)
                    if g == 0:
                        need(act, "pv_done", 2 * u + q - 1)
                    act.activation(EXPS[q][:, 512 * g:512 * g + 512], PS[:, 4 + g % 2, :], ACT.Exp).then_inc(S["p_done"], 1)

            def evac_o(i, j, q):
                u, grp = 4 * i + j, 2 * (j % 2) + q
                act.wait_ge(S["pv_done"], 2 * u + q + 1)
                if grp == 0:
                    need(act, "o_out", 64 * (2 * i + j // 2 - 1))
                act.activation(osb[:, j // 2, grp, :], PS[:, 6 + q, 0:L], ACT.Copy).then_inc(S["o_sb"], 1)

            def act_unit(i, j, first, before_last=lambda: None):
                exps(i, j, 0)
                if not (first and j == 0):
                    evac_o(i + (j - 1) // 4, (j - 1) % 4, 1)
                exps(i, j, 1)
                before_last()
                evac_o(i, j, 0)

            for j in range(4):
                act_unit(0, j, True)
            with act.Fori(1, B // 2 - 1) as i:
                for j in range(4):
                    act_unit(i, j, False)

            def router_exp(t):
                b = slice(4 * t, 4 * t + 4)
                act.wait_ge(S["l_done"], 2 * t + 2)
                act.activation(EX[:, b, :], EX[:, b, :], ACT.Exp).then_inc(S["l_exp"], 1)
                act.activation(CB[:, b, NE:NE + 1], LG[:, b, NE:NE + 1], ACT.Exp, scale=-1.0).then_inc(S["l_exp"], 1)

            def split_w(i, r):
                act.wait_ge(w_in[r % 2], 16 * (2 * i + r // 2) + 16)
                if isinstance(i, int) and i == 0:
                    act.wait_ge(S["e_ps"], 8 * NU)
                    act.wait_ge(S["whi_done"], 2)
                else:
                    act.wait_ge(S["down_done"], 8 * i + r - 3)
                act.activation(WHI[r], WST[r % 2], ACT.Copy).then_inc(S["whi_done"], 1)

            def act_silu(i, m):
                n = 8 * i + m
                act.wait_ge(S["guc_g"], n + 1)
                need(act, "t_done", n - 1)
                act.activation(SIL[m % 2], PS[:, 4 + (3 * m) % 4, :], ACT.Silu).then_inc(S["sil_done"], 1)

            def act_hi(i, m):
                n = 8 * i + m
                act.wait_ge(S["h_done"], n + 1)
                need(act, "down_done", n - 1)
                act.activation(HHI[m % 2], HH[m % 2], ACT.Copy).then_inc(S["hhi_done"], 1)

            def act_chunks(i, first=False, last=False):
                for m in range(8):
                    if m < 2:
                        split_w(i, m + 2)
                    elif m == 6 or (m == 7 and not last):
                        split_w(i + 1, m - 6)
                    if first and m == 4:
                        router_exp(1)
                    act_silu(i, m)
                    act_hi(i, m)

            for j in range(4):
                act_unit(B // 2 - 1, j, False, before_last=lambda: router_exp(0) if j == 3 else None)
            evac_o(B // 2 - 1, 3, 1)
            act_chunks(0, first=True)
            with act.Fori(1, NCH // 4 - 1) as i:
                act_chunks(i)
            act_chunks(NCH // 4 - 1, last=True)
            for m in range(2):
                act_silu(NCH // 4, m)
                act_hi(NCH // 4, m)

        @block.gpsimd
        def _(pool):
            ps = Steps(pool, "pstep")

            def power(k, b=slice(0, B)):
                pool.wait_ge(S["var_done"], k)
                pool.tensor_tensor(rstd[:, b], ve[:, b], mhalf[:, b], ALU.pow).then_inc(S["rstd_done"], 1)

            pool.memset(mhalf[:, :], -0.5).then_inc(S["pstep"], 1)
            ps.n += 1
            ps.sync()
            power(1)
            pool.wait_ge(S["ctxT_in"], 32)
            pool.wait_ge(S["vt_done"], 4)
            vt16 = VT[:, :, :, :].rearrange("p k b t -> p (k b) t")
            cr16 = CR.rearrange("p k b t -> p (k b) t")

            def products(i):
                for j in range(4):
                    h = 4 * i + j
                    need(pool, "y_ps", h - 1)
                    v = vt16[:, :, ds(h * HD0, HD0)].unsqueeze(2).to_broadcast([128, 2 * B, HD0, HD0])
                    c = cr16[:, :, ds(h * HD0, HD0)].unsqueeze(3).to_broadcast([128, 2 * B, HD0, HD0])
                    o = KVP[:, j % 2, :].rearrange("p (n j i) -> p n j i", n=2 * B, j=HD0)
                    pool.tensor_tensor(o, v, c, ALU.mult).then_inc(S["kv_done"], 1)

            products(0)
            with pool.Fori(1, NH0 // 4) as i:
                products(i)

            pool.wait_ge(S["mask_in"], 48)
            aux = [0]

            def a(ins):
                aux[0] += 1
                after(pool, ins, "aux_done", aux[0])

            a(pool.tensor_scalar(mtmp[:, 0, :], msk[:, :], -NEG, None, ALU.mult))
            a(pool.tensor_scalar(mtmp[:, 1, :], msk[:, :], -1.0, 1.0, ALU.mult, ALU.add))
            a(pool.tensor_scalar(AQ[:, 0, :], mtmp[:, 0, :], 1.0, None, ALU.mult))
            a(pool.tensor_scalar(AQ[:, 1, :], mtmp[:, 0, :], 1.0, None, ALU.mult))
            a(pool.tensor_tensor(AQ[:, 2, :], mtmp[:, 0, :], AQ[:, 0, :].bitcast(f32), ALU.subtract))
            a(pool.tensor_tensor(AQ[:, 3, :], mtmp[:, 0, :], AQ[:, 0, :].bitcast(f32), ALU.subtract))
            a(pool.memset(AQ[:, 4:6, :].bitcast(f32), 0.0))
            a(pool.tensor_scalar(AK[:, 0, :], mtmp[:, 1, :], 1.0, None, ALU.mult))
            a(pool.tensor_scalar(AK[:, 2, :], mtmp[:, 1, :], 1.0, None, ALU.mult))
            a(pool.tensor_tensor(AK[:, 1, :], mtmp[:, 1, :], AK[:, 0, :].bitcast(f32), ALU.subtract))
            a(pool.tensor_tensor(AK[:, 3, :], mtmp[:, 1, :], AK[:, 0, :].bitcast(f32), ALU.subtract))
            a(pool.memset(AK[:, 4:6, :].bitcast(f32), 1.0))
            a(pool.memset(VA[:, :, :, :].rearrange("p n h (d s) -> p n h d s", s=2)[:, :, :, :, 1], 1.0))
            power(2)
            for n in range(4):
                c = slice(n * 512, (n + 1) * 512)
                pool.wait_ge(S["k_hi"], n + 1)
                pool.tensor_tensor(row(LO[:, :, :])[:, c], KF[:, c], row(HI[:, :, :])[:, c].bitcast(f32), ALU.subtract).then_inc(S["k_lo"], 1)
            pool.wait_ge(S["v_t"], 4)
            for n in range(4):
                v = VF[:, n * 512:(n + 1) * 512].rearrange("p (n h d) -> p n h d", n=4, h=NH1)
                m = smt[:, 4 * n:4 * n + 4].unsqueeze(2).unsqueeze(3).to_broadcast([128, 4, NH1, HD1])
                o = VA[:, 4 * n:4 * n + 4, :, :].rearrange("p n h (d s) -> p n h d s", s=2)[:, :, :, :, 0]
                pool.tensor_tensor(o, v, m, ALU.mult).then_inc(S["v_done"], 1)
            pool.wait_ge(S["aux_out"], 32)
            for t in QS + KS:
                pool.memset(row(t[:, :, :]).bitcast(f32), 0.0).then_inc(S["zeroed"], 1)
            power(3)
            pool.wait_ge(S["k_out"], 32)
            for n in range(4):
                c = slice(n * 512, (n + 1) * 512)
                pool.wait_ge(S["q_hi"], n + 1)
                pool.tensor_tensor(row(LO[:, :, :])[:, c], QF[:, c], row(HI[:, :, :])[:, c].bitcast(f32), ALU.subtract).then_inc(S["q_lo"], 1)
            pool.wait_ge(S["tanh_done"], 1)
            after(pool, pool.tensor_scalar(row(MB[:, :, :]), row(MB[:, :, :]), tg[:, 1:2], None, ALU.mult), "x3_done", 1)
            pool.wait_ge(S["v_done"], 4)

            def copy_v(b, r):
                need(pool, "pv_done", 4 * (b - 1))
                pool.tensor_copy(VR[:, r, :, :, :].rearrange("p k h c -> p (k h c)"),
                                 VA[:, ds(2 * b, 2), :, :].rearrange("p k h c -> p (k h c)")).then_inc(S["vr_done"], 1)

            def add_attention(b, r):
                pool.wait_ge(S["rden_done"], b + 1)
                n = nd[:, r, 0, :]
                after(pool, pool.tensor_tensor(n, n, rden[:, r, :], ALU.mult), "x3_done", 3 * b + 2)
                after(pool, pool.tensor_tensor(n, n, MB[:, ds(b, 1), :].rearrange("p b l -> p (b l)"), ALU.mult), "x3_done", 3 * b + 3)
                xb = X[:, ds(b, 1), :].rearrange("p b l -> p (b l)")
                pool.tensor_tensor(xb, xb, n, ALU.add).then_inc(S["x3_done"], 1)

            copy_v(0, 0)
            copy_v(1, 1)

            def pool_pair(i):
                for r in range(2):
                    copy_v(2 * i + r, r)
                    add_attention(2 * i + r - 2, r)

            def split_low(c, r):
                pool.wait_ge(S["whi_done"], c + 1)
                pool.tensor_tensor(WLO[r], WST[r % 2][:, 0:768], WHI[r][:, 0:768].bitcast(f32), ALU.subtract).then_inc(S["wlo_done"], 1)

            with pool.Fori(1, B // 2 - 1) as i:
                pool_pair(i)
            copy_v(B - 2, 0)
            add_attention(B - 4, 0)
            copy_v(B - 1, 1)
            power(4, slice(0, 4))
            pool.wait_ge(S["e_ps"], 8 * (NU - 2))
            for t in (CBT[0], ZR, CBT[1]):
                pool.memset(t.bitcast(f32), 0.0).then_inc(S["cbt_zero"], 1)
            split_low(0, 0)
            add_attention(B - 3, 1)
            split_low(1, 1)
            add_attention(B - 2, 0)
            add_attention(B - 1, 1)
            split_low(2, 2)
            power(5, slice(4, 8))
            split_low(3, 3)
            with pool.Fori(1, NCH // 4) as i:
                for r in range(4):
                    split_low(4 * i + r, r)
            split_low(NCH - 1, 0)

        @block.vector
        def _(dve):
            st = Steps(dve, "dstep")
            link, tick = st.link, st.tick

            def backwards(t):
                return t.rearrange("p b (k l) -> p b k l", k=2)[:, :, :, 127::-1]

            def statistics(bs):
                for b in bs:
                    tick(dve.bn_stats(bst[:, b, :], X[:, b, :]))

            def variance(bs):
                st.sync()
                for b in bs:
                    tick(dve.bn_aggr(mv[:, b, :], bst[:, b, :]))
                st.sync()
                b = slice(bs[0], bs[-1] + 1)
                dve.tensor_scalar(ve[:, b], mv[:, b, 1], EPS, None, ALU.add).then_inc(S["var_done"], 1)

            def normalise(k, bs):
                dve.wait_ge(S["rstd_done"], k)
                for b in bs:
                    xb = X[:, b:b + 1, :]
                    xb, o = (backwards(xb), XN[:, b:b + 1, :].rearrange("p b (k l) -> p b k l", k=2)) if k == 1 else (xb, XN[:, b:b + 1, :])
                    dve.tensor_scalar(o, xb, mv[:, b, 0:1], rstd[:, b:b + 1],
                                      ALU.subtract, ALU.mult).then_inc(S["xn_done"], 1)

            def layer_norm(k):
                statistics(range(B))
                variance(range(B))
                normalise(k, range(B))

            def scale_of(amax, scale, inv, zero):
                link(dve.tensor_scalar(zero, amax, 0.0, None, ALU.is_equal))
                link(dve.scalar_tensor_tensor(out=scale, in0=amax, scalar=1.0 / QMAX, in1=zero, op0=ALU.mult, op1=ALU.add))
                if inv is not None:
                    link(dve.reciprocal(inv, scale))

            link(dve.memset(ones[:, :], 1.0))
            dve.wait_ge(S["consts_in"], 64)
            dve.tensor_copy(identb[:, :], ident[:, :]).then_inc(S["consts_done"], 1)
            dve.tensor_scalar(heads[:, :], heads[:, :], skipc[:, 0:1], None, ALU.mult).then_inc(S["consts_done"], 1)
            dve.wait_ge(S["attn_in"], 48)
            link(dve.tensor_scalar(W3[:, 0, :], W3[:, 0, :], HD1 ** -0.5, None, ALU.mult))
            dve.tensor_scalar(bqk_sb[:, 0:1], bqk_sb[:, 0:1], HD1 ** -0.5, None, ALU.mult).then_inc(S["wq_done"], 1)
            dve.wait_ge(S["kt_ps"], 1)
            link(dve.tensor_reduce(akf[:, :], PS[:, 0, :].rearrange("p (f d) -> p f d", f=2), AX.X, ALU.max, apply_absolute_value=True))
            scale_of(akf[:, :], small[:, 0, 0:2], None, small[:, 1, 0:2])
            for f in range(2):
                dve.tensor_scalar(diag[:, f, :], ident[:, :], small[:, 0, f:f + 1], None, ALU.mult).then_inc(S["diag_done"], 1)
            dve.wait_ge(S["sk_ps"], 1)
            link(dve.tensor_copy(skb[:, :], PS[:, 1, 0:L]))
            link(dve.reciprocal(kinv, skb[:, :]))
            link(dve.tensor_tensor(kt2, kw, kinv.unsqueeze(1).to_broadcast([128, 2, L]), ALU.mult))
            link(dve.tensor_scalar(kt2, kt2, ROUND, ROUND - QMAX, ALU.add, ALU.max))
            dve.tensor_scalar(kq[:, :, :], kt2, ROUND + QMAX, ROUND, ALU.min, ALU.subtract).then_inc(S["kq_done"], 1)
            link(dve.tensor_reduce(small[:, 2, 0:1], bqb[:, :], AX.X, ALU.max, apply_absolute_value=True))
            scale_of(small[:, 2, 0:1], small[:, 3, 0:1], small[:, 4, 0:1], small[:, 5, 0:1])
            link(dve.tensor_scalar(bqb[:, :], bqb[:, :], small[:, 4, 0:1], ROUND, ALU.mult, ALU.add))
            link(dve.tensor_scalar(bqb[:, :], bqb[:, :], ROUND - QMAX, ROUND + QMAX, ALU.max, ALU.min))
            link(dve.tensor_scalar(bqb[:, :], bqb[:, :], ROUND, small[:, 3, 0:1], ALU.subtract, ALU.mult))

            dve.wait_ge(S["x_in"], 16)
            layer_norm(1)
            dve.wait_ge(S["xn_done"], B)
            dve.wait_ge(S["ctx_in"], 16)
            halved = "p b (k l) -> p b k l"
            dve.tensor_tensor(CG[:, :, :].rearrange(halved, k=2), XN[:, :, :].rearrange(halved, k=2), backwards(C[:, :, :]),
                              ALU.mult).then_inc(S["vc_done"], 1)
            dve.wait_ge(S["ctxT_in"], 32)
            ct16 = CT[:, :, :, :].rearrange("p k b t -> p (k b) t")
            ot16 = OT[:, :, :, :].rearrange("p k b t -> p (k b) t")

            def gate_rows(i):
                for j in range(4):
                    h, r = 4 * i + j, j % 2
                    dve.wait_ge(S["y_ps"], h + 1)
                    need(dve, "ot_part", h - 1)
                    c = ct16[:, :, ds(h * HD0, HD0)].unsqueeze(2).to_broadcast([128, 2 * B, HD0, HD0])
                    y = banks(2 * r, 2).rearrange("p (n j i) -> p n j i", n=2 * B, j=HD0)
                    yx = KVP[:, 2 + r, :].rearrange("p (n j i) -> p n j i", n=2 * B, j=HD0)
                    after(dve, dve.tensor_tensor(yx, y, c, ALU.mult), "yx_done", h + 1)
                    dve.tensor_reduce(ot16[:, :, ds(h * HD0, HD0)], yx, AX.X, ALU.add).then_inc(S["ot_part"], 1)

            gate_rows(0)
            dve.wait_ge(S["g_ps"], 4)
            dve.tensor_tensor(CG[:, :, :].rearrange(halved, k=2), backwards(banks(4, 4).rearrange("p (b l) -> p b l", b=B)),
                              C[:, :, :].rearrange(halved, k=2), ALU.mult).then_inc(S["cg_done"], 1)
            with dve.Fori(1, NH0 // 4) as i:
                gate_rows(i)
            dve.wait_ge(S["tanh_done"], 1)
            dve.wait_ge(S["cg_done"], 1)
            for n in range(4):
                c = slice(n * 512, (n + 1) * 512)
                dve.wait_ge(S["ot_ps"], n + 1)
                link(dve.tensor_tensor(QF[:, c], PS[:, 4 + n, :], QF[:, c], ALU.add))
                dve.scalar_tensor_tensor(out=row(X[:, :, :])[:, c], in0=QF[:, c], scalar=tg[:, 0:1],
                                         in1=row(X[:, :, :])[:, c], op0=ALU.mult, op1=ALU.add).then_inc(S["x1_done"], 1)
            dve.wait_ge(S["x1_done"], 4)

            dve.wait_ge(S["vc_done"], 1)
            layer_norm(2)
            dve.wait_ge(S["attn_in"], 48)
            dve.wait_ge(S["mask_in"], 48)
            for n in range(4):
                c = slice(n * 512, (n + 1) * 512)
                dve.wait_ge(S["kp_ps"], n + 1)
                dve.scalar_tensor_tensor(out=KF[:, c], in0=PS[:, n, :], scalar=bqk_sb[:, 1:2], in1=row(MB[:, :, :])[:, c],
                                         op0=ALU.add, op1=ALU.mult).then_inc(S["k_done"], 1)
            dve.wait_ge(S["xn_done"], 2 * B)
            amax, sx, inv, zero = (small[:, n, :] for n in (6, 7, 8, 9))
            link(dve.tensor_reduce(amax, XN[:, :, :], AX.X, ALU.max, apply_absolute_value=True))
            scale_of(amax, sx, inv, zero)
            for b in range(B):
                tick(dve.tensor_scalar(CG[:, b, :], XN[:, b, :], inv[:, b:b + 1], ROUND, ALU.mult, ALU.add))
            st.sync()
            after(dve, dve.tensor_scalar(QF, QF, ROUND - QMAX, ROUND + QMAX, ALU.max, ALU.min), "xq_t", 1)
            for n in range(4):
                dve.wait_ge(S["vp_ps"], n + 1)
                dve.tensor_tensor(VF[:, n * 512:(n + 1) * 512].rearrange("p (n o) -> p n o", n=4),
                                  PS[:, 4 + n, :].rearrange("p (n o) -> p n o", n=4),
                                  bv_sb[:, :].unsqueeze(1).to_broadcast([128, 4, 128]), ALU.add).then_inc(S["v_t"], 1)
            dve.wait_ge(S["xq_done"], 1)
            for b in range(B):
                if b % 2 == 0:
                    dve.wait_ge(S["f_ps"], b // 2 + 1)
                tick(dve.scalar_tensor_tensor(out=CG[:, b, :], in0=PS[:, 4 + b // 2, (b % 2) * L:(b % 2 + 1) * L], scalar=sx[:, b:b + 1],
                                              in1=skb[:, :], op0=ALU.mult, op1=ALU.mult))
            st.sync()
            link(dve.tensor_tensor(CG[:, :, :], CG[:, :, :], bqb[:, :].unsqueeze(1).to_broadcast([128, B, L]), ALU.add))
            ymax, sy, yinv, yz = (small[:, n, :] for n in (10, 11, 12, 13))
            link(dve.tensor_reduce(ymax, CG[:, :, :], AX.X, ALU.max))
            link(dve.tensor_scalar(ymax, ymax, 0.0, None, ALU.max))
            scale_of(ymax, sy, yinv, yz)
            for b in range(B):
                tick(dve.tensor_scalar(CG[:, b, :], CG[:, b, :], yinv[:, b:b + 1], ROUND, ALU.mult, ALU.add))
            link(dve.tensor_scalar(sy, sy, tg[:, 2:3], None, ALU.mult))
            link(dve.tensor_scalar(QF, QF, ROUND, ROUND + QMAX, ALU.max, ALU.min))
            for b in range(B):
                tick(dve.tensor_scalar(CG[:, b, :], CG[:, b, :], ROUND, sy[:, b:b + 1], ALU.subtract, ALU.mult))
            st.sync()
            dve.tensor_tensor(row(X[:, :, :]), row(X[:, :, :]), QF, ALU.add).then_inc(S["x2_done"], 1)
            dve.wait_ge(S["x2_done"], 1)

            layer_norm(3)
            dve.wait_ge(S["aux_done"], 13)
            for n in range(4):
                c = slice(n * 512, (n + 1) * 512)
                dve.wait_ge(S["q_ps"], n + 1)
                dve.scalar_tensor_tensor(out=QF[:, c], in0=PS[:, n, :], scalar=bqk_sb[:, 0:1], in1=row(MB[:, :, :])[:, c],
                                         op0=ALU.add, op1=ALU.mult).then_inc(S["q_done"], 1)

            def maximum(i, j, k):
                u = 4 * i + j
                dve.wait_ge(S["s_ps"], 4 * u + k + 1)
                if k == 0:
                    need(dve, "turned", u - 1)
                half, hb = k // 2, 4 * (k % 2)
                dve.tensor_reduce(negm[:, j % 2, hb:hb + 4, half], banks(tile_bank(j, k), 2).rearrange("p (h s) -> p h s", h=4),
                                  AX.X, ALU.max, negate=True).then_inc(S["s_used"], 1)

            def split_max(i, j):
                u = 4 * i + j
                dve.wait_ge(S["turned"], u + 1)
                if not (isinstance(i, int) and i == 0 and j < 2):
                    dve.wait_ge(m_in[(j + 2) % 4], 32 * (i + j // 2))
                src = PS[0:16, turn_bank(j), 0:128]
                after(dve, dve.tensor_copy(mT[:, j % 2, 0, :], src), "mt_done", 2 * u + 1)
                dve.tensor_tensor(mT[:, j % 2, 1, :], src, mT[:, j % 2, 0, :].bitcast(f32), ALU.subtract).then_inc(S["mt_done"], 1)

            def reciprocal_of(i, r):
                dve.wait_ge(nd_in[r], 16 * i + 16)
                dve.reciprocal(rden[:, r, :], nd[:, r, 1, :]).then_inc(S["rden_done"], 1)

            dve.wait_ge(S["q_done"], 4)
            for k in range(4):
                maximum(0, 0, k)
            maximum(0, 1, 0)
            split_max(0, 0)
            for k in range(1, 4):
                maximum(0, 1, k)

            early_b, late_b = range(0, 4), range(4, 8)

            def dve_unit(i, j, first, last):
                def max_ahead(k):
                    if not (last and j >= 2):
                        maximum(i + (j + 2) // 4, (j + 2) % 4, k)

                max_ahead(0)
                if not (last and j == 3):
                    split_max(i + (j + 1) // 4, (j + 1) % 4)
                if last and j == 2:
                    for r in range(2):
                        dve.wait_ge(w_in[r], 16)
                        dve.wait_ge(S["e_ps"], 8 * (NU - 3 + r))
                        dve.tensor_copy(WHI[r], WST[r]).then_inc(S["whi_done"], 1)
                max_ahead(1)
                max_ahead(2)
                if j % 2 == 0 and not first:
                    reciprocal_of(i - 1, j // 2)
                if last and j == 1:
                    dve.wait_ge(S["x3_done"], 3 * 4 + 1)
                    statistics(early_b)
                    variance(early_b)
                max_ahead(3)

            for j in range(4):
                dve_unit(0, j, True, False)
            with dve.Fori(1, B // 2 - 1) as i:
                for j in range(4):
                    dve_unit(i, j, False, False)
            for j in range(4):
                dve_unit(B // 2 - 1, j, False, True)

            def split_x(t):
                cols = slice(t * 512, (t + 1) * 512)
                dve.wait_ge(S["xt_ps"], t + 1)
                xt = VF.rearrange("p (k t) -> p k t", k=2)[:, :, cols]
                after(dve, dve.tensor_copy(xt, banks(2, 2).rearrange("p (k t) -> p k t", k=2)), "xt_done", t + 1)
                after(dve, dve.tensor_copy(XTH[:, :, cols], xt), "xth_done", t + 1)
                dve.tensor_tensor(XTL[:, :, cols], xt, XTH[:, :, cols].bitcast(f32), ALU.subtract).then_inc(S["xtl_done"], 1)

            def route(t):
                b = slice(4 * t, 4 * t + 4)
                n = B // 2
                dve.wait_ge(S["l_ps"], t + 1)
                link(dve.tensor_copy(LG[:, b, :], PS[:, 2, 0:n * (NE + 1)].rearrange("p (b e) -> p b e", b=n)))
                lg = LG[:, b, 0:NE]
                after(dve, dve.tensor_reduce(small[:, 14, b], lg, AX.X, ALU.max), "l_done", 2 * t + 1)
                after(dve, dve.tensor_tensor(EX[:, b, :], lg, small[:, 14, b].unsqueeze(2).to_broadcast([128, n, NE]), ALU.subtract), "l_done", 2 * t + 2)
                lj = lg.unsqueeze(2).to_broadcast([128, n, NE, NE])
                li = lg.unsqueeze(3).to_broadcast([128, n, NE, NE])
                tick(dve.tensor_tensor(R1, lj, li, ALU.is_gt))
                link(dve.tensor_tensor(R2, lj, li, ALU.is_equal))
                r1, r2 = (t.rearrange("p b i j -> p b (i j)") for t in (R1, R2))
                link(dve.tensor_tensor(r2, r2, early[:, :, :].rearrange("p i j -> p (i j)").unsqueeze(1).to_broadcast([128, n, NE * NE]), ALU.mult))
                link(dve.tensor_tensor(r1, r1, r2, ALU.add))
                link(dve.tensor_reduce(rank[:, b, :], R1, AX.X, ALU.add))

            def expert_weights(t):
                b = slice(4 * t, 4 * t + 4)
                dve.wait_ge(S["l_exp"], 2 * t + 2)
                tick(dve.tensor_scalar(CB[:, b, NE:NE + 1], CB[:, b, NE:NE + 1], 1.0, None, ALU.add))
                link(dve.scalar_tensor_tensor(out=EX[:, b, :], in0=rank[:, b, :], scalar=1.5, in1=EX[:, b, :], op0=ALU.is_lt, op1=ALU.mult))
                tick(dve.reciprocal(CB[:, b, NE:NE + 1], CB[:, b, NE:NE + 1]))
                link(dve.tensor_reduce(small[:, 14, b], EX[:, b, :], AX.X, ALU.add))
                link(dve.reciprocal(small[:, 15, b], small[:, 14, b]))
                dve.tensor_tensor(CB[:, b, 0:NE], EX[:, b, :], small[:, 15, b].unsqueeze(2).to_broadcast([128, B // 2, NE]), ALU.mult).then_inc(S["cb_done"], 1)

            def split_weights(t):
                dve.wait_ge(S["cbt_ps"], t + 1)
                high, low = CBT[t][0:NE + 1, :], CBT[t][32:32 + NE + 1, :]
                after(dve, dve.tensor_copy(high, PS[0:NE + 1, 3, :]), "cbt_done", 2 * t + 1)
                dve.tensor_tensor(low, PS[0:NE + 1, 3, :], high.bitcast(f32), ALU.subtract).then_inc(S["cbt_done"], 1)

            def gate_hidden(i, m):
                n = 8 * i + m
                dve.wait_ge(S["sil_done"], n + 1)
                dve.wait_ge(S["guc_u"], n + 1)
                after(dve, dve.tensor_tensor(TU[m % 2], SIL[m % 2], PS[:, 4 + (3 * m + 1) % 4, :], ALU.mult), "t_done", n + 1)
                dve.wait_ge(S["guc_c"], n + 1)
                need(dve, "hlo_done", n - 1)
                dve.tensor_tensor(HH[m % 2], TU[m % 2], PS[:, 4 + (3 * m + 2) % 4, :], ALU.mult).then_inc(S["h_done"], 1)
                dve.wait_ge(S["hhi_done"], n + 1)
                need(dve, "down_done", n - 1)
                dve.tensor_tensor(HLO[m % 2], HH[m % 2], HHI[m % 2].bitcast(f32), ALU.subtract).then_inc(S["hlo_done"], 1)

            normalise(4, early_b)
            dve.wait_ge(S["q_out"], 48)
            split_x(0)
            reciprocal_of(B // 2 - 1, 0)
            dve.wait_ge(S["cbt_zero"], 3)
            dve.wait_ge(S["router_in"], 32)
            route(0)
            expert_weights(0)
            split_weights(0)
            dve.wait_ge(S["x3_done"], 3 * (B - 1) + 1)
            statistics(late_b[:3])
            reciprocal_of(B // 2 - 1, 1)
            dve.wait_ge(S["o_out"], 64 * (B - 1))
            gate_hidden(0, 0)
            dve.wait_ge(S["x3_done"], 3 * B + 1)
            statistics(late_b[3:])
            variance(late_b)
            normalise(5, late_b)
            gate_hidden(0, 1)
            split_x(1)
            gate_hidden(0, 2)
            gate_hidden(0, 3)
            route(1)
            expert_weights(1)
            split_weights(1)
            for m in range(4, 8):
                gate_hidden(0, m)
            with dve.Fori(1, NCH // 4) as i:
                for m in range(8):
                    gate_hidden(i, m)
            for m in range(2):
                gate_hidden(NCH // 4, m)
            for b in range(B):
                dve.wait_ge(S["down_done"], 2 * NCH - 1 + b // 4)
                dve.scalar_tensor_tensor(out=X[:, b, :], in0=PS[:, b // 2, (b % 2) * L:(b % 2 + 1) * L], scalar=tg[:, 3:4],
                                         in1=X[:, b, :], op0=ALU.mult, op1=ALU.add).then_inc(S["y_done"], 1)

        @block.tensor
        def _(pe):
            mm = pe.matmul
            pe.wait_ge(S["consts_in"], 64)
            pe.wait_ge(S["kern_in"], 32)
            for f in range(2):
                for d in range(2):
                    last = pe.transpose(PS[:, 0, f * L + d * 128:f * L + d * 128 + 128], kw[:, d, f * 128:(f + 1) * 128], ident[:, :])
            last.then_inc(S["kt_ps"], 1)
            pe.wait_ge(S["diag_done"], 2)
            for f in range(2):
                last = mm(PS[:, 1, f * 128:(f + 1) * 128], ones[:, :], diag[:, f, :], start=True, stop=True)
            last.then_inc(S["sk_ps"], 1)
            for n in range(4):
                k = n // 2
                for b in range(4 * (n % 2), 4 * (n % 2) + 4):
                    pe.wait_ge(S["xn_done"], b + 1)
                    last = pe.transpose(PS[:, 4 + n, (b % 4) * 128:(b % 4 + 1) * 128], XN[:, b, k * 128:(k + 1) * 128], ident[:, :])
                last.then_inc(S["vt_ps"], 1)
            pe.wait_ge(S["vt_done"], 4)
            pe.wait_ge(S["vc_done"], 1)
            pe.wait_ge(S["consts_done"], 2)
            for n in range(4):
                mm(PS[:, 4 + n, :], heads[:, :], QF[:, n * 512:(n + 1) * 512], start=True, stop=True).then_inc(S["g_ps"], 1)
            pe.wait_ge(S["kq_done"], 1)

            def convolve(i):
                for j in range(4):
                    h, r = 4 * i + j, j % 2
                    pe.wait_ge(T_in[j], 16 * i + 16)
                    pe.wait_ge(S["kv_done"], h + 1)
                    need(pe, "yx_done", h - 1)
                    kv = KVP[:, r, :].rearrange("p (k n) -> p k n", k=2)
                    near, far = T[:, j, 0:128], T[:, j, 128:256]
                    mm(PS[:, 2 * r, :], near, kv[:, 0, :], start=True, stop=True)
                    mm(PS[:, 2 * r + 1, :], far, kv[:, 0, :], start=True, stop=False)
                    mm(PS[:, 2 * r + 1, :], near, kv[:, 1, :], start=False, stop=True).then_inc(S["y_ps"], 1)

            convolve(0)
            with pe.Fori(1, NH0 // 4) as i:
                convolve(i)
            pe.wait_ge(S["ot_part"], NH0)
            pe.wait_ge(S["cg_done"], 1)
            for n in range(4):
                for b in (2 * n, 2 * n + 1):
                    for k in range(2):
                        last = pe.transpose(PS[:, 4 + n, (b % 2) * L + k * 128:(b % 2) * L + (k + 1) * 128], OT[:, k, b, :], ident[:, :])
                last.then_inc(S["ot_ps"], 1)
            pe.wait_ge(S["attn_in"], 48)
            pe.wait_ge(S["ctx_in"], 16)
            pe.wait_ge(S["yx_done"], NH0)
            for n in range(4):
                mm(PS[:, n, :], W3[:, 1, :], row(C[:, :, :])[:, n * 512:(n + 1) * 512], start=True, stop=True).then_inc(S["kp_ps"], 1)
            for n in range(4):
                pe.wait_ge(S["x1_done"], n + 1)
                for b in (2 * n, 2 * n + 1):
                    for k in range(2):
                        last = mm(PS[:, 4 + n, (b % 2) * L + k * 128:(b % 2) * L + (k + 1) * 128], C[:, b, k * 128:(k + 1) * 128],
                                  W3[:, 2, :], start=True, stop=True)
                last.then_inc(S["vp_ps"], 1)
            pe.wait_ge(S["xq_done"], 1)
            pe.wait_ge(S["k_done"], 4)
            qT = banks(0, 2).bitcast(bf16).rearrange("p (k b t) -> p k b t", k=2, b=B)
            for k in range(2):
                for b in range(B):
                    last = pe.transpose(qT[:, k, b, :], qb[:, b, k * 128:(k + 1) * 128], identb[:, :])
            last.then_inc(S["qT_ps"], 1)
            pe.wait_ge(S["qT_done"], 1)
            pe.wait_ge(S["v_t"], 4)
            for b in range(B):
                for k in range(2):
                    last = mm(PS[:, 4 + b // 2, (b % 2) * L:(b % 2 + 1) * L], qbT[:, k, b, :], kq[:, k, :], start=(k == 0), stop=(k == 1))
                if b % 2:
                    last.then_inc(S["f_ps"], 1)
            pe.wait_ge(S["wq_done"], 1)
            for n in range(4):
                pe.wait_ge(S["xn_done"], 2 * B + 2 * n + 2)
                mm(PS[:, n, :], W3[:, 0, :], row(XN[:, :, :])[:, n * 512:(n + 1) * 512], start=True, stop=True).then_inc(S["q_ps"], 1)

            def max_tile(i, j, k):
                u = 4 * i + j
                if k == 0:
                    pe.wait_ge(st_in[j], 80 * i + 80)
                need(pe, *(("s_used", 4 * u - 1), ("s_used", 4 * u + 1), ("mt_done", 2 * u), ("s_used", 4 * u + 2))[k])
                for n in range(4):
                    h, half = 4 * (k % 2) + n, k // 2
                    last = mm(banks(tile_bank(j, k), 2)[:, n * L:(n + 1) * L], QS[j][:, h, half * 128:(half + 1) * 128],
                              KS[j][:, h, :], start=True, stop=True)
                last.then_inc(S["s_ps"], 1)

            def turn_max(i, j):
                u = 4 * i + j
                pe.wait_ge(S["s_used"], 4 * u + 4)
                pe.transpose(PS[0:16, turn_bank(j), 0:128], negm[:, j % 2, :, :].rearrange("p h c -> p (h c)"),
                             ident[:, :]).then_inc(S["turned"], 1)

            def score(i, j, g):
                if g == 0:
                    pe.wait_ge(m_in[j], 32 * i + 32)
                need(pe, "p_done", 8 * (4 * i + j) + g - 1)
                for k in range(2):
                    last = mm(PS[:, 4 + g % 2, k * L:(k + 1) * L], KS[j][:, g, k * 128:(k + 1) * 128],
                              QS[j][:, g, :], start=True, stop=True)
                last.then_inc(S["e_ps"], 1)

            def weigh(i, j, q):
                u = 4 * i + j
                if q == 0 and j % 2 == 0:
                    pe.wait_ge(S["vr_done"], 2 * i + j // 2 + 1)
                pe.wait_ge(S["p_done"], 8 * u + 4 * q + 4)
                need(pe, "o_sb", 2 * u + q - 1)
                for k in range(2):
                    for g in range(4):
                        h = 8 * (j % 2) + 4 * q + g
                        last = mm(PS[32 * g:32 * g + 16, 6 + q, 0:L], VR[:, (j // 2) % 2, k, h, :],
                                  EXPS[q][:, 512 * g + k * L:512 * g + (k + 1) * L], start=(k == 0), stop=(k == 1))
                last.then_inc(S["pv_done"], 1)

            def pe_unit(i, j, first, last, between=None):
                def max_ahead(k):
                    if not (last and j >= 2):
                        max_tile(i + (j + 2) // 4, (j + 2) % 4, k)

                score(i, j, 0)
                score(i, j, 1)
                max_ahead(0)
                if not (last and j == 3):
                    turn_max(i + (j + 1) // 4, (j + 1) % 4)
                score(i, j, 2)
                if not (first and j == 0):
                    weigh(i + (j - 1) // 4, (j - 1) % 4, 1)
                score(i, j, 3)
                max_ahead(1)
                score(i, j, 4)
                score(i, j, 5)
                if between:
                    between()
                max_ahead(2)
                score(i, j, 6)
                weigh(i, j, 0)
                score(i, j, 7)
                max_ahead(3)

            pe.wait_ge(S["q_done"], 4)
            for k in range(4):
                max_tile(0, 0, k)
            max_tile(0, 1, 0)
            turn_max(0, 0)
            for k in range(1, 4):
                max_tile(0, 1, k)
            for j in range(4):
                pe_unit(0, j, True, False)
            with pe.Fori(1, B // 2 - 1) as i:
                for j in range(4):
                    pe_unit(i, j, False, False)
            def turn_x(t):
                for k in range(2):
                    for b in range(4 * t, 4 * t + 4):
                        pe.wait_ge(S["xn_done"], 3 * B + b + 1)
                        last = pe.transpose(PS[:, 2 + k, (b % 4) * 128:(b % 4 + 1) * 128], XN[:, b, k * 128:(k + 1) * 128], ident[:, :])
                last.then_inc(S["xt_ps"], 1)

            def logits(t):
                pe.wait_ge(S["xt_done"], t + 1)
                for b in range(4 * t, 4 * t + 4):
                    for k in range(2):
                        last = mm(PS[:, 2, (b % 4) * (NE + 1):(b % 4 + 1) * (NE + 1)], XT[:, k, b, :], rt[:, k, :], start=(k == 0), stop=(k == 1))
                last.then_inc(S["l_ps"], 1)

            def turn_weights(t):
                pe.wait_ge(S["cb_done"], t + 1)
                for b in range(4 * t, 4 * t + 4):
                    last = pe.transpose(PS[0:NE + 1, 3, (b % 4) * 128:(b % 4 + 1) * 128], CB[:, b, :], ident[:, :])
                last.then_inc(S["cbt_ps"], 1)

            def clear(t):
                for n in range(2 * t, 2 * t + 2):
                    mm(PS[:, n, :], ZR[:, 0:128], ZR, start=True, stop=False, skip_group_check=True)

            def gate_up(i, m, t, before_weights=None):
                n, r = 8 * i + m, m % 4 if t == m // 4 else 0
                cols = slice(512 * t, 512 * t + 512)
                if t == 0:
                    pe.wait_ge(S["whi_done"], 4 * i + r + 1)
                    pe.wait_ge(S["wlo_done"], 4 * i + r + 1)
                for part, ready, count, signal in ((0, "h_done", n - 1, "guc_g"), (1, "sil_done", n, "guc_u")):
                    need(pe, ready, count)
                    o = PS[:, 4 + (3 * m + part) % 4, :]
                    for k in range(2):
                        c = slice(256 * part + 128 * k, 256 * part + 128 * k + 128)
                        mm(o, WHI[r][:, c], XTH[:, k, cols], start=(k == 0), stop=False)
                        mm(o, WHI[r][:, c], XTL[:, k, cols], start=False, stop=False)
                        last = mm(o, WLO[r][:, c], XTH[:, k, cols], start=False, stop=(k == 1))
                    last.then_inc(S[signal], 1)
                if before_weights:
                    before_weights()
                need(pe, "t_done", n)
                mm(PS[:, 4 + (3 * m + 2) % 4, :], WHI[r][:, 768:896], CBT[t], start=True, stop=True).then_inc(S["guc_c"], 1)

            def down(i, m, t):
                n, r = 8 * i + m, m % 4 if t == m // 4 else 0
                pe.wait_ge(S["hhi_done"], n + 1)
                pe.wait_ge(S["hlo_done"], n + 1)
                for b in range(4):
                    o = PS[:, 2 * t + b // 2, (b % 2) * L:(b % 2 + 1) * L]
                    c = slice(128 * b, 128 * b + 128)
                    mm(o, HHI[m % 2][:, c], WHI[r][:, 512:768], start=False, stop=False, skip_group_check=True)
                    mm(o, HHI[m % 2][:, c], WLO[r][:, 512:768], start=False, stop=False, skip_group_check=True)
                    last = mm(o, HLO[m % 2][:, c], WHI[r][:, 512:768], start=False, stop=False, skip_group_check=True)
                last.then_inc(S["down_done"], 1)

            def pe_chunks(i):
                for m in range(8):
                    gate_up(i + (m + 1) // 8, (m + 1) % 8, (m + 1) % 8 // 4)
                    down(i, m, m // 4)

            def weights_of_second():
                turn_weights(1)
                pe.wait_ge(S["cbt_done"], 4)
                clear(1)

            for j in range(3):
                pe_unit(B // 2 - 1, j, False, True)
            pe.wait_ge(S["mt_done"], 2 * NU)
            turn_x(0)
            pe.wait_ge(S["router_in"], 32)
            pe_unit(B // 2 - 1, 3, False, True, lambda: logits(0))
            weigh(B // 2 - 1, 3, 1)
            turn_weights(0)
            pe.wait_ge(S["cbt_zero"], 3)
            clear(0)
            pe.wait_ge(S["xtl_done"], 1)
            pe.wait_ge(S["o_sb"], 2 * NU)
            pe.wait_ge(S["cbt_done"], 2)
            gate_up(0, 0, 0)
            gate_up(0, 1, 0)
            down(0, 0, 0)
            gate_up(0, 2, 0)
            turn_x(1)
            down(0, 1, 0)
            gate_up(0, 3, 0)
            logits(1)
            down(0, 2, 0)
            down(0, 3, 0)
            pe.wait_ge(S["xtl_done"], 2)
            gate_up(0, 4, 1, weights_of_second)
            for m in range(4, 8):
                gate_up((m + 1) // 8, (m + 1) % 8, (m + 1) % 8 // 4)
                down(0, m, 1)
            with pe.Fori(1, NCH // 4) as i:
                pe_chunks(i)
            gate_up(NCH // 4, 1, 1)
            down(NCH // 4, 0, 0)
            down(NCH // 4, 1, 1)


def kernel(**inputs):
    import numpy as np
    import concourse.bacc as bacc
    from concourse.bass_utils import run_bass_kernel_spmd

    a = {n: np.asarray(v) for n, v in inputs.items()}
    f = np.float32
    pad = NCH * 128 - NI
    turn = np.arange(128).reshape(NH1, HD1).T.reshape(-1)

    def hidden(experts, shared):
        w = np.concatenate([experts.transpose(1, 0, 2).reshape(L, NE * EI), shared, np.zeros((L, pad), f)], 1)
        return w.reshape(2, 128, NCH, 128).transpose(2, 1, 0, 3).reshape(NCH, 128, 256)

    down = np.concatenate([a["L1_ffn_w_down"].reshape(NE * EI, L), a["L1_ffn_sw_down"], np.zeros((pad, L), f)], 0)
    owner = np.minimum(np.arange(NCH * 128) // EI, NE)
    sel = np.zeros((128, NCH * 128), f)
    for e in range(NE + 1):
        sel[[e, 32 + e]] = owner == e
    wpack = np.concatenate([hidden(a["L1_ffn_w_gate"], a["L1_ffn_sw_gate"]), hidden(a["L1_ffn_w_up"], a["L1_ffn_sw_up"]),
                            down.reshape(NCH, 128, L), sel.reshape(128, NCH, 128).transpose(1, 0, 2)], 2)
    mask = a["mask_Bx1x2048_fk1"].reshape(B, L)
    ctxT = a["ctx_2048"].transpose(2, 0, 1)
    arrays = {
        "x": a["x"], "ctx": a["ctx_2048"], "ctxT": np.stack([ctxT, ctxT.reshape(2, 128, B, TOK)[:, ::-1].reshape(L, B, TOK)]),
        "mask": mask, "maskT": mask.reshape(B, 2, 128).transpose(2, 0, 1).reshape(128, 2 * B),
        "kpad": np.concatenate([np.zeros((NH0, L), f), a["L0_xattn_k"]], 1),
        "skip": a["fside_S2_0"], "gains": np.concatenate([a["g_xattn"], a["g_ffn"]]),
        "kern": a["L0_ffn_kernel"], "biasq": a["L0_ffn_bias"],
        "wqkvT": np.stack([a["L1_xattn_Wq"][turn].T, a["L1_xattn_Wk"][turn].T, a["L1_xattn_Wv"].T]),
        "bqk": np.stack([a["L1_xattn_bq"][turn], a["L1_xattn_bk"][turn]], 1), "bv": a["L1_xattn_bv"],
        "routerT": np.concatenate([a["L1_ffn_gate_w"].T, a["L1_ffn_shared_gate_w"]], 1),
        "wpack": wpack, "ident_d": np.eye(128, dtype=f),
        "heads_d": np.kron(np.eye(NH0, dtype=f), np.ones((HD0, HD0), f)),
        "earlier_d": np.tril(np.ones((NE, NE), f), -1),
    }
    arrays = {n + "_in": np.ascontiguousarray(v) for n, v in arrays.items()}
    nc = bacc.Bacc("TRN2", target_bir_lowering=False, num_devices=1)
    args = [nc.dram_tensor(n, v.shape, mybir.dt.from_np(v.dtype), kind="ExternalInput").ap() for n, v in arrays.items()]
    out = nc.dram_tensor("out", (B, TOK, L), mybir.dt.float32, kind="ExternalOutput").ap()
    flamingo_program(nc, *args, out)
    r = run_bass_kernel_spmd(nc, [arrays], core_ids=[0])
    return r.results[0]["out"]
```

```python
import concourse.bass as bass
from concourse import mybir
from contextlib import ExitStack

B, TOK, L = 8, 128, 256
NH0, HD0 = 16, 8
NH1, HD1 = 16, 8
NE, EI, SI = 8, 176, 704
NI = NE * EI + SI
NCH = -(-NI // 128)
WCOLS = 2 * 128 + 2 * 128 + L + 128
NEG = 1000000.0
QMAX = 127.0
ROUND = 12582912.0
EPS = 1e-05
NU = 2 * B
HU = NH1 // 2


def flamingo_program(nc, x, ctx, ctxT, mask, maskT, kpad, skip, gains, kern, biasq, wqkvT, bqk, bv,
                     routerT, wpack, ident_d, heads_d, earlier_d, out):
    f32, f32r, bf16 = mybir.dt.float32, mybir.dt.float32r, mybir.dt.bfloat16
    ALU, ACT, AX = mybir.AluOpType, mybir.ActivationFunctionType, mybir.AxisListType
    ds = bass.ds
    stack = ExitStack()
    with stack:
        def sb(name, shape, dt=f32):
            return stack.enter_context(nc.sbuf_tensor(name, shape, dt))

        def sem(name):
            return stack.enter_context(nc.semaphore(name))

        X = sb("X", [128, B, L])
        C = sb("C", [128, B, L])
        XN = sb("XN", [128, B, L])
        CT = sb("CT", [128, 2, B, TOK])
        VT = sb("VT", [128, 2, B, TOK])
        OT = sb("OT", [128, 2, B, TOK])
        CG = sb("CG", [128, B, L])
        T = sb("T", [128, 4, L])
        KVP = sb("KVP", [128, 4, 1024])
        ident = sb("ident", [128, 128])
        identb = sb("identb", [128, 128], bf16)
        ones = sb("ones", [128, 128])
        heads = sb("heads", [128, 128])
        skipc = sb("skipc", [128, 1])
        gain = sb("gain", [128, 4])
        tg = sb("tg", [128, 4])
        mhalf = sb("mhalf", [128, B])
        rnd = sb("rnd", [128, 1])
        bst = sb("bst", [128, B, 6])
        mv = sb("mv", [128, B, 2])
        ve = sb("ve", [128, B])
        rstd = sb("rstd", [128, B])
        kq = sb("kq", [128, 2, L], bf16)
        akf = sb("akf", [128, 2])
        skb = sb("skb", [128, L])
        bqb = sb("bqb", [128, L])
        small = sb("small", [128, 16, B])
        W3 = sb("W3", [128, 3, 128])
        bqk_sb = sb("bqk_sb", [128, 2])
        bv_sb = sb("bv_sb", [128, 128])
        smt = sb("smt", [128, 2 * B])
        MB = sb("MB", [128, B, L])
        msk = sb("msk", [B, L])
        HI = sb("HI", [128, B, L], f32r)
        LO = sb("LO", [128, B, L], f32r)
        VA = sb("VA", [128, 2 * B, NH1, 16])
        VR = sb("VR", [128, 2, 2, NH1, 16])
        QS = [sb(f"QS{j}", [128, HU, L], f32r) for j in range(4)]
        KS = [sb(f"KS{j}", [128, HU, L], f32r) for j in range(4)]
        negm = sb("negm", [128, 2, HU, 2])
        mT = sb("mT", [16, 2, 2, 128], f32r)
        osb = sb("osb", [128, 2, 4, L])
        rden = sb("rden", [128, 2, L])
        def row(t):
            return t.rearrange("p h l -> p (h l)")

        kw, kt2 = osb[:, 0, 0:2, :], osb[:, 0, 2:4, :]
        diag = osb[:, 1, 0:2, :].rearrange("p a (f c) -> p (a f) c", f=2)
        mtmp = osb[0:B, 1, 2:4, :]
        nd = T[:, :, :].rearrange("p (r s) l -> p r s l", r=2)
        qb = T[:, :, :].rearrange("p j l -> p (j l)").bitcast(bf16).rearrange("p (b l) -> p b l", b=B)
        qbT = VR[:, :, :, :, :].rearrange("p r k h c -> p (r k h c)").bitcast(bf16).rearrange("p (k b t) -> p k b t", k=2, b=B)
        CR = VA[:, 0:B, :, :].rearrange("p b h c -> p (b h c)").rearrange("p (k b t) -> p k b t", k=2, b=B)
        KF = OT[:, :, :, :].rearrange("p k b t -> p (k b t)")
        VF = VT[:, :, :, :].rearrange("p k b t -> p (k b t)")
        QF = row(CG[:, :, :])
        AQ = row(HI[0:B, 0:6, :]).rearrange("p (r l) -> p r l", r=6)
        AK = row(LO[0:B, 0:6, :]).rearrange("p (r l) -> p r l", r=6)
        EXPS = [KVP[:, 2 * r:2 * r + 2, :].rearrange("p a n -> p (a n)") for r in range(2)]
        XT = VT
        XTH = row(HI[:, :, :]).rearrange("p (k t) -> p k t", k=2)
        XTL = row(LO[:, :, :]).rearrange("p (k t) -> p k t", k=2)
        WST = [row(C[:, :, :])[:, r * 1024:r * 1024 + WCOLS] for r in range(2)]
        SIL = [KVP[:, 2, r * 512:(r + 1) * 512] for r in range(2)]
        TU = [KVP[:, 3, r * 512:(r + 1) * 512] for r in range(2)]
        HH = [osb[:, 0, 2 * r:2 * r + 2, :].rearrange("p a l -> p (a l)") for r in range(2)]
        WHI = [row(QS[r][:, :, :])[:, 0:WCOLS] for r in range(4)]
        WLO = [row(KS[r][:, :, :])[:, 0:768] for r in range(4)]
        HHI = [row(QS[r][:, :, :])[:, 1024:1536] for r in range(2)]
        HLO = [row(KS[r][:, :, :])[:, 1024:1536] for r in range(2)]
        CBT = [row(QS[t][:, :, :])[:, 1536:2048] for t in range(2)]
        ZR = row(KS[0][:, :, :])[:, 1536:2048]
        R1, R2 = (QF[:, c:c + 256].rearrange("p (b i j) -> p b i j", b=B // 2, i=NE) for c in (1536, 1792))
        rt = sb("rt", [128, 2, NE + 1])
        LG = sb("LG", [128, B, NE + 1])
        EX = sb("EX", [128, B, NE])
        early = sb("early", [128, NE, NE])
        rank = sb("rank", [128, B, NE])
        CB = sb("CB", [128, B, NE + 1])

        PS = stack.enter_context(nc.psum_tensor("PS", [128, 8, 512], f32))

        def banks(a, n):
            return PS[:, a:a + n, :].rearrange("p a c -> p (a c)")

        def scratch(name, shape):
            return nc.dram_tensor(name, shape, f32, kind="Internal").ap()

        q_dram = scratch("q_dram", [B, 3, 128, L])
        k_dram = scratch("k_dram", [B, 2, 128, L])
        aq_dram = scratch("aq_dram", [B, 6, L])
        ak_dram = scratch("ak_dram", [B, 6, L])
        o_dram = scratch("o_dram", [B, 128, 2, L])

        names = """x_in ctx_in cr_in ct_in consts_in kern_in attn_in msk_in mask_in router_in
            consts_done wq_done tanh_done var_done rstd_done xn_done vt_ps vt_done vc_done g_ps cg_done skip_done
            dstep kt_ps diag_done sk_ps skb_done kq_done kv_done y_ps yx_done ot_part ot_ps x1_done
            kp_ps k_done k_hi k_lo k_out vp_ps v_t v_b v_done va_ones aux_done aux_low aux_out zeroed const_set
            xs_done xr_done xq_t xq_done qT_ps qT_done f_ps ys_done yr_done x2_done q_ps q_done q_hi q_lo q_out
            s_ps s_used mt_done e_ps p_done pv_done o_sb o_out
            vr_done turned rden_done x3_done xt_ps xt_done xth_done xtl_done l_ps l_done l_exp cb_done
            cbt_ps cbt_done cbt_zero whi_done wlo_done
            guc_g guc_u guc_c sil_done t_done h_done hhi_done hlo_done down_done y_done out_done""".split()
        S = {n: sem(n) for n in names}
        T_in = [sem(f"T_in{j}") for j in range(4)]
        st_in = [sem(f"st_in{j}") for j in range(4)]
        m_in = [sem(f"m_in{j}") for j in range(4)]
        w_in = [sem(f"w_in{j}") for j in range(2)]
        nd_in = [sem(f"nd_in{j}") for j in range(2)]

        block = stack.enter_context(nc.Block())

        def need(eng, name, n):
            if not (isinstance(n, int) and n <= 0):
                eng.wait_ge(S[name], n)

        def after(eng, ins, name, n):
            ins.then_inc(S[name], 1)
            eng.wait_ge(S[name], n)

        def tile_bank(j, k):
            return 2 * ((5 * j + (k or -1)) % 2)

        def turn_bank(j):
            return 2 * ((j + 1) % 2)

        def backwards(t):
            return t.rearrange("p b (k l) -> p b k l", k=2)[:, :, :, 127::-1]

        class Steps:

            def __init__(self, eng, name):
                self.eng, self.name, self.n = eng, name, 0

            def tick(self, ins):
                ins.then_inc(S[self.name], 1)
                self.n += 1

            def sync(self):
                self.eng.wait_ge(S[self.name], self.n)

            def link(self, ins):
                self.tick(ins)
                self.sync()

        @block.sync
        def _(sp):
            sp.dma_start(X[:, :, :], x.rearrange("b p l -> p b l")).then_inc(S["x_in"], 16)
            sp.dma_start(CR, ctxT[1].rearrange("(k p) b t -> p k b t", p=128)).then_inc(S["cr_in"], 16)
            shifted = bass.AP(kpad.tensor, L - 127, [[2 * L, NH0], [1, 128], [1, L]])

            def load_T(i):
                for j in range(4):
                    need(sp, "y_ps", 4 * i + j - 3)
                    sp.dma_start(T[:, j, :], shifted[ds(4 * i + j, 1), :, :].rearrange("h p l -> (h p) l")).then_inc(T_in[j], 16)

            load_T(0)
            sp.dma_start(CT[:, :, :, :], ctxT[0].rearrange("(k p) b t -> p k b t", p=128)).then_inc(S["ct_in"], 16)
            sp.wait_ge(S["aux_low"], 2)
            sp.dma_start(aq_dram, AQ.bitcast(f32)).then_inc(S["aux_out"], 16)
            sp.dma_start(ak_dram, AK.bitcast(f32)).then_inc(S["aux_out"], 16)
            with sp.Fori(1, NH0 // 4) as i:
                load_T(i)

            def store_part(dst, part, src, b=slice(0, B)):
                return sp.dma_start(dst[b, part].rearrange("b p t -> p b t"), src[:, b, :].bitcast(f32))

            def store_q(n):
                b = slice(2 * n, 2 * n + 2)
                sp.wait_ge(S["q_hi"], n + 1)
                store_part(q_dram, 0, HI, b).then_inc(S["q_out"], 16)
                store_part(q_dram, 2, HI, b).then_inc(S["q_out"], 16)
                sp.wait_ge(S["q_lo"], n + 1)
                store_part(q_dram, 1, LO, b).then_inc(S["q_out"], 16)

            sp.wait_ge(S["k_hi"], 4)
            store_part(k_dram, 0, HI).then_inc(S["k_out"], 16)
            sp.wait_ge(S["k_lo"], 4)
            store_part(k_dram, 1, LO).then_inc(S["k_out"], 16)
            store_q(0)
            sp.wait_ge(S["k_out"], 32)
            sp.wait_ge(S["aux_out"], 32)
            sp.wait_ge(S["zeroed"], 8)
            sp.wait_ge(S["q_out"], 48)

            def stack_rows(src, parts, b, half, n):
                v = bass.AP(src.tensor, half * HU * L, [[128 * L, parts * (B - 1) + n], [NH1 * L, 2 * HD1], [1, HU * L]])
                return v[ds(parts * b, n), :, :]

            def load_stack(i, j):
                b, half = 2 * i + j // 2, j % 2
                need(sp, "e_ps", 8 * (4 * i + j - 3))
                sp.dma_start(QS[j][0:32, :, :].bitcast(f32), stack_rows(q_dram, 3, b, half, 2)).then_inc(st_in[j], 16)
                for r in range(2):
                    sp.dma_start(KS[j][16 * r:16 * r + 16, :, :].bitcast(f32), stack_rows(k_dram, 2, b, half, 1)).then_inc(st_in[j], 16)
                for dst, src in ((QS, aq_dram), (KS, ak_dram)):
                    rows = src[ds(b, 1), :, :].rearrange("b r t -> (b r) t").unsqueeze(1).to_broadcast([6, HU, L])
                    sp.dma_start(dst[j][32:38, :, :].bitcast(f32), rows).then_inc(st_in[j], 16)

            def move_max(i, j):
                sp.wait_ge(S["mt_done"], 2 * (4 * i + j) + 2)
                for s in range(2):
                    sp.dma_start(QS[j][36 + s:37 + s, :, :].bitcast(f32).rearrange("p h (c t) -> p (h c) t", c=2),
                                 mT[:, j % 2, s, :].bitcast(f32)).then_inc(m_in[j], 16)

            def store_o(b, r):
                sp.wait_ge(S["o_sb"], 4 * b + 4)
                for c in range(4):
                    dst = o_dram[ds(b, 1)].rearrange("b (a c d) s t -> (b c) (d s) a t", a=4, c=4)[c]
                    sp.dma_start(dst, osb[32 * c:32 * c + 16, r, :, :]).then_inc(S["o_out"], 16)

            def load_nd(b, r):
                sp.wait_ge(S["o_out"], 64 * b + 64)
                need(sp, "x3_done", 3 * (b - 1) + 1)
                sp.dma_start(nd[:, r, :, :], o_dram[ds(b, 1)].rearrange("b c s t -> (b c) s t")).then_inc(nd_in[r], 16)

            for j in range(4):
                load_stack(0, j)
            for n in range(1, 4):
                store_q(n)
            move_max(0, 0)
            sp.wait_ge(S["q_out"], 48 * 4)

            def load_w(c, r, first=False):
                if not first:
                    sp.wait_ge(S["whi_done"], c - 1)
                    sp.wait_ge(S["wlo_done"], c - 1)
                sp.dma_start(WST[r], wpack[ds(c, 1), :, :].rearrange("c p n -> (c p) n")).then_inc(w_in[r], 16)

            def sp_unit(i, j, first, last):
                b = 2 * i + j // 2
                if not (last and j == 3):
                    move_max(i + (j + 1) // 4, (j + 1) % 4)
                if j % 2 == 0 and not (first and j == 0):
                    store_o(b - 1, (j // 2 + 1) % 2)
                if not last:
                    load_stack(i + 1, j)
                if j % 2 == (0 if last else 1) and not (first and j == 1):
                    load_nd(b - 1, (j // 2 + 1) % 2)

            for j in range(4):
                sp_unit(0, j, True, False)
            with sp.Fori(1, B // 2 - 1) as i:
                for j in range(4):
                    sp_unit(i, j, False, False)
            load_w(0, 0, True)
            load_w(1, 1, True)
            for j in range(4):
                sp_unit(B // 2 - 1, j, False, True)
            store_o(B - 1, 1)
            load_nd(B - 1, 1)

            for c in range(2, 4):
                load_w(c, c % 2)
            with sp.Fori(1, NCH // 4) as i:
                for r in range(4):
                    load_w(4 * i + r, r % 2)
            load_w(NCH - 1, 0)
            for t in range(2):
                sp.wait_ge(S["y_done"], 4 * t + 4)
                sp.dma_start(out[4 * t:4 * t + 4].rearrange("b p l -> p b l"), X[:, 4 * t:4 * t + 4, :]).then_inc(S["out_done"], 16)
            sp.wait_ge(S["out_done"], 32)

        @block.scalar
        def _(act):
            for dst, src, name in (
                (msk[:, :], mask, "msk_in"),
                (ident[:, :], ident_d, "consts_in"), (heads[:, :], heads_d, "consts_in"),
                (skipc[:, :], skip.rearrange("(p a) -> p a", a=1), "consts_in"),
                (gain[:, :], gains.partition_broadcast(128), "consts_in"),
                (kw, kern.rearrange("(k p) f -> p k f", p=128), "kern_in"),
                (bqb[:, :], biasq.partition_broadcast(128), "kern_in"),
                (C[:, :, :], ctx.rearrange("b p l -> p b l"), "ctx_in"),
                (W3[:, :, :], wqkvT.rearrange("w p n -> p w n"), "attn_in"),
                (bqk_sb[:, :], bqk, "attn_in"), (bv_sb[:, :], bv.partition_broadcast(128), "attn_in"),
                (smt[:, :], maskT, "mask_in"), (MB[:, :, :], mask.partition_broadcast(128), "mask_in"),
                (rt[:, :, :], routerT.rearrange("(k p) e -> p k e", p=128), "router_in"),
                (early[:, :, :], earlier_d.partition_broadcast(128), "router_in"),
            ):
                act.dma_start(dst, src).then_inc(S[name], 16)
            act.wait_ge(S["msk_in"], 16)
            act.activation(mtmp[:, 0, :], msk[:, :], ACT.Copy, scale=-NEG).then_inc(S["aux_done"], 1)
            act.activation(mtmp[:, 1, :], msk[:, :], ACT.Copy, bias=1.0, scale=-1.0).then_inc(S["aux_done"], 1)
            act.wait_ge(S["aux_done"], 2)
            for rows, src in ((AQ[:, 0:2, :], mtmp[:, 0:1, :]), (AK[:, 0:3:2, :], mtmp[:, 1:2, :])):
                act.activation(rows, src.to_broadcast([B, 2, L]), ACT.Copy).then_inc(S["aux_done"], 1)
            act.activation(AQ[:, 4:6, :], mtmp[:, 0:1, :].to_broadcast([B, 2, L]), ACT.Copy, scale=0.0).then_inc(S["aux_done"], 1)
            act.activation(AK[:, 4:6, :], mtmp[:, 0:1, :].to_broadcast([B, 2, L]), ACT.Copy, bias=1.0, scale=0.0).then_inc(S["aux_done"], 1)
            act.wait_ge(S["consts_in"], 64)
            act.activation(tg[:, :], gain[:, :], ACT.Tanh).then_inc(S["tanh_done"], 1)
            for n in range(4):
                act.wait_ge(S["vt_ps"], n + 1)
                act.activation(VF[:, n * 512:(n + 1) * 512], PS[:, 4 + n, :], ACT.Copy).then_inc(S["vt_done"], 1)
            act.wait_ge(S["sk_ps"], 1)
            act.activation(skb[:, :], PS[:, 2, 0:L], ACT.Copy).then_inc(S["skb_done"], 1)

            def take_v(n):
                act.wait_ge(S["vp_ps"], n + 1)
                act.activation(VF[:, n * 512:(n + 1) * 512], PS[:, 4 + n, :], ACT.Copy).then_inc(S["v_t"], 1)

            def high(n, src, ready, done):
                act.wait_ge(S[ready], n + 1)
                act.activation(row(HI[:, :, :])[:, n * 512:(n + 1) * 512], src[:, n * 512:(n + 1) * 512], ACT.Copy).then_inc(S[done], 1)

            def round_in(t):
                act.wait_ge(S["xs_done"], t + 1)
                for b in range(4 * t, 4 * t + 4):
                    act.activation(CG[:, b, :], XN[:, b, :], ACT.Identity, bias=rnd[:, 0:1], scale=small[:, 8, b:b + 1]).then_inc(S["xr_done"], 1)

            def turn_in(t):
                b = slice(4 * t, 4 * t + 4)
                act.wait_ge(S["xq_t"], t + 1)
                act.activation(qb[:, b, :], CG[:, b, :], ACT.Copy, bias=-ROUND).then_inc(S["xq_done"], 1)
                act.wait_ge(S["qT_ps"], t + 1)
                act.activation(qbT[:, :, b, :], PS[:, t, :].bitcast(bf16).rearrange("p (k b t) -> p k b t", k=2, b=4),
                               ACT.Copy).then_inc(S["qT_done"], 1)

            def round_out(t):
                act.wait_ge(S["ys_done"], t + 1)
                for b in range(4 * t, 4 * t + 4):
                    act.activation(CG[:, b, :], CG[:, b, :], ACT.Identity, bias=rnd[:, 0:1], scale=small[:, 12, b:b + 1]).then_inc(S["yr_done"], 1)

            act.wait_ge(S["const_set"], 2)
            act.wait_ge(S["aux_out"], 32)
            high(0, KF, "k_done", "k_hi")
            high(1, KF, "k_done", "k_hi")
            take_v(0)
            take_v(1)
            round_in(0)
            take_v(2)
            take_v(3)
            turn_in(0)
            round_in(1)
            high(2, KF, "k_done", "k_hi")
            turn_in(1)
            round_out(0)
            high(3, KF, "k_done", "k_hi")
            round_out(1)
            act.wait_ge(S["k_out"], 32)
            for n in range(4):
                high(n, QF, "q_done", "q_hi")

            def exps(i, j, q):
                u = 4 * i + j
                for g in range(4):
                    act.wait_ge(S["e_ps"], 8 * u + 4 * q + g + 1)
                    if g == 0:
                        need(act, "pv_done", 2 * u + q - 1)
                    act.activation(EXPS[q][:, 512 * g:512 * g + 512], PS[:, 4 + g % 2, :], ACT.Exp).then_inc(S["p_done"], 1)

            def evac_o(i, j, q):
                u, grp = 4 * i + j, 2 * (j % 2) + q
                act.wait_ge(S["pv_done"], 2 * u + q + 1)
                if grp == 0:
                    need(act, "o_out", 64 * (2 * i + j // 2 - 1))
                act.activation(osb[:, j // 2, grp, :], PS[:, 6 + q, 0:L], ACT.Copy).then_inc(S["o_sb"], 1)

            def act_unit(i, j, first, before_last=lambda: None):
                exps(i, j, 0)
                if not (first and j == 0):
                    evac_o(i + (j - 1) // 4, (j - 1) % 4, 1)
                exps(i, j, 1)
                before_last()
                evac_o(i, j, 0)

            for j in range(4):
                act_unit(0, j, True)
            with act.Fori(1, B // 2 - 1) as i:
                for j in range(4):
                    act_unit(i, j, False)

            def router_exp(t):
                b = slice(4 * t, 4 * t + 4)
                act.wait_ge(S["l_done"], 2 * t + 2)
                act.activation(EX[:, b, :], EX[:, b, :], ACT.Exp).then_inc(S["l_exp"], 1)
                act.activation(CB[:, b, NE:NE + 1], LG[:, b, NE:NE + 1], ACT.Exp, scale=-1.0).then_inc(S["l_exp"], 1)

            def split_w(i, r):
                act.wait_ge(w_in[r % 2], 16 * (2 * i + r // 2) + 16)
                if isinstance(i, int) and i == 0:
                    act.wait_ge(S["e_ps"], 8 * NU)
                    act.wait_ge(S["whi_done"], 2)
                else:
                    act.wait_ge(S["down_done"], 8 * i + r - 3)
                act.activation(WHI[r], WST[r % 2], ACT.Copy).then_inc(S["whi_done"], 1)

            def act_silu(i, m):
                n = 8 * i + m
                act.wait_ge(S["guc_g"], n + 1)
                need(act, "t_done", n - 1)
                act.activation(SIL[m % 2], PS[:, 4 + (3 * m) % 4, :], ACT.Silu).then_inc(S["sil_done"], 1)

            def act_hi(i, m):
                n = 8 * i + m
                act.wait_ge(S["h_done"], n + 1)
                need(act, "down_done", n - 1)
                act.activation(HHI[m % 2], HH[m % 2], ACT.Copy).then_inc(S["hhi_done"], 1)

            def act_chunks(i, first=False, last=False):
                for m in range(8):
                    if m < 2:
                        split_w(i, m + 2)
                    elif m == 6 or (m == 7 and not last):
                        split_w(i + 1, m - 6)
                    if first and m == 4:
                        router_exp(1)
                    act_silu(i, m)
                    act_hi(i, m)

            for j in range(4):
                act_unit(B // 2 - 1, j, False, before_last=lambda: router_exp(0) if j == 3 else None)
            evac_o(B // 2 - 1, 3, 1)
            act_chunks(0, first=True)
            with act.Fori(1, NCH // 4 - 1) as i:
                act_chunks(i)
            act_chunks(NCH // 4 - 1, last=True)
            for m in range(2):
                act_silu(NCH // 4, m)
                act_hi(NCH // 4, m)

        @block.gpsimd
        def _(pool):
            def power(k, b=slice(0, B)):
                pool.wait_ge(S["var_done"], k)
                pool.tensor_tensor(rstd[:, b], ve[:, b], mhalf[:, b], ALU.pow).then_inc(S["rstd_done"], 1)

            after(pool, pool.memset(mhalf[:, :], -0.5), "const_set", 1)
            after(pool, pool.memset(rnd[:, :], ROUND), "const_set", 2)
            for t in QS + KS[:1]:
                pool.memset(row(t[:, :, :]).bitcast(f32), 0.0).then_inc(S["zeroed"], 1)
            power(1)
            pool.wait_ge(S["aux_done"], 6)
            for rows, src, high in ((AQ[:, 2:4, :], mtmp[:, 0:1, :], AQ[:, 0:1, :]), (AK[:, 1:4:2, :], mtmp[:, 1:2, :], AK[:, 0:1, :])):
                pool.tensor_tensor(rows, src.to_broadcast([B, 2, L]), high.bitcast(f32).to_broadcast([B, 2, L]), ALU.subtract).then_inc(S["aux_low"], 1)
            pool.wait_ge(S["xn_done"], B)
            pool.wait_ge(S["ctx_in"], 16)
            halved = "p b (k l) -> p b k l"
            pool.tensor_tensor(CG[:, :, :].rearrange(halved, k=2), XN[:, :, :].rearrange(halved, k=2), backwards(C[:, :, :]),
                               ALU.mult).then_inc(S["vc_done"], 1)
            pool.wait_ge(S["cr_in"], 16)
            pool.wait_ge(S["vt_done"], 4)
            vt16 = VT[:, :, :, :].rearrange("p k b t -> p (k b) t")
            cr16 = CR.rearrange("p k b t -> p (k b) t")

            def products(i):
                for j in range(4):
                    h = 4 * i + j
                    need(pool, "y_ps", h - 1)
                    v = vt16[:, :, ds(h * HD0, HD0)].unsqueeze(2).to_broadcast([128, 2 * B, HD0, HD0])
                    c = cr16[:, :, ds(h * HD0, HD0)].unsqueeze(3).to_broadcast([128, 2 * B, HD0, HD0])
                    o = KVP[:, j % 2, :].rearrange("p (n j i) -> p n j i", n=2 * B, j=HD0)
                    pool.tensor_tensor(o, v, c, ALU.mult).then_inc(S["kv_done"], 1)

            products(0)
            with pool.Fori(1, NH0 // 4) as i:
                products(i)

            pool.wait_ge(S["cg_done"], 1)
            pool.tensor_tensor(row(X[:, :, :]), row(X[:, :, :]), QF, ALU.add).then_inc(S["skip_done"], 1)
            for t in KS[1:3]:
                pool.memset(row(t[:, :, :]).bitcast(f32), 0.0).then_inc(S["zeroed"], 1)
            power(2, slice(0, 4))
            pool.wait_ge(S["kv_done"], NH0)
            pool.memset(VA[:, :, :, :].rearrange("p n h (d s) -> p n h d s", s=2)[:, :, :, :, 1], 1.0).then_inc(S["va_ones"], 1)
            power(3, slice(4, 8))

            def low(n, src, ready, done):
                c = slice(n * 512, (n + 1) * 512)
                pool.wait_ge(S[ready], n + 1)
                pool.tensor_tensor(row(LO[:, :, :])[:, c], src[:, c], row(HI[:, :, :])[:, c].bitcast(f32), ALU.subtract).then_inc(S[done], 1)

            def mask_v(n):
                pool.wait_ge(S["v_t"], n + 1)
                v = VF[:, n * 512:(n + 1) * 512]
                vb = v.rearrange("p (n o) -> p n o", n=4)
                after(pool, pool.tensor_tensor(vb, vb, bv_sb[:, :].unsqueeze(1).to_broadcast([128, 4, 128]), ALU.add), "v_b", n + 1)
                m = smt[:, 4 * n:4 * n + 4].unsqueeze(2).unsqueeze(3).to_broadcast([128, 4, NH1, HD1])
                o = VA[:, 4 * n:4 * n + 4, :, :].rearrange("p n h (d s) -> p n h d s", s=2)[:, :, :, :, 0]
                pool.tensor_tensor(o, v.rearrange("p (n h d) -> p n h d", n=4, h=NH1), m, ALU.mult).then_inc(S["v_done"], 1)

            pool.wait_ge(S["attn_in"], 48)
            pool.wait_ge(S["mask_in"], 32)
            pool.wait_ge(S["aux_out"], 32)
            low(0, KF, "k_hi", "k_lo")
            low(1, KF, "k_hi", "k_lo")
            for n in range(3):
                mask_v(n)
            low(2, KF, "k_hi", "k_lo")
            low(3, KF, "k_hi", "k_lo")
            power(4, slice(0, 4))
            pool.wait_ge(S["k_out"], 32)
            low(0, QF, "q_hi", "q_lo")
            power(5, slice(4, 8))
            for n in range(1, 4):
                low(n, QF, "q_hi", "q_lo")
            mask_v(3)
            pool.wait_ge(S["tanh_done"], 1)
            after(pool, pool.tensor_scalar(row(MB[:, :, :]), row(MB[:, :, :]), tg[:, 1:2], None, ALU.mult), "x3_done", 1)
            pool.wait_ge(S["v_done"], 4)

            def copy_v(b, r):
                need(pool, "pv_done", 4 * (b - 1))
                pool.tensor_copy(VR[:, r, :, :, :].rearrange("p k h c -> p (k h c)"),
                                 VA[:, ds(2 * b, 2), :, :].rearrange("p k h c -> p (k h c)")).then_inc(S["vr_done"], 1)

            def add_attention(b, r):
                pool.wait_ge(S["rden_done"], b + 1)
                n = nd[:, r, 0, :]
                after(pool, pool.tensor_tensor(n, n, rden[:, r, :], ALU.mult), "x3_done", 3 * b + 2)
                after(pool, pool.tensor_tensor(n, n, MB[:, ds(b, 1), :].rearrange("p b l -> p (b l)"), ALU.mult), "x3_done", 3 * b + 3)
                xb = X[:, ds(b, 1), :].rearrange("p b l -> p (b l)")
                pool.tensor_tensor(xb, xb, n, ALU.add).then_inc(S["x3_done"], 1)

            copy_v(0, 0)
            copy_v(1, 1)

            def pool_pair(i):
                for r in range(2):
                    copy_v(2 * i + r, r)
                    add_attention(2 * i + r - 2, r)

            def split_low(c, r):
                pool.wait_ge(S["whi_done"], c + 1)
                pool.tensor_tensor(WLO[r], WST[r % 2][:, 0:768], WHI[r][:, 0:768].bitcast(f32), ALU.subtract).then_inc(S["wlo_done"], 1)

            with pool.Fori(1, B // 2 - 1) as i:
                pool_pair(i)
            copy_v(B - 2, 0)
            add_attention(B - 4, 0)
            copy_v(B - 1, 1)
            power(6, slice(0, 4))
            pool.wait_ge(S["e_ps"], 8 * (NU - 2))
            for t in (CBT[0], ZR, CBT[1]):
                pool.memset(t.bitcast(f32), 0.0).then_inc(S["cbt_zero"], 1)
            split_low(0, 0)
            add_attention(B - 3, 1)
            split_low(1, 1)
            add_attention(B - 2, 0)
            add_attention(B - 1, 1)
            split_low(2, 2)
            power(7, slice(4, 8))
            split_low(3, 3)
            with pool.Fori(1, NCH // 4) as i:
                for r in range(4):
                    split_low(4 * i + r, r)
            split_low(NCH - 1, 0)

        @block.vector
        def _(dve):
            st = Steps(dve, "dstep")
            link, tick = st.link, st.tick

            def statistics(bs):
                for b in bs:
                    tick(dve.bn_stats(bst[:, b, :], X[:, b, :]))

            def variance(bs):
                st.sync()
                for b in bs:
                    tick(dve.bn_aggr(mv[:, b, :], bst[:, b, :]))
                st.sync()
                b = slice(bs[0], bs[-1] + 1)
                dve.tensor_scalar(ve[:, b], mv[:, b, 1], EPS, None, ALU.add).then_inc(S["var_done"], 1)

            def normalise(k, bs):
                dve.wait_ge(S["rstd_done"], k)
                for b in bs:
                    xb = X[:, b:b + 1, :]
                    xb, o = (backwards(xb), XN[:, b:b + 1, :].rearrange("p b (k l) -> p b k l", k=2)) if k == 1 else (xb, XN[:, b:b + 1, :])
                    dve.tensor_scalar(o, xb, mv[:, b, 0:1], rstd[:, b:b + 1],
                                      ALU.subtract, ALU.mult).then_inc(S["xn_done"], 1)

            def layer_norm(k):
                statistics(range(B))
                variance(range(B))
                normalise(k, range(B))

            def scale_of(amax, scale, inv, zero, done=None):
                link(dve.tensor_scalar(zero, amax, 0.0, None, ALU.is_equal))
                link(dve.scalar_tensor_tensor(out=scale, in0=amax, scalar=1.0 / QMAX, in1=zero, op0=ALU.mult, op1=ALU.add))
                if done:
                    after(dve, dve.reciprocal(inv, scale), *done)
                else:
                    link(dve.reciprocal(inv, scale))

            dve.memset(row(KS[3][:, :, :]).bitcast(f32), 0.0).then_inc(S["zeroed"], 1)
            link(dve.memset(ones[:, :], 1.0))

            dve.wait_ge(S["x_in"], 16)
            statistics(range(B))
            variance(range(B))
            dve.wait_ge(S["consts_in"], 64)
            dve.tensor_copy(identb[:, :], ident[:, :]).then_inc(S["consts_done"], 1)
            dve.tensor_scalar(heads[:, :], heads[:, :], skipc[:, 0:1], None, ALU.mult).then_inc(S["consts_done"], 1)
            normalise(1, range(B))
            dve.wait_ge(S["kt_ps"], 1)
            link(dve.tensor_reduce(akf[:, :], PS[:, 2, :].rearrange("p (f d) -> p f d", f=2), AX.X, ALU.max, apply_absolute_value=True))
            scale_of(akf[:, :], small[:, 0, 0:2], small[:, 0, 2:4], small[:, 1, 0:2])
            for f in range(4):
                dve.tensor_scalar(diag[:, f, :], ident[:, :], small[:, 0, f:f + 1], None, ALU.mult).then_inc(S["diag_done"], 1)
            halved = "p b (k l) -> p b k l"
            dve.wait_ge(S["sk_ps"], 2)
            link(dve.tensor_tensor(kt2, kw, PS[:, 3, 0:L].unsqueeze(1).to_broadcast([128, 2, L]), ALU.mult))
            link(dve.tensor_scalar(kt2, kt2, ROUND, ROUND - QMAX, ALU.add, ALU.max))
            dve.tensor_scalar(kq[:, :, :], kt2, ROUND + QMAX, ROUND, ALU.min, ALU.subtract).then_inc(S["kq_done"], 1)
            link(dve.tensor_reduce(small[:, 2, 0:1], bqb[:, :], AX.X, ALU.max, apply_absolute_value=True))
            scale_of(small[:, 2, 0:1], small[:, 3, 0:1], small[:, 4, 0:1], small[:, 5, 0:1])
            link(dve.tensor_scalar(bqb[:, :], bqb[:, :], small[:, 4, 0:1], ROUND, ALU.mult, ALU.add))
            link(dve.tensor_scalar(bqb[:, :], bqb[:, :], ROUND - QMAX, ROUND + QMAX, ALU.max, ALU.min))
            link(dve.tensor_scalar(bqb[:, :], bqb[:, :], ROUND, small[:, 3, 0:1], ALU.subtract, ALU.mult))
            dve.wait_ge(S["g_ps"], 4)
            dve.wait_ge(S["tanh_done"], 1)
            dve.scalar_tensor_tensor(out=CG[:, :, :].rearrange(halved, k=2), in0=backwards(banks(4, 4).rearrange("p (b l) -> p b l", b=B)),
                                     scalar=tg[:, 0:1], in1=C[:, :, :].rearrange(halved, k=2), op0=ALU.mult, op1=ALU.mult).then_inc(S["cg_done"], 1)
            dve.wait_ge(S["ct_in"], 16)
            ct16 = CT[:, :, :, :].rearrange("p k b t -> p (k b) t")
            ot16 = OT[:, :, :, :].rearrange("p k b t -> p (k b) t")

            def gate_rows(i):
                for j in range(4):
                    h, r = 4 * i + j, j % 2
                    dve.wait_ge(S["y_ps"], h + 1)
                    need(dve, "ot_part", h - 1)
                    c = ct16[:, :, ds(h * HD0, HD0)].unsqueeze(2).to_broadcast([128, 2 * B, HD0, HD0])
                    y = banks(2 * r, 2).rearrange("p (n j i) -> p n j i", n=2 * B, j=HD0)
                    yx = KVP[:, 2 + r, :].rearrange("p (n j i) -> p n j i", n=2 * B, j=HD0)
                    after(dve, dve.tensor_tensor(yx, y, c, ALU.mult), "yx_done", h + 1)
                    dve.tensor_reduce(ot16[:, :, ds(h * HD0, HD0)], yx, AX.X, ALU.add).then_inc(S["ot_part"], 1)

            gate_rows(0)
            dve.wait_ge(S["attn_in"], 48)
            link(dve.tensor_scalar(W3[:, 0, :], W3[:, 0, :], HD1 ** -0.5, None, ALU.mult))
            dve.tensor_scalar(bqk_sb[:, 0:1], bqk_sb[:, 0:1], HD1 ** -0.5, None, ALU.mult).then_inc(S["wq_done"], 1)
            with dve.Fori(1, NH0 // 4) as i:
                gate_rows(i)

            def add_mixer(n):
                c = slice(n * 512, (n + 1) * 512)
                dve.wait_ge(S["ot_ps"], n + 1)
                dve.scalar_tensor_tensor(out=row(X[:, :, :])[:, c], in0=PS[:, 4 + n, :], scalar=tg[:, 0:1],
                                         in1=row(X[:, :, :])[:, c], op0=ALU.mult, op1=ALU.add).then_inc(S["x1_done"], 1)

            def take_k(n):
                c = slice(n * 512, (n + 1) * 512)
                dve.wait_ge(S["kp_ps"], n + 1)
                dve.scalar_tensor_tensor(out=KF[:, c], in0=PS[:, n, :], scalar=bqk_sb[:, 1:2], in1=row(MB[:, :, :])[:, c],
                                         op0=ALU.add, op1=ALU.mult).then_inc(S["k_done"], 1)

            amax, sx, inv, zero, ymax, sy, yinv, yz = (small[:, n, :] for n in range(6, 14))

            def scale_in(t):
                b = slice(4 * t, 4 * t + 4)
                dve.wait_ge(S["xn_done"], B + 4 * t + 4)
                link(dve.tensor_reduce(amax[:, b], XN[:, b, :], AX.X, ALU.max, apply_absolute_value=True))
                scale_of(amax[:, b], sx[:, b], inv[:, b], zero[:, b], ("xs_done", t + 1))

            def clip_in(t):
                cg = QF[:, 1024 * t:1024 * t + 1024]
                dve.wait_ge(S["xr_done"], 4 * t + 4)
                dve.tensor_scalar(cg, cg, ROUND - QMAX, ROUND + QMAX, ALU.max, ALU.min).then_inc(S["xq_t"], 1)

            def take_out(t):
                for n in range(4 * t, 4 * t + 4):
                    if n % 2 == 0:
                        dve.wait_ge(S["f_ps"], n // 2 + 1)
                    tick(dve.scalar_tensor_tensor(out=CG[:, n, :], in0=PS[:, 4 + n // 2, (n % 2) * L:(n % 2 + 1) * L], scalar=sx[:, n:n + 1],
                                                  in1=skb[:, :], op0=ALU.mult, op1=ALU.mult))

            def bias_out(t):
                b = slice(4 * t, 4 * t + 4)
                st.sync()
                link(dve.tensor_tensor(CG[:, b, :], CG[:, b, :], bqb[:, :].unsqueeze(1).to_broadcast([128, 4, L]), ALU.add))

            def scale_out(t):
                b = slice(4 * t, 4 * t + 4)
                link(dve.tensor_reduce(ymax[:, b], CG[:, b, :], AX.X, ALU.max))
                link(dve.tensor_scalar(ymax[:, b], ymax[:, b], 0.0, None, ALU.max))
                scale_of(ymax[:, b], sy[:, b], yinv[:, b], yz[:, b], ("ys_done", t + 1))
                link(dve.tensor_scalar(sy[:, b], sy[:, b], tg[:, 2:3], None, ALU.mult))

            def add_mlp(t):
                cg = QF[:, 1024 * t:1024 * t + 1024]
                dve.wait_ge(S["yr_done"], 4 * t + 4)
                link(dve.tensor_scalar(cg, cg, ROUND, ROUND + QMAX, ALU.max, ALU.min))
                for b in range(4 * t, 4 * t + 4):
                    tick(dve.tensor_scalar(CG[:, b, :], CG[:, b, :], ROUND, sy[:, b:b + 1], ALU.subtract, ALU.mult))
                st.sync()
                x = row(X[:, :, :])[:, 1024 * t:1024 * t + 1024]
                after(dve, dve.tensor_tensor(x, x, cg, ALU.add), "x2_done", t + 1)

            def take_q(n):
                c = slice(n * 512, (n + 1) * 512)
                dve.wait_ge(S["q_ps"], n + 1)
                dve.scalar_tensor_tensor(out=QF[:, c], in0=PS[:, n, :], scalar=bqk_sb[:, 0:1], in1=row(MB[:, :, :])[:, c],
                                         op0=ALU.add, op1=ALU.mult).then_inc(S["q_done"], 1)

            half_a, half_b = range(0, 4), range(4, 8)
            dve.wait_ge(S["skip_done"], 1)
            add_mixer(0)
            add_mixer(1)
            dve.wait_ge(S["x1_done"], 2)
            statistics(half_a)
            variance(half_a)
            add_mixer(2)
            add_mixer(3)
            dve.wait_ge(S["mask_in"], 32)
            take_k(0)
            take_k(1)
            normalise(2, half_a)
            scale_in(0)
            dve.wait_ge(S["x1_done"], 4)
            statistics(half_b)
            variance(half_b)
            clip_in(0)
            take_k(2)
            normalise(3, half_b)
            scale_in(1)
            take_k(3)
            take_out(0)
            clip_in(1)
            bias_out(0)
            scale_out(0)
            take_out(1)
            add_mlp(0)
            statistics(half_a)
            variance(half_a)
            bias_out(1)
            normalise(4, half_a)
            scale_out(1)
            take_q(0)
            add_mlp(1)
            statistics(half_b)
            variance(half_b)
            take_q(1)
            normalise(5, half_b)
            take_q(2)
            take_q(3)

            def maximum(i, j, k):
                u = 4 * i + j
                dve.wait_ge(S["s_ps"], 4 * u + k + 1)
                if k == 0:
                    need(dve, "turned", u - 1)
                half, hb = k // 2, 4 * (k % 2)
                dve.tensor_reduce(negm[:, j % 2, hb:hb + 4, half], banks(tile_bank(j, k), 2).rearrange("p (h s) -> p h s", h=4),
                                  AX.X, ALU.max, negate=True).then_inc(S["s_used"], 1)

            def split_max(i, j):
                u = 4 * i + j
                dve.wait_ge(S["turned"], u + 1)
                if not (isinstance(i, int) and i == 0 and j < 2):
                    dve.wait_ge(m_in[(j + 2) % 4], 32 * (i + j // 2))
                src = PS[0:16, turn_bank(j), 0:128]
                after(dve, dve.tensor_copy(mT[:, j % 2, 0, :], src), "mt_done", 2 * u + 1)
                dve.tensor_tensor(mT[:, j % 2, 1, :], src, mT[:, j % 2, 0, :].bitcast(f32), ALU.subtract).then_inc(S["mt_done"], 1)

            def reciprocal_of(i, r):
                dve.wait_ge(nd_in[r], 16 * i + 16)
                dve.reciprocal(rden[:, r, :], nd[:, r, 1, :]).then_inc(S["rden_done"], 1)

            dve.wait_ge(S["q_done"], 4)
            for k in range(4):
                maximum(0, 0, k)
            maximum(0, 1, 0)
            split_max(0, 0)
            for k in range(1, 4):
                maximum(0, 1, k)

            early_b, late_b = range(0, 4), range(4, 8)

            def dve_unit(i, j, first, last):
                def max_ahead(k):
                    if not (last and j >= 2):
                        maximum(i + (j + 2) // 4, (j + 2) % 4, k)

                max_ahead(0)
                if not (last and j == 3):
                    split_max(i + (j + 1) // 4, (j + 1) % 4)
                if last and j == 2:
                    for r in range(2):
                        dve.wait_ge(w_in[r], 16)
                        dve.wait_ge(S["e_ps"], 8 * (NU - 3 + r))
                        dve.tensor_copy(WHI[r], WST[r]).then_inc(S["whi_done"], 1)
                max_ahead(1)
                max_ahead(2)
                if j % 2 == 0 and not first:
                    reciprocal_of(i - 1, j // 2)
                if last and j == 1:
                    dve.wait_ge(S["x3_done"], 3 * 4 + 1)
                    statistics(early_b)
                    variance(early_b)
                max_ahead(3)

            for j in range(4):
                dve_unit(0, j, True, False)
            with dve.Fori(1, B // 2 - 1) as i:
                for j in range(4):
                    dve_unit(i, j, False, False)
            for j in range(4):
                dve_unit(B // 2 - 1, j, False, True)

            def split_x(t):
                cols = slice(t * 512, (t + 1) * 512)
                dve.wait_ge(S["xt_ps"], t + 1)
                xt = VF.rearrange("p (k t) -> p k t", k=2)[:, :, cols]
                after(dve, dve.tensor_copy(xt, banks(2, 2).rearrange("p (k t) -> p k t", k=2)), "xt_done", t + 1)
                after(dve, dve.tensor_copy(XTH[:, :, cols], xt), "xth_done", t + 1)
                dve.tensor_tensor(XTL[:, :, cols], xt, XTH[:, :, cols].bitcast(f32), ALU.subtract).then_inc(S["xtl_done"], 1)

            def route(t):
                b = slice(4 * t, 4 * t + 4)
                n = B // 2
                dve.wait_ge(S["l_ps"], t + 1)
                link(dve.tensor_copy(LG[:, b, :], PS[:, 2, 0:n * (NE + 1)].rearrange("p (b e) -> p b e", b=n)))
                lg = LG[:, b, 0:NE]
                after(dve, dve.tensor_reduce(small[:, 14, b], lg, AX.X, ALU.max), "l_done", 2 * t + 1)
                after(dve, dve.tensor_tensor(EX[:, b, :], lg, small[:, 14, b].unsqueeze(2).to_broadcast([128, n, NE]), ALU.subtract), "l_done", 2 * t + 2)
                lj = lg.unsqueeze(2).to_broadcast([128, n, NE, NE])
                li = lg.unsqueeze(3).to_broadcast([128, n, NE, NE])
                tick(dve.tensor_tensor(R1, lj, li, ALU.is_gt))
                link(dve.tensor_tensor(R2, lj, li, ALU.is_equal))
                r1, r2 = (t.rearrange("p b i j -> p b (i j)") for t in (R1, R2))
                link(dve.tensor_tensor(r2, r2, early[:, :, :].rearrange("p i j -> p (i j)").unsqueeze(1).to_broadcast([128, n, NE * NE]), ALU.mult))
                link(dve.tensor_tensor(r1, r1, r2, ALU.add))
                link(dve.tensor_reduce(rank[:, b, :], R1, AX.X, ALU.add))

            def expert_weights(t):
                b = slice(4 * t, 4 * t + 4)
                dve.wait_ge(S["l_exp"], 2 * t + 2)
                tick(dve.tensor_scalar(CB[:, b, NE:NE + 1], CB[:, b, NE:NE + 1], 1.0, None, ALU.add))
                link(dve.scalar_tensor_tensor(out=EX[:, b, :], in0=rank[:, b, :], scalar=1.5, in1=EX[:, b, :], op0=ALU.is_lt, op1=ALU.mult))
                tick(dve.reciprocal(CB[:, b, NE:NE + 1], CB[:, b, NE:NE + 1]))
                link(dve.tensor_reduce(small[:, 14, b], EX[:, b, :], AX.X, ALU.add))
                link(dve.reciprocal(small[:, 15, b], small[:, 14, b]))
                dve.tensor_tensor(CB[:, b, 0:NE], EX[:, b, :], small[:, 15, b].unsqueeze(2).to_broadcast([128, B // 2, NE]), ALU.mult).then_inc(S["cb_done"], 1)

            def split_weights(t):
                dve.wait_ge(S["cbt_ps"], t + 1)
                high, low = CBT[t][0:NE + 1, :], CBT[t][32:32 + NE + 1, :]
                after(dve, dve.tensor_copy(high, PS[0:NE + 1, 3, :]), "cbt_done", 2 * t + 1)
                dve.tensor_tensor(low, PS[0:NE + 1, 3, :], high.bitcast(f32), ALU.subtract).then_inc(S["cbt_done"], 1)

            def gate_hidden(i, m):
                n = 8 * i + m
                dve.wait_ge(S["sil_done"], n + 1)
                dve.wait_ge(S["guc_u"], n + 1)
                after(dve, dve.tensor_tensor(TU[m % 2], SIL[m % 2], PS[:, 4 + (3 * m + 1) % 4, :], ALU.mult), "t_done", n + 1)
                dve.wait_ge(S["guc_c"], n + 1)
                need(dve, "hlo_done", n - 1)
                dve.tensor_tensor(HH[m % 2], TU[m % 2], PS[:, 4 + (3 * m + 2) % 4, :], ALU.mult).then_inc(S["h_done"], 1)
                dve.wait_ge(S["hhi_done"], n + 1)
                need(dve, "down_done", n - 1)
                dve.tensor_tensor(HLO[m % 2], HH[m % 2], HHI[m % 2].bitcast(f32), ALU.subtract).then_inc(S["hlo_done"], 1)

            normalise(6, early_b)
            dve.wait_ge(S["q_out"], 48)
            split_x(0)
            reciprocal_of(B // 2 - 1, 0)
            dve.wait_ge(S["cbt_zero"], 3)
            dve.wait_ge(S["router_in"], 32)
            route(0)
            expert_weights(0)
            split_weights(0)
            dve.wait_ge(S["x3_done"], 3 * (B - 1) + 1)
            statistics(late_b[:3])
            reciprocal_of(B // 2 - 1, 1)
            dve.wait_ge(S["o_out"], 64 * (B - 1))
            gate_hidden(0, 0)
            dve.wait_ge(S["x3_done"], 3 * B + 1)
            statistics(late_b[3:])
            variance(late_b)
            normalise(7, late_b)
            gate_hidden(0, 1)
            split_x(1)
            gate_hidden(0, 2)
            gate_hidden(0, 3)
            route(1)
            expert_weights(1)
            split_weights(1)
            for m in range(4, 8):
                gate_hidden(0, m)
            with dve.Fori(1, NCH // 4) as i:
                for m in range(8):
                    gate_hidden(i, m)
            for m in range(2):
                gate_hidden(NCH // 4, m)
            for b in range(B):
                dve.wait_ge(S["down_done"], 2 * NCH - 1 + b // 4)
                dve.scalar_tensor_tensor(out=X[:, b, :], in0=PS[:, b // 2, (b % 2) * L:(b % 2 + 1) * L], scalar=tg[:, 3:4],
                                         in1=X[:, b, :], op0=ALU.mult, op1=ALU.add).then_inc(S["y_done"], 1)

        @block.tensor
        def _(pe):
            mm = pe.matmul
            pe.wait_ge(S["consts_in"], 64)
            pe.wait_ge(S["kern_in"], 32)
            for f in range(2):
                for d in range(2):
                    last = pe.transpose(PS[:, 2, f * L + d * 128:f * L + d * 128 + 128], kw[:, d, f * 128:(f + 1) * 128], ident[:, :])
            last.then_inc(S["kt_ps"], 1)
            for n in range(4):
                k = n // 2
                for b in range(4 * (n % 2), 4 * (n % 2) + 4):
                    pe.wait_ge(S["xn_done"], b + 1)
                    last = pe.transpose(PS[:, 4 + n, (b % 4) * 128:(b % 4 + 1) * 128], XN[:, b, k * 128:(k + 1) * 128], ident[:, :])
                last.then_inc(S["vt_ps"], 1)
            pe.wait_ge(S["diag_done"], 4)
            for n in range(2):
                for f in range(2):
                    last = mm(PS[:, 2 + n, f * 128:(f + 1) * 128], ones[:, :], diag[:, 2 * n + f, :], start=True, stop=True)
                last.then_inc(S["sk_ps"], 1)
            pe.wait_ge(S["vt_done"], 4)
            pe.wait_ge(S["vc_done"], 1)
            pe.wait_ge(S["consts_done"], 2)
            for n in range(4):
                mm(PS[:, 4 + n, :], heads[:, :], QF[:, n * 512:(n + 1) * 512], start=True, stop=True).then_inc(S["g_ps"], 1)
            def convolve(i):
                for j in range(4):
                    h, r = 4 * i + j, j % 2
                    pe.wait_ge(T_in[j], 16 * i + 16)
                    pe.wait_ge(S["kv_done"], h + 1)
                    need(pe, "yx_done", h - 1)
                    if isinstance(i, int) and h == 1:
                        pe.wait_ge(S["skb_done"], 1)
                        pe.wait_ge(S["kq_done"], 1)
                    kv = KVP[:, r, :].rearrange("p (k n) -> p k n", k=2)
                    near, far = T[:, j, 0:128], T[:, j, 128:256]
                    mm(PS[:, 2 * r, :], near, kv[:, 0, :], start=True, stop=True)
                    mm(PS[:, 2 * r + 1, :], far, kv[:, 0, :], start=True, stop=False)
                    mm(PS[:, 2 * r + 1, :], near, kv[:, 1, :], start=False, stop=True).then_inc(S["y_ps"], 1)

            convolve(0)
            with pe.Fori(1, NH0 // 4) as i:
                convolve(i)
            pe.wait_ge(S["ot_part"], NH0)
            pe.wait_ge(S["cg_done"], 1)
            for n in range(4):
                for b in (2 * n, 2 * n + 1):
                    for k in range(2):
                        last = pe.transpose(PS[:, 4 + n, (b % 2) * L + k * 128:(b % 2) * L + (k + 1) * 128], OT[:, k, b, :], ident[:, :])
                last.then_inc(S["ot_ps"], 1)
            pe.wait_ge(S["attn_in"], 48)
            pe.wait_ge(S["ctx_in"], 16)
            pe.wait_ge(S["yx_done"], NH0)
            for n in range(4):
                mm(PS[:, n, :], W3[:, 1, :], row(C[:, :, :])[:, n * 512:(n + 1) * 512], start=True, stop=True).then_inc(S["kp_ps"], 1)
            for n in range(4):
                pe.wait_ge(S["x1_done"], n + 1)
                for b in (2 * n, 2 * n + 1):
                    for k in range(2):
                        last = mm(PS[:, 4 + n, (b % 2) * L + k * 128:(b % 2) * L + (k + 1) * 128], C[:, b, k * 128:(k + 1) * 128],
                                  W3[:, 2, :], start=True, stop=True)
                last.then_inc(S["vp_ps"], 1)
            for t in range(2):
                pe.wait_ge(S["xq_done"], t + 1)
                pe.wait_ge(S["k_done"], t + 1)
                qT = PS[:, t, :].bitcast(bf16).rearrange("p (k b t) -> p k b t", k=2, b=4)
                for k in range(2):
                    for b in range(4):
                        last = pe.transpose(qT[:, k, b, :], qb[:, 4 * t + b, k * 128:(k + 1) * 128], identb[:, :])
                last.then_inc(S["qT_ps"], 1)
                pe.wait_ge(S["qT_done"], t + 1)
                pe.wait_ge(S["v_t"], 2 * t + 2)
                for b in range(4 * t, 4 * t + 4):
                    for k in range(2):
                        last = mm(PS[:, 4 + b // 2, (b % 2) * L:(b % 2 + 1) * L], qbT[:, k, b, :], kq[:, k, :], start=(k == 0), stop=(k == 1))
                    if b % 2:
                        last.then_inc(S["f_ps"], 1)
            pe.wait_ge(S["wq_done"], 1)
            pe.wait_ge(S["k_done"], 4)
            for n in range(4):
                pe.wait_ge(S["xn_done"], 2 * B + 2 * n + 2)
                mm(PS[:, n, :], W3[:, 0, :], row(XN[:, :, :])[:, n * 512:(n + 1) * 512], start=True, stop=True).then_inc(S["q_ps"], 1)

            def max_tile(i, j, k):
                u = 4 * i + j
                if k == 0:
                    pe.wait_ge(st_in[j], 80 * i + 80)
                need(pe, *(("s_used", 4 * u - 1), ("s_used", 4 * u + 1), ("mt_done", 2 * u), ("s_used", 4 * u + 2))[k])
                for n in range(4):
                    h, half = 4 * (k % 2) + n, k // 2
                    last = mm(banks(tile_bank(j, k), 2)[:, n * L:(n + 1) * L], QS[j][:, h, half * 128:(half + 1) * 128],
                              KS[j][:, h, :], start=True, stop=True)
                last.then_inc(S["s_ps"], 1)

            def turn_max(i, j):
                u = 4 * i + j
                pe.wait_ge(S["s_used"], 4 * u + 4)
                pe.transpose(PS[0:16, turn_bank(j), 0:128], negm[:, j % 2, :, :].rearrange("p h c -> p (h c)"),
                             ident[:, :]).then_inc(S["turned"], 1)

            def score(i, j, g):
                if g == 0:
                    pe.wait_ge(m_in[j], 32 * i + 32)
                need(pe, "p_done", 8 * (4 * i + j) + g - 1)
                for k in range(2):
                    last = mm(PS[:, 4 + g % 2, k * L:(k + 1) * L], KS[j][:, g, k * 128:(k + 1) * 128],
                              QS[j][:, g, :], start=True, stop=True)
                last.then_inc(S["e_ps"], 1)

            def weigh(i, j, q):
                u = 4 * i + j
                if q == 0 and j % 2 == 0:
                    pe.wait_ge(S["vr_done"], 2 * i + j // 2 + 1)
                pe.wait_ge(S["p_done"], 8 * u + 4 * q + 4)
                need(pe, "o_sb", 2 * u + q - 1)
                for k in range(2):
                    for g in range(4):
                        h = 8 * (j % 2) + 4 * q + g
                        last = mm(PS[32 * g:32 * g + 16, 6 + q, 0:L], VR[:, (j // 2) % 2, k, h, :],
                                  EXPS[q][:, 512 * g + k * L:512 * g + (k + 1) * L], start=(k == 0), stop=(k == 1))
                last.then_inc(S["pv_done"], 1)

            def pe_unit(i, j, first, last, between=None):
                def max_ahead(k):
                    if not (last and j >= 2):
                        max_tile(i + (j + 2) // 4, (j + 2) % 4, k)

                score(i, j, 0)
                score(i, j, 1)
                max_ahead(0)
                score(i, j, 2)
                if not (first and j == 0):
                    weigh(i + (j - 1) // 4, (j - 1) % 4, 1)
                if not (last and j == 3):
                    turn_max(i + (j + 1) // 4, (j + 1) % 4)
                score(i, j, 3)
                max_ahead(1)
                score(i, j, 4)
                score(i, j, 5)
                if between:
                    between()
                max_ahead(2)
                score(i, j, 6)
                weigh(i, j, 0)
                score(i, j, 7)
                max_ahead(3)

            pe.wait_ge(S["q_done"], 4)
            for k in range(4):
                max_tile(0, 0, k)
            max_tile(0, 1, 0)
            turn_max(0, 0)
            for k in range(1, 4):
                max_tile(0, 1, k)
            for j in range(4):
                pe_unit(0, j, True, False)
            with pe.Fori(1, B // 2 - 1) as i:
                for j in range(4):
                    pe_unit(i, j, False, False)
            def turn_x(t):
                for k in range(2):
                    for b in range(4 * t, 4 * t + 4):
                        pe.wait_ge(S["xn_done"], 3 * B + b + 1)
                        last = pe.transpose(PS[:, 2 + k, (b % 4) * 128:(b % 4 + 1) * 128], XN[:, b, k * 128:(k + 1) * 128], ident[:, :])
                last.then_inc(S["xt_ps"], 1)

            def logits(t):
                pe.wait_ge(S["xt_done"], t + 1)
                for b in range(4 * t, 4 * t + 4):
                    for k in range(2):
                        last = mm(PS[:, 2, (b % 4) * (NE + 1):(b % 4 + 1) * (NE + 1)], XT[:, k, b, :], rt[:, k, :], start=(k == 0), stop=(k == 1))
                last.then_inc(S["l_ps"], 1)

            def turn_weights(t):
                pe.wait_ge(S["cb_done"], t + 1)
                for b in range(4 * t, 4 * t + 4):
                    last = pe.transpose(PS[0:NE + 1, 3, (b % 4) * 128:(b % 4 + 1) * 128], CB[:, b, :], ident[:, :])
                last.then_inc(S["cbt_ps"], 1)

            def clear(t):
                for n in range(2 * t, 2 * t + 2):
                    mm(PS[:, n, :], ZR[:, 0:128], ZR, start=True, stop=False, skip_group_check=True)

            def gate_up(i, m, t, before_weights=None):
                n, r = 8 * i + m, m % 4 if t == m // 4 else 0
                cols = slice(512 * t, 512 * t + 512)
                if t == 0:
                    pe.wait_ge(S["whi_done"], 4 * i + r + 1)
                    pe.wait_ge(S["wlo_done"], 4 * i + r + 1)
                for part, ready, count, signal in ((0, "h_done", n - 1, "guc_g"), (1, "sil_done", n, "guc_u")):
                    need(pe, ready, count)
                    o = PS[:, 4 + (3 * m + part) % 4, :]
                    for k in range(2):
                        c = slice(256 * part + 128 * k, 256 * part + 128 * k + 128)
                        mm(o, WHI[r][:, c], XTH[:, k, cols], start=(k == 0), stop=False)
                        mm(o, WHI[r][:, c], XTL[:, k, cols], start=False, stop=False)
                        last = mm(o, WLO[r][:, c], XTH[:, k, cols], start=False, stop=(k == 1))
                    last.then_inc(S[signal], 1)
                if before_weights:
                    before_weights()
                need(pe, "t_done", n)
                mm(PS[:, 4 + (3 * m + 2) % 4, :], WHI[r][:, 768:896], CBT[t], start=True, stop=True).then_inc(S["guc_c"], 1)

            def down(i, m, t):
                n, r = 8 * i + m, m % 4 if t == m // 4 else 0
                pe.wait_ge(S["hhi_done"], n + 1)
                pe.wait_ge(S["hlo_done"], n + 1)
                for b in range(4):
                    o = PS[:, 2 * t + b // 2, (b % 2) * L:(b % 2 + 1) * L]
                    c = slice(128 * b, 128 * b + 128)
                    mm(o, HHI[m % 2][:, c], WHI[r][:, 512:768], start=False, stop=False, skip_group_check=True)
                    mm(o, HHI[m % 2][:, c], WLO[r][:, 512:768], start=False, stop=False, skip_group_check=True)
                    last = mm(o, HLO[m % 2][:, c], WHI[r][:, 512:768], start=False, stop=False, skip_group_check=True)
                last.then_inc(S["down_done"], 1)

            def pe_chunks(i):
                for m in range(8):
                    gate_up(i + (m + 1) // 8, (m + 1) % 8, (m + 1) % 8 // 4)
                    down(i, m, m // 4)

            def weights_of_second():
                turn_weights(1)
                pe.wait_ge(S["cbt_done"], 4)
                clear(1)

            for j in range(3):
                pe_unit(B // 2 - 1, j, False, True)
            pe.wait_ge(S["mt_done"], 2 * NU)
            turn_x(0)
            pe.wait_ge(S["router_in"], 32)
            pe_unit(B // 2 - 1, 3, False, True, lambda: logits(0))
            weigh(B // 2 - 1, 3, 1)
            turn_weights(0)
            pe.wait_ge(S["cbt_zero"], 3)
            clear(0)
            pe.wait_ge(S["xtl_done"], 1)
            pe.wait_ge(S["o_sb"], 2 * NU)
            pe.wait_ge(S["cbt_done"], 2)
            gate_up(0, 0, 0)
            gate_up(0, 1, 0)
            down(0, 0, 0)
            gate_up(0, 2, 0)
            turn_x(1)
            down(0, 1, 0)
            gate_up(0, 3, 0)
            logits(1)
            down(0, 2, 0)
            down(0, 3, 0)
            pe.wait_ge(S["xtl_done"], 2)
            gate_up(0, 4, 1, weights_of_second)
            for m in range(4, 8):
                gate_up((m + 1) // 8, (m + 1) % 8, (m + 1) % 8 // 4)
                down(0, m, 1)
            with pe.Fori(1, NCH // 4) as i:
                pe_chunks(i)
            gate_up(NCH // 4, 1, 1)
            down(NCH // 4, 0, 0)
            down(NCH // 4, 1, 1)


def kernel(**inputs):
    import numpy as np
    import concourse.bacc as bacc
    from concourse.bass_utils import run_bass_kernel_spmd

    a = {n: np.asarray(v) for n, v in inputs.items()}
    f = np.float32
    pad = NCH * 128 - NI
    turn = np.arange(128).reshape(NH1, HD1).T.reshape(-1)

    def hidden(experts, shared):
        w = np.concatenate([experts.transpose(1, 0, 2).reshape(L, NE * EI), shared, np.zeros((L, pad), f)], 1)
        return w.reshape(2, 128, NCH, 128).transpose(2, 1, 0, 3).reshape(NCH, 128, 256)

    down = np.concatenate([a["L1_ffn_w_down"].reshape(NE * EI, L), a["L1_ffn_sw_down"], np.zeros((pad, L), f)], 0)
    owner = np.minimum(np.arange(NCH * 128) // EI, NE)
    sel = np.zeros((128, NCH * 128), f)
    for e in range(NE + 1):
        sel[[e, 32 + e]] = owner == e
    wpack = np.concatenate([hidden(a["L1_ffn_w_gate"], a["L1_ffn_sw_gate"]), hidden(a["L1_ffn_w_up"], a["L1_ffn_sw_up"]),
                            down.reshape(NCH, 128, L), sel.reshape(128, NCH, 128).transpose(1, 0, 2)], 2)
    mask = a["mask_Bx1x2048_fk1"].reshape(B, L)
    ctxT = a["ctx_2048"].transpose(2, 0, 1)
    arrays = {
        "x": a["x"], "ctx": a["ctx_2048"], "ctxT": np.stack([ctxT, ctxT.reshape(2, 128, B, TOK)[:, ::-1].reshape(L, B, TOK)]),
        "mask": mask, "maskT": mask.reshape(B, 2, 128).transpose(2, 0, 1).reshape(128, 2 * B),
        "kpad": np.concatenate([np.zeros((NH0, L), f), a["L0_xattn_k"]], 1),
        "skip": a["fside_S2_0"], "gains": np.concatenate([a["g_xattn"], a["g_ffn"]]),
        "kern": a["L0_ffn_kernel"], "biasq": a["L0_ffn_bias"],
        "wqkvT": np.stack([a["L1_xattn_Wq"][turn].T, a["L1_xattn_Wk"][turn].T, a["L1_xattn_Wv"].T]),
        "bqk": np.stack([a["L1_xattn_bq"][turn], a["L1_xattn_bk"][turn]], 1), "bv": a["L1_xattn_bv"],
        "routerT": np.concatenate([a["L1_ffn_gate_w"].T, a["L1_ffn_shared_gate_w"]], 1),
        "wpack": wpack, "ident_d": np.eye(128, dtype=f),
        "heads_d": np.kron(np.eye(NH0, dtype=f), np.ones((HD0, HD0), f)),
        "earlier_d": np.tril(np.ones((NE, NE), f), -1),
    }
    arrays = {n + "_in": np.ascontiguousarray(v) for n, v in arrays.items()}
    nc = bacc.Bacc("TRN2", target_bir_lowering=False, num_devices=1)
    args = [nc.dram_tensor(n, v.shape, mybir.dt.from_np(v.dtype), kind="ExternalInput").ap() for n, v in arrays.items()]
    out = nc.dram_tensor("out", (B, TOK, L), mybir.dt.float32, kind="ExternalOutput").ap()
    flamingo_program(nc, *args, out)
    r = run_bass_kernel_spmd(nc, [arrays], core_ids=[0])
    return r.results[0]["out"]
```

```python
import concourse.bass as bass
from concourse import mybir
from contextlib import ExitStack

B, TOK, L = 8, 128, 256
NH0, HD0 = 16, 8
NH1, HD1 = 16, 8
NE, EI, SI = 8, 176, 704
NI = NE * EI + SI
NCH = -(-NI // 128)
WCOLS = 2 * 128 + 2 * 128 + L + 128
NEG = 1000000.0
QMAX = 127.0
ROUND = 12582912.0
EPS = 1e-05
NU = 2 * B
HU = NH1 // 2


def flamingo_program(nc, x, ctx, ctxT, mask, maskT, kpad, skip, gains, kern, biasq, wqkvT, bqk, bv,
                     routerT, wpack, ident_d, heads_d, earlier_d, out):
    f32, f32r, bf16 = mybir.dt.float32, mybir.dt.float32r, mybir.dt.bfloat16
    ALU, ACT, AX = mybir.AluOpType, mybir.ActivationFunctionType, mybir.AxisListType
    ds = bass.ds
    stack = ExitStack()
    with stack:
        def sb(name, shape, dt=f32):
            return stack.enter_context(nc.sbuf_tensor(name, shape, dt))

        def sem(name):
            return stack.enter_context(nc.semaphore(name))

        X = sb("X", [128, B, L])
        C = sb("C", [128, B, L])
        XN = sb("XN", [128, B, L])
        CT = sb("CT", [128, 2, B, TOK])
        VT = sb("VT", [128, 2, B, TOK])
        OT = sb("OT", [128, 2, B, TOK])
        CG = sb("CG", [128, B, L])
        T = sb("T", [128, 4, L])
        KVP = sb("KVP", [128, 4, 1024])
        ident = sb("ident", [128, 128])
        identb = sb("identb", [128, 128], bf16)
        ones = sb("ones", [128, 128])
        heads = sb("heads", [128, 128])
        skipc = sb("skipc", [128, 1])
        gain = sb("gain", [128, 4])
        tg = sb("tg", [128, 4])
        mhalf = sb("mhalf", [128, B])
        rnd = sb("rnd", [128, 1])
        bst = sb("bst", [128, B, 6])
        mv = sb("mv", [128, B, 2])
        ve = sb("ve", [128, B])
        rstd = sb("rstd", [128, B])
        kq = sb("kq", [128, 2, L], bf16)
        akf = sb("akf", [128, 2])
        skb = sb("skb", [128, L])
        bqb = sb("bqb", [128, L])
        small = sb("small", [128, 16, B])
        W3 = sb("W3", [128, 3, 128])
        bqk_sb = sb("bqk_sb", [128, 2])
        bv_sb = sb("bv_sb", [128, 128])
        smt = sb("smt", [128, 2 * B])
        MB = sb("MB", [128, B, L])
        msk = sb("msk", [B, L])
        HI = sb("HI", [128, B, L], f32r)
        LO = sb("LO", [128, B, L], f32r)
        VA = sb("VA", [128, 2 * B, NH1, 16])
        VR = sb("VR", [128, 2, 2, NH1, 16])
        QS = [sb(f"QS{j}", [128, HU, L], f32r) for j in range(4)]
        KS = [sb(f"KS{j}", [128, HU, L], f32r) for j in range(4)]
        negm = sb("negm", [128, 2, HU, 2])
        mT = sb("mT", [16, 2, 2, 128], f32r)
        osb = sb("osb", [128, 2, 4, L])
        rden = sb("rden", [128, 2, L])
        def row(t):
            return t.rearrange("p h l -> p (h l)")

        kw, kt2 = osb[:, 0, 0:2, :], osb[:, 0, 2:4, :]
        diag = osb[:, 1, 0:2, :].rearrange("p a (f c) -> p (a f) c", f=2)
        mtmp = osb[0:B, 1, 2:4, :]
        nd = T[:, :, :].rearrange("p (r s) l -> p r s l", r=2)
        qb = T[:, :, :].rearrange("p j l -> p (j l)").bitcast(bf16).rearrange("p (b l) -> p b l", b=B)
        qbT = VR[:, :, :, :, :].rearrange("p r k h c -> p (r k h c)").bitcast(bf16).rearrange("p (k b t) -> p k b t", k=2, b=B)

        def token_group(t, n):
            return t[:, :, 4 * n:4 * n + 4, :]

        CR = VA[:, 0:B, :, :].rearrange("p b h c -> p (b h c)").rearrange("p (k b t) -> p k b t", k=2, b=B)
        KF = OT[:, :, :, :].rearrange("p k b t -> p (k b t)")
        VF = VT[:, :, :, :].rearrange("p k b t -> p (k b t)")
        QF = row(CG[:, :, :])
        AQ = row(HI[0:B, 0:6, :]).rearrange("p (r l) -> p r l", r=6)
        AK = row(LO[0:B, 0:6, :]).rearrange("p (r l) -> p r l", r=6)
        EXPS = [KVP[:, 2 * r:2 * r + 2, :].rearrange("p a n -> p (a n)") for r in range(2)]
        XT = VT
        XTH = row(HI[:, :, :]).rearrange("p (k b t) -> p k b t", k=2, b=B)
        XTL = row(LO[:, :, :]).rearrange("p (k b t) -> p k b t", k=2, b=B)
        WST = [row(C[:, :, :])[:, r * 1024:r * 1024 + WCOLS] for r in range(2)]
        SIL = [KVP[:, 2, r * 512:(r + 1) * 512] for r in range(2)]
        TU = [KVP[:, 3, r * 512:(r + 1) * 512] for r in range(2)]
        HH = [osb[:, 0, 2 * r:2 * r + 2, :].rearrange("p a l -> p (a l)") for r in range(2)]
        WHI = [row(QS[r][:, :, :])[:, 0:WCOLS] for r in range(4)]
        WLO = [row(KS[r][:, :, :])[:, 0:768] for r in range(4)]
        HHI = [row(QS[r][:, :, :])[:, 1024:1536] for r in range(2)]
        HLO = [row(KS[r][:, :, :])[:, 1024:1536] for r in range(2)]
        CBT = [row(QS[t][:, :, :])[:, 1536:2048] for t in range(2)]
        ZR = row(KS[0][:, :, :])[:, 1536:2048]
        R1, R2 = (QF[:, c:c + 256].rearrange("p (b i j) -> p b i j", b=B // 2, i=NE) for c in (1536, 1792))
        rt = sb("rt", [128, 2, NE + 1])
        LG = sb("LG", [128, B, NE + 1])
        EX = sb("EX", [128, B, NE])
        early = sb("early", [128, NE, NE])
        rank = sb("rank", [128, B, NE])
        CB = sb("CB", [128, B, NE + 1])

        PS = stack.enter_context(nc.psum_tensor("PS", [128, 8, 512], f32))

        def banks(a, n):
            return PS[:, a:a + n, :].rearrange("p a c -> p (a c)")

        def scratch(name, shape):
            return nc.dram_tensor(name, shape, f32, kind="Internal").ap()

        q_dram = scratch("q_dram", [B, 3, 128, L])
        k_dram = scratch("k_dram", [B, 2, 128, L])
        aq_dram = scratch("aq_dram", [B, 6, L])
        ak_dram = scratch("ak_dram", [B, 6, L])
        o_dram = scratch("o_dram", [B, 128, 2, L])

        names = """ctx_in cr_in ct_in consts_in kern_in attn_in msk_in mask_in router_in
            consts_done wq_done tanh_done var_done rstd_done xn_done vt_ps vt_done vc_done g_ps cg_done skip_done
            dstep kt_ps diag_done sk_ps skb_done kq_done kv_done y_ps yx_done ot_part ot_ps x1_done
            kp_ps k_t k_done k_hi k_lo k_out vp_ps v_t v_b v_done va_ones aux_done aux_low aux_out zeroed const_set
            xs_done xr_done xq_t xq_done qT_ps qT_done f_ps ys_done yr_done x2_done q_ps q_done q_hi q_lo q_out
            s_ps s_used mt_done e_ps p_done pv_done o_sb o_out
            vr_done turned rden_done x3_done xt_ps xt_done xth_done xtl_done l_ps l_done l_exp cb_done
            cbt_ps cbt_done cbt_zero whi_done wlo_done
            guc_g guc_u guc_c sil_done t_done h_done hhi_done hlo_done down_half down_done y_done out_done""".split()
        S = {n: sem(n) for n in names}
        x_in = [sem(f"x_in{j}") for j in range(2)]
        T_in = [sem(f"T_in{j}") for j in range(4)]
        st_in = [sem(f"st_in{j}") for j in range(4)]
        m_in = [sem(f"m_in{j}") for j in range(4)]
        w_in = [sem(f"w_in{j}") for j in range(2)]
        nd_in = [sem(f"nd_in{j}") for j in range(2)]

        block = stack.enter_context(nc.Block())

        def need(eng, name, n):
            if not (isinstance(n, int) and n <= 0):
                eng.wait_ge(S[name], n)

        def after(eng, ins, name, n):
            ins.then_inc(S[name], 1)
            eng.wait_ge(S[name], n)

        def tile_bank(j, k):
            return 2 * ((5 * j + (k or -1)) % 2)

        def turn_bank(j):
            return 2 * ((j + 1) % 2)

        def backwards(t):
            return t.rearrange("p b (k l) -> p b k l", k=2)[:, :, :, 127::-1]

        class Steps:

            def __init__(self, eng, name):
                self.eng, self.name, self.n = eng, name, 0

            def tick(self, ins):
                ins.then_inc(S[self.name], 1)
                self.n += 1

            def sync(self):
                self.eng.wait_ge(S[self.name], self.n)

            def link(self, ins):
                self.tick(ins)
                self.sync()

        @block.sync
        def _(sp):
            for t in range(2):
                sp.dma_start(X[:, 4 * t:4 * t + 4, :], x[4 * t:4 * t + 4].rearrange("b p l -> p b l")).then_inc(x_in[t], 16)
            sp.dma_start(CR, ctxT[1].rearrange("(k p) b t -> p k b t", p=128)).then_inc(S["cr_in"], 16)
            shifted = bass.AP(kpad.tensor, L - 127, [[2 * L, NH0], [1, 128], [1, L]])

            def load_T(i):
                for j in range(4):
                    need(sp, "y_ps", 4 * i + j - 3)
                    sp.dma_start(T[:, j, :], shifted[ds(4 * i + j, 1), :, :].rearrange("h p l -> (h p) l")).then_inc(T_in[j], 16)

            load_T(0)
            sp.dma_start(CT[:, :, :, :], ctxT[0].rearrange("(k p) b t -> p k b t", p=128)).then_inc(S["ct_in"], 16)
            for dst, src, name in (
                (W3[:, :, :], wqkvT.rearrange("w p n -> p w n"), "attn_in"),
                (bqk_sb[:, :], bqk, "attn_in"), (bv_sb[:, :], bv.partition_broadcast(128), "attn_in"),
                (smt[:, :], maskT, "mask_in"), (MB[:, :, :], mask.partition_broadcast(128), "mask_in"),
                (rt[:, :, :], routerT.rearrange("(k p) e -> p k e", p=128), "router_in"),
                (early[:, :, :], earlier_d.partition_broadcast(128), "router_in"),
            ):
                sp.dma_start(dst, src).then_inc(S[name], 16)
            sp.wait_ge(S["aux_low"], 2)
            sp.dma_start(aq_dram, AQ.bitcast(f32)).then_inc(S["aux_out"], 16)
            sp.dma_start(ak_dram, AK.bitcast(f32)).then_inc(S["aux_out"], 16)
            with sp.Fori(1, NH0 // 4) as i:
                load_T(i)

            def store_part(dst, part, src, b=slice(0, B)):
                return sp.dma_start(dst[b, part].rearrange("b p t -> p b t"), src[:, b, :].bitcast(f32))

            def store_q(n, m):
                b = slice(2 * n, 2 * m)
                sp.wait_ge(S["q_hi"], m)
                store_part(q_dram, 0, HI, b).then_inc(S["q_out"], 16)
                store_part(q_dram, 2, HI, b).then_inc(S["q_out"], 16)
                sp.wait_ge(S["q_lo"], m)
                store_part(q_dram, 1, LO, b).then_inc(S["q_out"], 16)

            sp.wait_ge(S["k_hi"], 4)
            store_part(k_dram, 0, HI).then_inc(S["k_out"], 16)
            sp.wait_ge(S["k_lo"], 4)
            store_part(k_dram, 1, LO).then_inc(S["k_out"], 16)
            store_q(0, 1)
            sp.wait_ge(S["k_out"], 32)
            sp.wait_ge(S["aux_out"], 32)
            sp.wait_ge(S["zeroed"], 8)
            sp.wait_ge(S["q_out"], 48)

            def stack_rows(src, parts, b, half, n):
                v = bass.AP(src.tensor, half * HU * L, [[128 * L, parts * (B - 1) + n], [NH1 * L, 2 * HD1], [1, HU * L]])
                return v[ds(parts * b, n), :, :]

            def load_stack(i, j):
                b, half = 2 * i + j // 2, j % 2
                need(sp, "e_ps", 8 * (4 * i + j - 3))
                sp.dma_start(QS[j][0:32, :, :].bitcast(f32), stack_rows(q_dram, 3, b, half, 2)).then_inc(st_in[j], 16)
                for r in range(2):
                    sp.dma_start(KS[j][16 * r:16 * r + 16, :, :].bitcast(f32), stack_rows(k_dram, 2, b, half, 1)).then_inc(st_in[j], 16)
                for dst, src in ((QS, aq_dram), (KS, ak_dram)):
                    rows = src[ds(b, 1), :, :].rearrange("b r t -> (b r) t").unsqueeze(1).to_broadcast([6, HU, L])
                    sp.dma_start(dst[j][32:38, :, :].bitcast(f32), rows).then_inc(st_in[j], 16)

            def move_max(i, j):
                sp.wait_ge(S["mt_done"], 2 * (4 * i + j) + 2)
                for s in range(2):
                    sp.dma_start(QS[j][36 + s:37 + s, :, :].bitcast(f32).rearrange("p h (c t) -> p (h c) t", c=2),
                                 mT[:, j % 2, s, :].bitcast(f32)).then_inc(m_in[j], 16)

            def store_o(b, r):
                sp.wait_ge(S["o_sb"], 4 * b + 4)
                for c in range(4):
                    dst = o_dram[ds(b, 1)].rearrange("b (a c d) s t -> (b c) (d s) a t", a=4, c=4)[c]
                    sp.dma_start(dst, osb[32 * c:32 * c + 16, r, :, :]).then_inc(S["o_out"], 16)

            def load_nd(b, r):
                sp.wait_ge(S["o_out"], 64 * b + 64)
                need(sp, "x3_done", 3 * (b - 1) + 1)
                sp.dma_start(nd[:, r, :, :], o_dram[ds(b, 1)].rearrange("b c s t -> (b c) s t")).then_inc(nd_in[r], 16)

            for j in range(3):
                load_stack(0, j)
            store_q(1, 4)
            move_max(0, 0)
            load_stack(0, 3)

            def load_w(c, r, first=False):
                if not first:
                    sp.wait_ge(S["whi_done"], c - 1)
                    sp.wait_ge(S["wlo_done"], c - 1)
                sp.dma_start(WST[r], wpack[ds(c, 1), :, :].rearrange("c p n -> (c p) n")).then_inc(w_in[r], 16)

            def sp_unit(i, j, first, last):
                b = 2 * i + j // 2
                if not (last and j == 3):
                    move_max(i + (j + 1) // 4, (j + 1) % 4)
                if j % 2 == 0 and not (first and j == 0):
                    store_o(b - 1, (j // 2 + 1) % 2)
                if first and j == 0:
                    sp.wait_ge(S["q_out"], 48 * 2)
                if not last:
                    load_stack(i + 1, j)
                if j % 2 == (0 if last else 1) and not (first and j == 1):
                    load_nd(b - 1, (j // 2 + 1) % 2)

            for j in range(4):
                sp_unit(0, j, True, False)
            with sp.Fori(1, B // 2 - 1) as i:
                for j in range(4):
                    sp_unit(i, j, False, False)
            load_w(0, 0, True)
            load_w(1, 1, True)
            for j in range(4):
                sp_unit(B // 2 - 1, j, False, True)
            for c in range(2, 4):
                load_w(c, c % 2)
            store_o(B - 1, 1)
            load_nd(B - 1, 1)
            with sp.Fori(1, NCH // 4) as i:
                for r in range(4):
                    load_w(4 * i + r, r % 2)
            load_w(NCH - 1, 0)
            for b in range(0, B, 2):
                sp.wait_ge(S["y_done"], b + 2)
                sp.dma_start(out[b:b + 2].rearrange("b p l -> p b l"), X[:, b:b + 2, :]).then_inc(S["out_done"], 16)
            sp.wait_ge(S["out_done"], 64)

        @block.scalar
        def _(act):
            for dst, src, name in (
                (ident[:, :], ident_d, "consts_in"), (kw, kern.rearrange("(k p) f -> p k f", p=128), "kern_in"),
                (heads[:, :], heads_d, "consts_in"), (skipc[:, :], skip.rearrange("(p a) -> p a", a=1), "consts_in"),
                (gain[:, :], gains.partition_broadcast(128), "consts_in"), (msk[:, :], mask, "msk_in"),
                (bqb[:, :], biasq.partition_broadcast(128), "kern_in"),
                (C[:, :, :], ctx.rearrange("b p l -> p b l"), "ctx_in"),
            ):
                act.dma_start(dst, src).then_inc(S[name], 16)
            act.wait_ge(S["msk_in"], 16)
            act.activation(mtmp[:, 0, :], msk[:, :], ACT.Copy, scale=-NEG).then_inc(S["aux_done"], 1)
            act.activation(mtmp[:, 1, :], msk[:, :], ACT.Copy, bias=1.0, scale=-1.0).then_inc(S["aux_done"], 1)
            act.wait_ge(S["aux_done"], 2)
            for rows, src in ((AQ[:, 0:2, :], mtmp[:, 0:1, :]), (AK[:, 0:3:2, :], mtmp[:, 1:2, :])):
                act.activation(rows, src.to_broadcast([B, 2, L]), ACT.Copy).then_inc(S["aux_done"], 1)
            act.activation(AQ[:, 4:6, :], mtmp[:, 0:1, :].to_broadcast([B, 2, L]), ACT.Copy, scale=0.0).then_inc(S["aux_done"], 1)
            act.activation(AK[:, 4:6, :], mtmp[:, 0:1, :].to_broadcast([B, 2, L]), ACT.Copy, bias=1.0, scale=0.0).then_inc(S["aux_done"], 1)
            act.wait_ge(S["consts_in"], 64)
            act.activation(tg[:, :], gain[:, :], ACT.Tanh).then_inc(S["tanh_done"], 1)
            for n in range(4):
                act.wait_ge(S["vt_ps"], n + 1)
                act.activation(VF[:, n * 512:(n + 1) * 512], PS[:, 4 + n, :], ACT.Copy).then_inc(S["vt_done"], 1)
            act.wait_ge(S["sk_ps"], 1)
            act.activation(skb[:, :], PS[:, 2, 0:L], ACT.Copy).then_inc(S["skb_done"], 1)

            def take_k(n):
                act.wait_ge(S["kp_ps"], n + 1)
                act.activation(KF[:, n * 512:(n + 1) * 512], PS[:, n, :], ACT.Identity, bias=bqk_sb[:, 1:2]).then_inc(S["k_t"], 1)

            def take_v(n):
                act.wait_ge(S["vp_ps"], n + 1)
                act.activation(VF[:, n * 512:(n + 1) * 512], PS[:, 4 + n, :], ACT.Copy).then_inc(S["v_t"], 1)

            def high(n, src, ready, done):
                act.wait_ge(S[ready], n + 1)
                act.activation(row(HI[:, :, :])[:, n * 512:(n + 1) * 512], src[:, n * 512:(n + 1) * 512], ACT.Copy).then_inc(S[done], 1)

            def round_in(t):
                act.wait_ge(S["xs_done"], t + 1)
                for b in range(4 * t, 4 * t + 4):
                    act.activation(CG[:, b, :], XN[:, b, :], ACT.Identity, bias=rnd[:, 0:1], scale=small[:, 8, b:b + 1]).then_inc(S["xr_done"], 1)

            def turn_in(t):
                b = slice(4 * t, 4 * t + 4)
                act.wait_ge(S["xq_t"], t + 1)
                act.activation(qb[:, b, :], CG[:, b, :], ACT.Copy, bias=-ROUND).then_inc(S["xq_done"], 1)
                act.wait_ge(S["qT_ps"], t + 1)
                act.activation(qbT[:, :, b, :], PS[:, t, :].bitcast(bf16).rearrange("p (k b t) -> p k b t", k=2, b=4),
                               ACT.Copy).then_inc(S["qT_done"], 1)

            def round_out(t):
                act.wait_ge(S["ys_done"], t + 1)
                for b in range(4 * t, 4 * t + 4):
                    act.activation(CG[:, b, :], CG[:, b, :], ACT.Identity, bias=rnd[:, 0:1], scale=small[:, 12, b:b + 1]).then_inc(S["yr_done"], 1)

            act.wait_ge(S["const_set"], 2)
            act.wait_ge(S["attn_in"], 48)
            act.wait_ge(S["ot_ps"], 4)
            take_k(0)
            take_k(1)
            take_v(0)
            take_v(1)
            round_in(0)
            take_k(2)
            take_v(2)
            take_v(3)
            turn_in(0)
            take_k(3)
            round_in(1)
            act.wait_ge(S["aux_out"], 32)
            high(0, KF, "k_done", "k_hi")
            turn_in(1)
            round_out(0)
            for n in range(1, 4):
                high(n, KF, "k_done", "k_hi")
            round_out(1)
            act.wait_ge(S["k_out"], 32)
            for n in range(4):
                high(n, QF, "q_done", "q_hi")
            act.wait_ge(S["tanh_done"], 1)
            act.activation(row(MB[:, :, :]), row(MB[:, :, :]), ACT.Copy, scale=tg[:, 1:2]).then_inc(S["x3_done"], 1)

            def exps(i, j, q):
                u = 4 * i + j
                for g in range(4):
                    act.wait_ge(S["e_ps"], 8 * u + 4 * q + g + 1)
                    if g == 0:
                        need(act, "pv_done", 2 * u + q - 1)
                    act.activation(EXPS[q][:, 512 * g:512 * g + 512], PS[:, 4 + g % 2, :], ACT.Exp).then_inc(S["p_done"], 1)

            def evac_o(i, j, q):
                u, grp = 4 * i + j, 2 * (j % 2) + q
                act.wait_ge(S["pv_done"], 2 * u + q + 1)
                if grp == 0:
                    need(act, "o_out", 64 * (2 * i + j // 2 - 1))
                act.activation(osb[:, j // 2, grp, :], PS[:, 6 + q, 0:L], ACT.Copy).then_inc(S["o_sb"], 1)

            def act_unit(i, j, first, before_last=lambda: None):
                exps(i, j, 0)
                if not (first and j == 0):
                    evac_o(i + (j - 1) // 4, (j - 1) % 4, 1)
                exps(i, j, 1)
                before_last()
                evac_o(i, j, 0)

            for j in range(4):
                act_unit(0, j, True)
            with act.Fori(1, B // 2 - 1) as i:
                for j in range(4):
                    act_unit(i, j, False)

            def router_exp(t):
                b = slice(4 * t, 4 * t + 4)
                act.wait_ge(S["l_done"], 2 * t + 2)
                act.activation(EX[:, b, :], EX[:, b, :], ACT.Exp).then_inc(S["l_exp"], 1)
                act.activation(CB[:, b, NE:NE + 1], LG[:, b, NE:NE + 1], ACT.Exp, scale=-1.0).then_inc(S["l_exp"], 1)

            def split_w(i, r):
                act.wait_ge(w_in[r % 2], 16 * (2 * i + r // 2) + 16)
                if isinstance(i, int) and i == 0:
                    act.wait_ge(S["e_ps"], 8 * NU)
                    act.wait_ge(S["whi_done"], 2)
                else:
                    act.wait_ge(S["down_done"], 8 * i + r - 3)
                act.activation(WHI[r], WST[r % 2], ACT.Copy).then_inc(S["whi_done"], 1)

            def act_silu(i, m):
                n = 8 * i + m
                act.wait_ge(S["guc_g"], n + 1)
                need(act, "t_done", n - 1)
                act.activation(SIL[m % 2], PS[:, 4 + (3 * m) % 4, :], ACT.Silu).then_inc(S["sil_done"], 1)

            def act_hi(i, m):
                n = 8 * i + m
                act.wait_ge(S["h_done"], n + 1)
                need(act, "down_done", n - 1)
                act.activation(HHI[m % 2], HH[m % 2], ACT.Copy).then_inc(S["hhi_done"], 1)

            def act_chunks(i, first=False, last=False):
                for m in range(8):
                    if m < 2:
                        split_w(i, m + 2)
                    elif m == 6 or (m == 7 and not last):
                        split_w(i + 1, m - 6)
                    if first and m == 4:
                        router_exp(1)
                    act_silu(i, m)
                    act_hi(i, m)
                    if first and m == 3:
                        act.wait_ge(S["xt_done"], 2)
                        for k in range(2):
                            act.activation(token_group(XTH, 1)[:, k], token_group(XT, 1)[:, k], ACT.Copy).then_inc(S["xth_done"], 1)

            for j in range(4):
                act_unit(B // 2 - 1, j, False, before_last=lambda: router_exp(0) if j == 3 else None)
            evac_o(B // 2 - 1, 3, 1)
            act_chunks(0, first=True)
            with act.Fori(1, NCH // 4 - 1) as i:
                act_chunks(i)
            act_chunks(NCH // 4 - 1, last=True)
            for m in range(2):
                act_silu(NCH // 4, m)
                act_hi(NCH // 4, m)

        @block.gpsimd
        def _(pool):
            def power(k, b=slice(0, B)):
                pool.wait_ge(S["var_done"], k)
                pool.tensor_tensor(rstd[:, b], ve[:, b], mhalf[:, b], ALU.pow).then_inc(S["rstd_done"], 1)

            after(pool, pool.memset(mhalf[:, :], -0.5), "const_set", 1)
            after(pool, pool.memset(rnd[:, :], ROUND), "const_set", 2)
            def clear(stacks):
                for t in stacks:
                    pool.memset(row(t[:, :, :]).bitcast(f32), 0.0).then_inc(S["zeroed"], 1)

            clear(QS[0:2])
            power(1, slice(0, 4))
            power(2, slice(4, 8))
            clear(QS[2:4])
            pool.wait_ge(S["aux_done"], 6)
            for rows, src, high in ((AQ[:, 2:4, :], mtmp[:, 0:1, :], AQ[:, 0:1, :]), (AK[:, 1:4:2, :], mtmp[:, 1:2, :], AK[:, 0:1, :])):
                pool.tensor_tensor(rows, src.to_broadcast([B, 2, L]), high.bitcast(f32).to_broadcast([B, 2, L]), ALU.subtract).then_inc(S["aux_low"], 1)
            pool.wait_ge(S["cr_in"], 16)
            pool.wait_ge(S["vt_done"], 4)
            vt16 = VT[:, :, :, :].rearrange("p k b t -> p (k b) t")
            cr16 = CR.rearrange("p k b t -> p (k b) t")

            def products(i):
                for j in range(4):
                    h = 4 * i + j
                    need(pool, "y_ps", h - 1)
                    v = vt16[:, :, ds(h * HD0, HD0)].unsqueeze(2).to_broadcast([128, 2 * B, HD0, HD0])
                    c = cr16[:, :, ds(h * HD0, HD0)].unsqueeze(3).to_broadcast([128, 2 * B, HD0, HD0])
                    o = KVP[:, j % 2, :].rearrange("p (n j i) -> p n j i", n=2 * B, j=HD0)
                    pool.tensor_tensor(o, v, c, ALU.mult).then_inc(S["kv_done"], 1)

            products(0)
            with pool.Fori(1, NH0 // 4) as i:
                products(i)

            pool.wait_ge(S["cg_done"], 1)
            pool.tensor_tensor(row(X[:, :, :]), row(X[:, :, :]), QF, ALU.add).then_inc(S["skip_done"], 1)
            clear(KS[0:3])
            power(3, slice(0, 4))
            pool.wait_ge(S["kv_done"], NH0)
            pool.memset(VA[:, :, :, :].rearrange("p n h (d s) -> p n h d s", s=2)[:, :, :, :, 1], 1.0).then_inc(S["va_ones"], 1)

            def low(n, src, ready, done):
                c = slice(n * 512, (n + 1) * 512)
                pool.wait_ge(S[ready], n + 1)
                pool.tensor_tensor(row(LO[:, :, :])[:, c], src[:, c], row(HI[:, :, :])[:, c].bitcast(f32), ALU.subtract).then_inc(S[done], 1)

            def mask_k(n):
                c = slice(n * 512, (n + 1) * 512)
                pool.wait_ge(S["k_t"], n + 1)
                pool.tensor_tensor(KF[:, c], KF[:, c], row(MB[:, :, :])[:, c], ALU.mult).then_inc(S["k_done"], 1)

            def mask_v(n):
                pool.wait_ge(S["v_t"], n + 1)
                v = VF[:, n * 512:(n + 1) * 512]
                vb = v.rearrange("p (n o) -> p n o", n=4)
                after(pool, pool.tensor_tensor(vb, vb, bv_sb[:, :].unsqueeze(1).to_broadcast([128, 4, 128]), ALU.add), "v_b", n + 1)
                m = smt[:, 4 * n:4 * n + 4].unsqueeze(2).unsqueeze(3).to_broadcast([128, 4, NH1, HD1])
                o = VA[:, 4 * n:4 * n + 4, :, :].rearrange("p n h (d s) -> p n h d s", s=2)[:, :, :, :, 0]
                pool.tensor_tensor(o, v.rearrange("p (n h d) -> p n h d", n=4, h=NH1), m, ALU.mult).then_inc(S["v_done"], 1)

            pool.wait_ge(S["attn_in"], 48)
            pool.wait_ge(S["mask_in"], 32)
            pool.wait_ge(S["aux_out"], 32)
            mask_k(0)
            mask_k(1)
            power(4, slice(4, 8))
            mask_v(0)
            for n in (2, 3):
                mask_k(n)
            mask_v(1)
            for n in range(4):
                low(n, KF, "k_hi", "k_lo")
            power(5, slice(0, 4))
            mask_v(2)
            pool.wait_ge(S["k_out"], 32)
            low(0, QF, "q_hi", "q_lo")
            power(6, slice(4, 8))
            for n in range(1, 4):
                low(n, QF, "q_hi", "q_lo")
            mask_v(3)
            pool.wait_ge(S["v_done"], 4)

            def copy_v(b, r):
                need(pool, "pv_done", 4 * (b - 1))
                pool.tensor_copy(VR[:, r, :, :, :].rearrange("p k h c -> p (k h c)"),
                                 VA[:, ds(2 * b, 2), :, :].rearrange("p k h c -> p (k h c)")).then_inc(S["vr_done"], 1)

            pool.wait_ge(S["x3_done"], 1)

            def add_attention(b, r):
                pool.wait_ge(S["rden_done"], 2 * b + 2)
                n = nd[:, r, 0, :]
                after(pool, pool.tensor_tensor(n, n, rden[:, r, :], ALU.mult), "x3_done", 3 * b + 2)
                after(pool, pool.tensor_tensor(n, n, MB[:, ds(b, 1), :].rearrange("p b l -> p (b l)"), ALU.mult), "x3_done", 3 * b + 3)
                xb = X[:, ds(b, 1), :].rearrange("p b l -> p (b l)")
                pool.tensor_tensor(xb, xb, n, ALU.add).then_inc(S["x3_done"], 1)

            copy_v(0, 0)
            copy_v(1, 1)

            def pool_pair(i):
                for r in range(2):
                    copy_v(2 * i + r, r)
                    add_attention(2 * i + r - 2, r)

            def split_low(c, r):
                pool.wait_ge(S["whi_done"], c + 1)
                pool.tensor_tensor(WLO[r], WST[r % 2][:, 0:768], WHI[r][:, 0:768].bitcast(f32), ALU.subtract).then_inc(S["wlo_done"], 1)

            with pool.Fori(1, B // 2 - 1) as i:
                pool_pair(i)
            copy_v(B - 2, 0)
            add_attention(B - 4, 0)
            copy_v(B - 1, 1)
            power(7, slice(0, 4))
            pool.wait_ge(S["e_ps"], 8 * (NU - 2))
            for t in (CBT[0], ZR, CBT[1]):
                pool.memset(t.bitcast(f32), 0.0).then_inc(S["cbt_zero"], 1)
            split_low(0, 0)
            add_attention(B - 3, 1)
            split_low(1, 1)
            add_attention(B - 2, 0)
            split_low(2, 2)
            split_low(3, 3)
            add_attention(B - 1, 1)
            power(8, slice(4, 8))
            for k in range(2):
                pool.wait_ge(S["xth_done"], 2 + k)
                pool.tensor_tensor(token_group(XTL, 1)[:, k], token_group(XT, 1)[:, k], token_group(XTH, 1)[:, k].bitcast(f32),
                                   ALU.subtract).then_inc(S["xtl_done"], 1)
            with pool.Fori(1, NCH // 4) as i:
                for r in range(4):
                    split_low(4 * i + r, r)
            split_low(NCH - 1, 0)

        @block.vector
        def _(dve):
            st = Steps(dve, "dstep")
            link, tick = st.link, st.tick

            def statistics(bs):
                for b in bs:
                    tick(dve.bn_stats(bst[:, b, :], X[:, b, :]))

            def variance(bs):
                st.sync()
                for b in bs:
                    tick(dve.bn_aggr(mv[:, b, :], bst[:, b, :]))
                st.sync()
                b = slice(bs[0], bs[-1] + 1)
                dve.tensor_scalar(ve[:, b], mv[:, b, 1], EPS, None, ALU.add).then_inc(S["var_done"], 1)

            def normalise(k, bs, mirror=False):
                dve.wait_ge(S["rstd_done"], k)
                for b in bs:
                    xb, o = X[:, b:b + 1, :], XN[:, b:b + 1, :]
                    if mirror:
                        xb, o = backwards(xb), o.rearrange("p b (k l) -> p b k l", k=2)
                    dve.tensor_scalar(o, xb, mv[:, b, 0:1], rstd[:, b:b + 1], ALU.subtract, ALU.mult).then_inc(S["xn_done"], 1)

            def scale_of(amax, scale, inv, zero, done=None):
                link(dve.tensor_scalar(zero, amax, 0.0, None, ALU.is_equal))
                link(dve.scalar_tensor_tensor(out=scale, in0=amax, scalar=1.0 / QMAX, in1=zero, op0=ALU.mult, op1=ALU.add))
                if done:
                    after(dve, dve.reciprocal(inv, scale), *done)
                else:
                    link(dve.reciprocal(inv, scale))

            dve.memset(row(KS[3][:, :, :]).bitcast(f32), 0.0).then_inc(S["zeroed"], 1)
            link(dve.memset(ones[:, :], 1.0))

            for t in range(2):
                dve.wait_ge(x_in[t], 16)
                statistics(range(4 * t, 4 * t + 4))
                variance(range(4 * t, 4 * t + 4))
            for t in range(2):
                normalise(t + 1, range(4 * t, 4 * t + 4), mirror=True)
            dve.wait_ge(S["consts_in"], 64)
            dve.tensor_copy(identb[:, :], ident[:, :]).then_inc(S["consts_done"], 1)
            dve.tensor_scalar(heads[:, :], heads[:, :], skipc[:, 0:1], None, ALU.mult).then_inc(S["consts_done"], 1)
            dve.wait_ge(S["kt_ps"], 1)
            link(dve.tensor_reduce(akf[:, :], PS[:, 2, :].rearrange("p (f d) -> p f d", f=2), AX.X, ALU.max, apply_absolute_value=True))
            scale_of(akf[:, :], small[:, 0, 0:2], small[:, 0, 2:4], small[:, 1, 0:2])
            for f in range(4):
                dve.tensor_scalar(diag[:, f, :], ident[:, :], small[:, 0, f:f + 1], None, ALU.mult).then_inc(S["diag_done"], 1)
            dve.wait_ge(S["xn_done"], B)
            dve.wait_ge(S["ctx_in"], 16)
            halved = "p b (k l) -> p b k l"
            dve.tensor_tensor(CG[:, :, :].rearrange(halved, k=2), XN[:, :, :].rearrange(halved, k=2), backwards(C[:, :, :]),
                              ALU.mult).then_inc(S["vc_done"], 1)
            dve.wait_ge(S["sk_ps"], 2)
            link(dve.tensor_tensor(kt2, kw, PS[:, 3, 0:L].unsqueeze(1).to_broadcast([128, 2, L]), ALU.mult))
            link(dve.tensor_scalar(kt2, kt2, ROUND, ROUND - QMAX, ALU.add, ALU.max))
            dve.tensor_scalar(kq[:, :, :], kt2, ROUND + QMAX, ROUND, ALU.min, ALU.subtract).then_inc(S["kq_done"], 1)
            dve.wait_ge(S["ct_in"], 16)
            ct16 = CT[:, :, :, :].rearrange("p k b t -> p (k b) t")
            ot16 = OT[:, :, :, :].rearrange("p k b t -> p (k b) t")

            def gate_rows(i, heads_of=range(4)):
                for j in heads_of:
                    h, r = 4 * i + j, j % 2
                    dve.wait_ge(S["y_ps"], h + 1)
                    need(dve, "ot_part", h - 1)
                    c = ct16[:, :, ds(h * HD0, HD0)].unsqueeze(2).to_broadcast([128, 2 * B, HD0, HD0])
                    y = banks(2 * r, 2).rearrange("p (n j i) -> p n j i", n=2 * B, j=HD0)
                    yx = KVP[:, 2 + r, :].rearrange("p (n j i) -> p n j i", n=2 * B, j=HD0)
                    after(dve, dve.tensor_tensor(yx, y, c, ALU.mult), "yx_done", h + 1)
                    dve.tensor_reduce(ot16[:, :, ds(h * HD0, HD0)], yx, AX.X, ALU.add).then_inc(S["ot_part"], 1)

            gate_rows(0, [0])
            link(dve.tensor_reduce(small[:, 2, 0:1], bqb[:, :], AX.X, ALU.max, apply_absolute_value=True))
            scale_of(small[:, 2, 0:1], small[:, 3, 0:1], small[:, 4, 0:1], small[:, 5, 0:1])
            link(dve.tensor_scalar(bqb[:, :], bqb[:, :], small[:, 4, 0:1], ROUND, ALU.mult, ALU.add))
            link(dve.tensor_scalar(bqb[:, :], bqb[:, :], ROUND - QMAX, ROUND + QMAX, ALU.max, ALU.min))
            link(dve.tensor_scalar(bqb[:, :], bqb[:, :], ROUND, small[:, 3, 0:1], ALU.subtract, ALU.mult))
            dve.wait_ge(S["g_ps"], 4)
            dve.wait_ge(S["tanh_done"], 1)
            dve.scalar_tensor_tensor(out=CG[:, :, :].rearrange(halved, k=2), in0=backwards(banks(4, 4).rearrange("p (b l) -> p b l", b=B)),
                                     scalar=tg[:, 0:1], in1=C[:, :, :].rearrange(halved, k=2), op0=ALU.mult, op1=ALU.mult).then_inc(S["cg_done"], 1)
            gate_rows(0, range(1, 4))
            dve.wait_ge(S["attn_in"], 48)
            link(dve.tensor_scalar(W3[:, 0, :], W3[:, 0, :], HD1 ** -0.5, None, ALU.mult))
            dve.tensor_scalar(bqk_sb[:, 0:1], bqk_sb[:, 0:1], HD1 ** -0.5, None, ALU.mult).then_inc(S["wq_done"], 1)
            with dve.Fori(1, NH0 // 4) as i:
                gate_rows(i)

            def add_mixer(n):
                c = slice(n * 512, (n + 1) * 512)
                dve.wait_ge(S["ot_ps"], n + 1)
                dve.scalar_tensor_tensor(out=row(X[:, :, :])[:, c], in0=PS[:, 4 + n, :], scalar=tg[:, 0:1],
                                         in1=row(X[:, :, :])[:, c], op0=ALU.mult, op1=ALU.add).then_inc(S["x1_done"], 1)

            amax, sx, inv, zero, ymax, sy, yinv, yz = (small[:, n, :] for n in range(6, 14))

            def scale_in(t):
                b = slice(4 * t, 4 * t + 4)
                dve.wait_ge(S["xn_done"], B + 4 * t + 4)
                link(dve.tensor_reduce(amax[:, b], XN[:, b, :], AX.X, ALU.max, apply_absolute_value=True))
                scale_of(amax[:, b], sx[:, b], inv[:, b], zero[:, b], ("xs_done", t + 1))

            def clip_in(t):
                cg = QF[:, 1024 * t:1024 * t + 1024]
                dve.wait_ge(S["xr_done"], 4 * t + 4)
                dve.tensor_scalar(cg, cg, ROUND - QMAX, ROUND + QMAX, ALU.max, ALU.min).then_inc(S["xq_t"], 1)

            def take_out(t):
                for n in range(4 * t, 4 * t + 4):
                    if n % 2 == 0:
                        dve.wait_ge(S["f_ps"], n // 2 + 1)
                    tick(dve.scalar_tensor_tensor(out=CG[:, n, :], in0=PS[:, 4 + n // 2, (n % 2) * L:(n % 2 + 1) * L], scalar=sx[:, n:n + 1],
                                                  in1=skb[:, :], op0=ALU.mult, op1=ALU.mult))

            def bias_out(t):
                b = slice(4 * t, 4 * t + 4)
                st.sync()
                link(dve.tensor_tensor(CG[:, b, :], CG[:, b, :], bqb[:, :].unsqueeze(1).to_broadcast([128, 4, L]), ALU.add))

            def scale_out(t):
                b = slice(4 * t, 4 * t + 4)
                link(dve.tensor_reduce(ymax[:, b], CG[:, b, :], AX.X, ALU.max))
                link(dve.tensor_scalar(ymax[:, b], ymax[:, b], 0.0, None, ALU.max))
                scale_of(ymax[:, b], sy[:, b], yinv[:, b], yz[:, b], ("ys_done", t + 1))
                link(dve.tensor_scalar(sy[:, b], sy[:, b], tg[:, 2:3], None, ALU.mult))

            def add_mlp(t):
                cg = QF[:, 1024 * t:1024 * t + 1024]
                dve.wait_ge(S["yr_done"], 4 * t + 4)
                link(dve.tensor_scalar(cg, cg, ROUND, ROUND + QMAX, ALU.max, ALU.min))
                for b in range(4 * t, 4 * t + 4):
                    tick(dve.tensor_scalar(CG[:, b, :], CG[:, b, :], ROUND, sy[:, b:b + 1], ALU.subtract, ALU.mult))
                st.sync()
                x = row(X[:, :, :])[:, 1024 * t:1024 * t + 1024]
                after(dve, dve.tensor_tensor(x, x, cg, ALU.add), "x2_done", t + 1)

            def take_q(n):
                c = slice(n * 512, (n + 1) * 512)
                dve.wait_ge(S["q_ps"], n + 1)
                dve.scalar_tensor_tensor(out=QF[:, c], in0=PS[:, n if n < 2 else n + 2, :], scalar=bqk_sb[:, 0:1], in1=row(MB[:, :, :])[:, c],
                                         op0=ALU.add, op1=ALU.mult).then_inc(S["q_done"], 1)

            half_a, half_b = range(0, 4), range(4, 8)
            dve.wait_ge(S["skip_done"], 1)
            add_mixer(0)
            add_mixer(1)
            dve.wait_ge(S["x1_done"], 2)
            statistics(half_a)
            variance(half_a)
            add_mixer(2)
            add_mixer(3)
            dve.wait_ge(S["mask_in"], 32)
            normalise(3, half_a)
            scale_in(0)
            dve.wait_ge(S["x1_done"], 4)
            statistics(half_b)
            variance(half_b)
            clip_in(0)
            normalise(4, half_b)
            scale_in(1)
            take_out(0)
            clip_in(1)
            bias_out(0)
            scale_out(0)
            take_out(1)
            add_mlp(0)
            statistics(half_a)
            variance(half_a)
            bias_out(1)
            normalise(5, half_a)
            scale_out(1)
            take_q(0)
            add_mlp(1)
            statistics(half_b)
            variance(half_b)
            take_q(1)
            normalise(6, half_b)
            take_q(2)
            take_q(3)

            def maximum(i, j, k):
                u = 4 * i + j
                dve.wait_ge(S["s_ps"], 4 * u + k + 1)
                if k == 0:
                    need(dve, "turned", u - 1)
                half, hb = k // 2, 4 * (k % 2)
                dve.tensor_reduce(negm[:, j % 2, hb:hb + 4, half], banks(tile_bank(j, k), 2).rearrange("p (h s) -> p h s", h=4),
                                  AX.X, ALU.max, negate=True).then_inc(S["s_used"], 1)

            def split_max(i, j):
                u = 4 * i + j
                dve.wait_ge(S["turned"], u + 1)
                if not (isinstance(i, int) and i == 0 and j < 2):
                    dve.wait_ge(m_in[(j + 2) % 4], 32 * (i + j // 2))
                src = PS[0:16, turn_bank(j), 0:128]
                after(dve, dve.tensor_copy(mT[:, j % 2, 0, :], src), "mt_done", 2 * u + 1)
                dve.tensor_tensor(mT[:, j % 2, 1, :], src, mT[:, j % 2, 0, :].bitcast(f32), ALU.subtract).then_inc(S["mt_done"], 1)

            def reciprocal_of(i, r, half):
                t = slice(half * 128, half * 128 + 128)
                dve.wait_ge(nd_in[r], 16 * i + 16)
                dve.reciprocal(rden[:, r, t], nd[:, r, 1, t]).then_inc(S["rden_done"], 1)

            dve.wait_ge(S["q_done"], 4)
            for k in range(4):
                maximum(0, 0, k)
            split_max(0, 0)
            maximum(0, 1, 0)
            for k in range(1, 4):
                maximum(0, 1, k)

            early_b, late_b = range(0, 4), range(4, 8)

            def dve_unit(i, j, first, last):
                def max_ahead(k):
                    if not (last and j >= 2):
                        maximum(i + (j + 2) // 4, (j + 2) % 4, k)

                max_ahead(0)
                if not (last and j == 3):
                    split_max(i + (j + 1) // 4, (j + 1) % 4)
                if last and j == 2:
                    for r in range(2):
                        dve.wait_ge(w_in[r], 16)
                        dve.wait_ge(S["e_ps"], 8 * (NU - 3 + r))
                        dve.tensor_copy(WHI[r], WST[r]).then_inc(S["whi_done"], 1)
                max_ahead(1)
                max_ahead(2)
                if not first:
                    reciprocal_of(i - 1, j // 2, j % 2)
                if last and j == 1:
                    dve.wait_ge(S["x3_done"], 3 * 4 + 1)
                    statistics(early_b)
                    variance(early_b)
                max_ahead(3)

            for j in range(4):
                dve_unit(0, j, True, False)
            with dve.Fori(1, B // 2 - 1) as i:
                for j in range(4):
                    dve_unit(i, j, False, False)
            for j in range(4):
                dve_unit(B // 2 - 1, j, False, True)

            def take_x(t):
                dve.wait_ge(S["xt_ps"], t + 1)
                after(dve, dve.tensor_copy(token_group(XT, t), banks(2, 2).rearrange("p (k b t) -> p k b t", k=2, b=4)), "xt_done", t + 1)

            def route(t):
                b = slice(4 * t, 4 * t + 4)
                n = B // 2
                dve.wait_ge(S["l_ps"], t + 1)
                link(dve.tensor_copy(LG[:, b, :], PS[:, 2, 0:n * (NE + 1)].rearrange("p (b e) -> p b e", b=n)))
                lg = LG[:, b, 0:NE]
                after(dve, dve.tensor_reduce(small[:, 14, b], lg, AX.X, ALU.max), "l_done", 2 * t + 1)
                after(dve, dve.tensor_tensor(EX[:, b, :], lg, small[:, 14, b].unsqueeze(2).to_broadcast([128, n, NE]), ALU.subtract), "l_done", 2 * t + 2)
                lj = lg.unsqueeze(2).to_broadcast([128, n, NE, NE])
                li = lg.unsqueeze(3).to_broadcast([128, n, NE, NE])
                tick(dve.tensor_tensor(R1, lj, li, ALU.is_gt))
                link(dve.tensor_tensor(R2, lj, li, ALU.is_equal))
                r1, r2 = (t.rearrange("p b i j -> p b (i j)") for t in (R1, R2))
                link(dve.tensor_tensor(r2, r2, early[:, :, :].rearrange("p i j -> p (i j)").unsqueeze(1).to_broadcast([128, n, NE * NE]), ALU.mult))
                link(dve.tensor_tensor(r1, r1, r2, ALU.add))
                link(dve.tensor_reduce(rank[:, b, :], R1, AX.X, ALU.add))

            def expert_weights(t):
                b = slice(4 * t, 4 * t + 4)
                dve.wait_ge(S["l_exp"], 2 * t + 2)
                tick(dve.tensor_scalar(CB[:, b, NE:NE + 1], CB[:, b, NE:NE + 1], 1.0, None, ALU.add))
                link(dve.scalar_tensor_tensor(out=EX[:, b, :], in0=rank[:, b, :], scalar=1.5, in1=EX[:, b, :], op0=ALU.is_lt, op1=ALU.mult))
                tick(dve.reciprocal(CB[:, b, NE:NE + 1], CB[:, b, NE:NE + 1]))
                link(dve.tensor_reduce(small[:, 14, b], EX[:, b, :], AX.X, ALU.add))
                link(dve.reciprocal(small[:, 15, b], small[:, 14, b]))
                dve.tensor_tensor(CB[:, b, 0:NE], EX[:, b, :], small[:, 15, b].unsqueeze(2).to_broadcast([128, B // 2, NE]), ALU.mult).then_inc(S["cb_done"], 1)

            def split_weights(t):
                dve.wait_ge(S["cbt_ps"], t + 1)
                high, low = CBT[t][0:NE + 1, :], CBT[t][32:32 + NE + 1, :]
                after(dve, dve.tensor_copy(high, PS[0:NE + 1, 3, :]), "cbt_done", 2 * t + 1)
                dve.tensor_tensor(low, PS[0:NE + 1, 3, :], high.bitcast(f32), ALU.subtract).then_inc(S["cbt_done"], 1)

            def gate_hidden(i, m):
                multiply_gates(i, m)
                low_hidden(i, m)

            def multiply_gates(i, m):
                n = 8 * i + m
                dve.wait_ge(S["sil_done"], n + 1)
                dve.wait_ge(S["guc_u"], n + 1)
                after(dve, dve.tensor_tensor(TU[m % 2], SIL[m % 2], PS[:, 4 + (3 * m + 1) % 4, :], ALU.mult), "t_done", n + 1)
                dve.wait_ge(S["guc_c"], n + 1)
                need(dve, "hlo_done", n - 1)
                dve.tensor_tensor(HH[m % 2], TU[m % 2], PS[:, 4 + (3 * m + 2) % 4, :], ALU.mult).then_inc(S["h_done"], 1)

            def low_hidden(i, m):
                n = 8 * i + m
                dve.wait_ge(S["hhi_done"], n + 1)
                need(dve, "down_done", n - 1)
                dve.tensor_tensor(HLO[m % 2], HH[m % 2], HHI[m % 2].bitcast(f32), ALU.subtract).then_inc(S["hlo_done"], 1)

            normalise(7, early_b)
            dve.wait_ge(S["q_out"], 48 * 2)
            take_x(0)
            after(dve, dve.tensor_copy(token_group(XTH, 0), token_group(XT, 0)), "xth_done", 1)
            dve.tensor_tensor(token_group(XTL, 0), token_group(XT, 0), token_group(XTH, 0).bitcast(f32), ALU.subtract).then_inc(S["xtl_done"], 1)
            reciprocal_of(B // 2 - 1, 0, 0)
            reciprocal_of(B // 2 - 1, 0, 1)
            dve.wait_ge(S["cbt_zero"], 3)
            dve.wait_ge(S["router_in"], 32)
            route(0)
            expert_weights(0)
            split_weights(0)
            dve.wait_ge(S["x3_done"], 3 * (B - 1) + 1)
            statistics(late_b[:3])
            dve.wait_ge(S["o_out"], 64 * (B - 1))
            gate_hidden(0, 0)
            reciprocal_of(B // 2 - 1, 1, 0)
            reciprocal_of(B // 2 - 1, 1, 1)
            gate_hidden(0, 1)
            dve.wait_ge(S["x3_done"], 3 * B + 1)
            statistics(late_b[3:])
            variance(late_b)
            gate_hidden(0, 2)
            normalise(8, late_b)
            multiply_gates(0, 3)
            take_x(1)
            low_hidden(0, 3)
            route(1)
            expert_weights(1)
            split_weights(1)
            for m in range(4, 8):
                gate_hidden(0, m)
            with dve.Fori(1, NCH // 4) as i:
                for m in range(8):
                    gate_hidden(i, m)
            for m in range(2):
                gate_hidden(NCH // 4, m)
            for b in range(B):
                dve.wait_ge(*((S["down_half"], b // 4 + 1) if b % 4 < 2 else (S["down_done"], 2 * NCH - 1 + b // 4)))
                dve.scalar_tensor_tensor(out=X[:, b, :], in0=PS[:, b // 2, (b % 2) * L:(b % 2 + 1) * L], scalar=tg[:, 3:4],
                                         in1=X[:, b, :], op0=ALU.mult, op1=ALU.add).then_inc(S["y_done"], 1)

        @block.tensor
        def _(pe):
            mm = pe.matmul
            pe.wait_ge(S["consts_in"], 64)
            pe.wait_ge(S["kern_in"], 32)
            for f in range(2):
                for d in range(2):
                    last = pe.transpose(PS[:, 2, f * L + d * 128:f * L + d * 128 + 128], kw[:, d, f * 128:(f + 1) * 128], ident[:, :])
            last.then_inc(S["kt_ps"], 1)
            for n in range(4):
                k = n // 2
                for b in range(4 * (n % 2), 4 * (n % 2) + 4):
                    pe.wait_ge(S["xn_done"], b + 1)
                    last = pe.transpose(PS[:, 4 + n, (b % 4) * 128:(b % 4 + 1) * 128], XN[:, b, k * 128:(k + 1) * 128], ident[:, :])
                last.then_inc(S["vt_ps"], 1)
            pe.wait_ge(S["diag_done"], 4)
            for n in range(2):
                for f in range(2):
                    last = mm(PS[:, 2 + n, f * 128:(f + 1) * 128], ones[:, :], diag[:, 2 * n + f, :], start=True, stop=True)
                last.then_inc(S["sk_ps"], 1)

            def convolve(i, heads_of=range(4)):
                for j in heads_of:
                    h, r = 4 * i + j, j % 2
                    pe.wait_ge(T_in[j], 16 * i + 16)
                    pe.wait_ge(S["kv_done"], h + 1)
                    need(pe, "yx_done", h - 1)
                    kv = KVP[:, r, :].rearrange("p (k n) -> p k n", k=2)
                    near, far = T[:, j, 0:128], T[:, j, 128:256]
                    mm(PS[:, 2 * r, :], near, kv[:, 0, :], start=True, stop=True)
                    mm(PS[:, 2 * r + 1, :], far, kv[:, 0, :], start=True, stop=False)
                    mm(PS[:, 2 * r + 1, :], near, kv[:, 1, :], start=False, stop=True).then_inc(S["y_ps"], 1)

            convolve(0, [0])
            pe.wait_ge(S["vt_done"], 4)
            pe.wait_ge(S["vc_done"], 1)
            pe.wait_ge(S["consts_done"], 2)
            for n in range(4):
                mm(PS[:, 4 + n, :], heads[:, :], QF[:, n * 512:(n + 1) * 512], start=True, stop=True).then_inc(S["g_ps"], 1)
            pe.wait_ge(S["skb_done"], 1)
            pe.wait_ge(S["kq_done"], 1)
            convolve(0, range(1, 4))
            with pe.Fori(1, NH0 // 4) as i:
                convolve(i)
            pe.wait_ge(S["ot_part"], NH0)
            pe.wait_ge(S["cg_done"], 1)
            for n in range(4):
                for b in (2 * n, 2 * n + 1):
                    for k in range(2):
                        last = pe.transpose(PS[:, 4 + n, (b % 2) * L + k * 128:(b % 2) * L + (k + 1) * 128], OT[:, k, b, :], ident[:, :])
                last.then_inc(S["ot_ps"], 1)
            pe.wait_ge(S["attn_in"], 48)
            pe.wait_ge(S["ctx_in"], 16)
            pe.wait_ge(S["yx_done"], NH0)
            for n in range(4):
                mm(PS[:, n, :], W3[:, 1, :], row(C[:, :, :])[:, n * 512:(n + 1) * 512], start=True, stop=True).then_inc(S["kp_ps"], 1)
            for n in range(4):
                pe.wait_ge(S["x1_done"], n + 1)
                for b in (2 * n, 2 * n + 1):
                    for k in range(2):
                        last = mm(PS[:, 4 + n, (b % 2) * L + k * 128:(b % 2) * L + (k + 1) * 128], C[:, b, k * 128:(k + 1) * 128],
                                  W3[:, 2, :], start=True, stop=True)
                last.then_inc(S["vp_ps"], 1)
            def stay_warm(bank, n):
                for _ in range(n):
                    mm(PS[:, bank, :], identb[:, :], kq[:, :, :].rearrange("p k f -> p (k f)"), start=True, stop=True)

            for t in range(2):
                pe.wait_ge(S["v_t"], 2 * t + 1)
                stay_warm(4 + 2 * t, (18, 8)[t])
                pe.wait_ge(S["xq_done"], t + 1)
                pe.wait_ge(S["k_t"], t + 1)
                qT = PS[:, t, :].bitcast(bf16).rearrange("p (k b t) -> p k b t", k=2, b=4)
                for k in range(2):
                    for b in range(4):
                        last = pe.transpose(qT[:, k, b, :], qb[:, 4 * t + b, k * 128:(k + 1) * 128], identb[:, :])
                last.then_inc(S["qT_ps"], 1)
                pe.wait_ge(S["qT_done"], t + 1)
                pe.wait_ge(S["v_t"], 2 * t + 2)
                for b in range(4 * t, 4 * t + 4):
                    for k in range(2):
                        last = mm(PS[:, 4 + b // 2, (b % 2) * L:(b % 2 + 1) * L], qbT[:, k, b, :], kq[:, k, :], start=(k == 0), stop=(k == 1))
                    if b % 2:
                        last.then_inc(S["f_ps"], 1)
            pe.wait_ge(S["wq_done"], 1)
            pe.wait_ge(S["k_t"], 4)
            stay_warm(0, 30)
            for n in range(4):
                if n == 2:
                    pe.wait_ge(S["ys_done"], 2)
                    stay_warm(4, 42)
                pe.wait_ge(S["xn_done"], 2 * B + 2 * n + 2)
                mm(PS[:, n if n < 2 else n + 2, :], W3[:, 0, :], row(XN[:, :, :])[:, n * 512:(n + 1) * 512], start=True, stop=True).then_inc(S["q_ps"], 1)

            def max_tile(i, j, k):
                u = 4 * i + j
                if k == 0:
                    pe.wait_ge(st_in[j], 80 * i + 80)
                need(pe, *(("s_used", 4 * u - 1), ("s_used", 4 * u + 1), ("mt_done", 2 * u), ("s_used", 4 * u + 2))[k])
                for n in range(4):
                    h, half = 4 * (k % 2) + n, k // 2
                    last = mm(banks(tile_bank(j, k), 2)[:, n * L:(n + 1) * L], QS[j][:, h, half * 128:(half + 1) * 128],
                              KS[j][:, h, :], start=True, stop=True)
                last.then_inc(S["s_ps"], 1)

            def turn_max(i, j):
                u = 4 * i + j
                pe.wait_ge(S["s_used"], 4 * u + 4)
                pe.transpose(PS[0:16, turn_bank(j), 0:128], negm[:, j % 2, :, :].rearrange("p h c -> p (h c)"),
                             ident[:, :]).then_inc(S["turned"], 1)

            def score(i, j, g):
                if g == 0:
                    pe.wait_ge(m_in[j], 32 * i + 32)
                need(pe, "p_done", 8 * (4 * i + j) + g - 1)
                for k in range(2):
                    last = mm(PS[:, 4 + g % 2, k * L:(k + 1) * L], KS[j][:, g, k * 128:(k + 1) * 128],
                              QS[j][:, g, :], start=True, stop=True)
                last.then_inc(S["e_ps"], 1)

            def weigh(i, j, q):
                u = 4 * i + j
                if q == 0 and j % 2 == 0:
                    pe.wait_ge(S["vr_done"], 2 * i + j // 2 + 1)
                pe.wait_ge(S["p_done"], 8 * u + 4 * q + 4)
                need(pe, "o_sb", 2 * u + q - 1)
                for k in range(2):
                    for g in range(4):
                        h = 8 * (j % 2) + 4 * q + g
                        last = mm(PS[32 * g:32 * g + 16, 6 + q, 0:L], VR[:, (j // 2) % 2, k, h, :],
                                  EXPS[q][:, 512 * g + k * L:512 * g + (k + 1) * L], start=(k == 0), stop=(k == 1))
                last.then_inc(S["pv_done"], 1)

            def pe_unit(i, j, first, last, between=None):
                def max_ahead(k):
                    if not (last and j >= 2):
                        max_tile(i + (j + 2) // 4, (j + 2) % 4, k)
                    elif j == 3 or k > 0:
                        stay_warm(1, 4)

                score(i, j, 0)
                score(i, j, 1)
                max_ahead(0)
                score(i, j, 2)
                if not (first and j == 0):
                    weigh(i + (j - 1) // 4, (j - 1) % 4, 1)
                if not (last and j == 3):
                    turn_max(i + (j + 1) // 4, (j + 1) % 4)
                score(i, j, 3)
                max_ahead(1)
                score(i, j, 4)
                score(i, j, 5)
                if between:
                    between()
                max_ahead(2)
                score(i, j, 6)
                weigh(i, j, 0)
                score(i, j, 7)
                max_ahead(3)

            pe.wait_ge(S["q_done"], 2)
            for k in range(4):
                max_tile(0, 0, k)
            max_tile(0, 1, 0)
            turn_max(0, 0)
            for k in range(1, 4):
                max_tile(0, 1, k)
            pe.wait_ge(S["q_done"], 4)
            for j in range(4):
                pe_unit(0, j, True, False)
            with pe.Fori(1, B // 2 - 1) as i:
                for j in range(4):
                    pe_unit(i, j, False, False)
            def turn_x(t):
                for k in range(2):
                    for b in range(4 * t, 4 * t + 4):
                        pe.wait_ge(S["xn_done"], 3 * B + b + 1)
                        last = pe.transpose(PS[:, 2 + k, (b % 4) * 128:(b % 4 + 1) * 128], XN[:, b, k * 128:(k + 1) * 128], ident[:, :])
                last.then_inc(S["xt_ps"], 1)

            def logits(t):
                pe.wait_ge(S["xt_done"], t + 1)
                for b in range(4 * t, 4 * t + 4):
                    for k in range(2):
                        last = mm(PS[:, 2, (b % 4) * (NE + 1):(b % 4 + 1) * (NE + 1)], XT[:, k, b, :], rt[:, k, :], start=(k == 0), stop=(k == 1))
                last.then_inc(S["l_ps"], 1)

            def turn_weights(t):
                pe.wait_ge(S["cb_done"], t + 1)
                for b in range(4 * t, 4 * t + 4):
                    last = pe.transpose(PS[0:NE + 1, 3, (b % 4) * 128:(b % 4 + 1) * 128], CB[:, b, :], ident[:, :])
                last.then_inc(S["cbt_ps"], 1)

            def clear(t):
                for n in range(2 * t, 2 * t + 2):
                    mm(PS[:, n, :], ZR[:, 0:128], ZR, start=True, stop=False, skip_group_check=True)

            def gate_up(i, m, t, before_weights=None):
                n, r = 8 * i + m, m % 4 if t == m // 4 else 0
                xh, xl = token_group(XTH, t), token_group(XTL, t)
                if t == 0:
                    pe.wait_ge(S["whi_done"], 4 * i + r + 1)
                    pe.wait_ge(S["wlo_done"], 4 * i + r + 1)
                for part, ready, count, signal in ((0, "h_done", n - 1, "guc_g"), (1, "sil_done", n, "guc_u")):
                    need(pe, ready, count)
                    o = PS[:, 4 + (3 * m + part) % 4, :]
                    for k in range(2):
                        if before_weights and part == 0 and t == 1:
                            pe.wait_ge(S["xtl_done"], 2 + k)
                        c = slice(256 * part + 128 * k, 256 * part + 128 * k + 128)
                        mm(o, WHI[r][:, c], xh[:, k, :, :], start=(k == 0), stop=False)
                        mm(o, WHI[r][:, c], xl[:, k, :, :], start=False, stop=False)
                        last = mm(o, WLO[r][:, c], xh[:, k, :, :], start=False, stop=(k == 1))
                    last.then_inc(S[signal], 1)
                if before_weights:
                    before_weights()
                need(pe, "t_done", n)
                mm(PS[:, 4 + (3 * m + 2) % 4, :], WHI[r][:, 768:896], CBT[t], start=True, stop=True).then_inc(S["guc_c"], 1)

            def down(i, m, t, ends=False):
                n, r = 8 * i + m, m % 4 if t == m // 4 else 0
                pe.wait_ge(S["hhi_done"], n + 1)
                pe.wait_ge(S["hlo_done"], n + 1)
                for b in range(4):
                    o = PS[:, 2 * t + b // 2, (b % 2) * L:(b % 2 + 1) * L]
                    c = slice(128 * b, 128 * b + 128)
                    mm(o, HHI[m % 2][:, c], WHI[r][:, 512:768], start=False, stop=False, skip_group_check=True)
                    mm(o, HHI[m % 2][:, c], WLO[r][:, 512:768], start=False, stop=False, skip_group_check=True)
                    last = mm(o, HLO[m % 2][:, c], WHI[r][:, 512:768], start=False, stop=False, skip_group_check=True)
                    if ends and b == 1:
                        last.then_inc(S["down_half"], 1)
                last.then_inc(S["down_done"], 1)

            def pe_chunks(i):
                for m in range(8):
                    gate_up(i + (m + 1) // 8, (m + 1) % 8, (m + 1) % 8 // 4)
                    down(i, m, m // 4)

            def prepare(t):
                turn_weights(t)
                if t == 0:
                    clear(0)
                pe.wait_ge(S["cbt_done"], 2 * t + 2)
                if t == 1:
                    clear(1)

            for j in range(3):
                pe_unit(B // 2 - 1, j, False, True)
            pe.wait_ge(S["mt_done"], 2 * NU)
            turn_x(0)
            pe.wait_ge(S["router_in"], 32)
            pe_unit(B // 2 - 1, 3, False, True, lambda: logits(0))
            weigh(B // 2 - 1, 3, 1)
            pe.wait_ge(S["cbt_zero"], 3)
            pe.wait_ge(S["xtl_done"], 1)
            pe.wait_ge(S["p_done"], 8 * NU)
            gate_up(0, 0, 0, lambda: (prepare(0), pe.wait_ge(S["o_sb"], 2 * NU)))
            gate_up(0, 1, 0)
            down(0, 0, 0)
            gate_up(0, 2, 0)
            down(0, 1, 0)
            gate_up(0, 3, 0)
            turn_x(1)
            down(0, 2, 0)
            logits(1)
            down(0, 3, 0)
            gate_up(0, 4, 1, lambda: prepare(1))
            for m in range(4, 8):
                gate_up((m + 1) // 8, (m + 1) % 8, (m + 1) % 8 // 4)
                down(0, m, 1)
            with pe.Fori(1, NCH // 4) as i:
                pe_chunks(i)
            gate_up(NCH // 4, 1, 1)
            down(NCH // 4, 0, 0, True)
            down(NCH // 4, 1, 1, True)


def kernel(**inputs):
    import numpy as np
    import concourse.bacc as bacc
    from concourse.bass_utils import run_bass_kernel_spmd

    a = {n: np.asarray(v) for n, v in inputs.items()}
    f = np.float32
    pad = NCH * 128 - NI
    turn = np.arange(128).reshape(NH1, HD1).T.reshape(-1)

    def hidden(experts, shared):
        w = np.concatenate([experts.transpose(1, 0, 2).reshape(L, NE * EI), shared, np.zeros((L, pad), f)], 1)
        return w.reshape(2, 128, NCH, 128).transpose(2, 1, 0, 3).reshape(NCH, 128, 256)

    down = np.concatenate([a["L1_ffn_w_down"].reshape(NE * EI, L), a["L1_ffn_sw_down"], np.zeros((pad, L), f)], 0)
    owner = np.minimum(np.arange(NCH * 128) // EI, NE)
    sel = np.zeros((128, NCH * 128), f)
    for e in range(NE + 1):
        sel[[e, 32 + e]] = owner == e
    wpack = np.concatenate([hidden(a["L1_ffn_w_gate"], a["L1_ffn_sw_gate"]), hidden(a["L1_ffn_w_up"], a["L1_ffn_sw_up"]),
                            down.reshape(NCH, 128, L), sel.reshape(128, NCH, 128).transpose(1, 0, 2)], 2)
    mask = a["mask_Bx1x2048_fk1"].reshape(B, L)
    ctxT = a["ctx_2048"].transpose(2, 0, 1)
    arrays = {
        "x": a["x"], "ctx": a["ctx_2048"], "ctxT": np.stack([ctxT, ctxT.reshape(2, 128, B, TOK)[:, ::-1].reshape(L, B, TOK)]),
        "mask": mask, "maskT": mask.reshape(B, 2, 128).transpose(2, 0, 1).reshape(128, 2 * B),
        "kpad": np.concatenate([np.zeros((NH0, L), f), a["L0_xattn_k"]], 1),
        "skip": a["fside_S2_0"], "gains": np.concatenate([a["g_xattn"], a["g_ffn"]]),
        "kern": a["L0_ffn_kernel"], "biasq": a["L0_ffn_bias"],
        "wqkvT": np.stack([a["L1_xattn_Wq"][turn].T, a["L1_xattn_Wk"][turn].T, a["L1_xattn_Wv"].T]),
        "bqk": np.stack([a["L1_xattn_bq"][turn], a["L1_xattn_bk"][turn]], 1), "bv": a["L1_xattn_bv"],
        "routerT": np.concatenate([a["L1_ffn_gate_w"].T, a["L1_ffn_shared_gate_w"]], 1),
        "wpack": wpack, "ident_d": np.eye(128, dtype=f),
        "heads_d": np.kron(np.eye(NH0, dtype=f), np.ones((HD0, HD0), f)),
        "earlier_d": np.tril(np.ones((NE, NE), f), -1),
    }
    arrays = {n + "_in": np.ascontiguousarray(v) for n, v in arrays.items()}
    nc = bacc.Bacc("TRN2", target_bir_lowering=False, num_devices=1)
    args = [nc.dram_tensor(n, v.shape, mybir.dt.from_np(v.dtype), kind="ExternalInput").ap() for n, v in arrays.items()]
    out = nc.dram_tensor("out", (B, TOK, L), mybir.dt.float32, kind="ExternalOutput").ap()
    flamingo_program(nc, *args, out)
    r = run_bass_kernel_spmd(nc, [arrays], core_ids=[0])
    return r.results[0]["out"]
```
